# Optimizing a Trainium2 kernel written in Bass

```python
import numpy as np
import jax
import jax.numpy as jnp

def _softmax(x, axis=-1):
    return jax.nn.softmax(x, axis=axis)

def _gelu(x):
    return jax.nn.gelu(x, approximate=True)

def _silu(x):
    return jax.nn.silu(x)

def _sigmoid(x):
    return jax.nn.sigmoid(x)

def _layernorm(x, axis=-1, eps=1e-05):
    m = jnp.mean(x, axis=axis, keepdims=True)
    v = jnp.var(x, axis=axis, keepdims=True)
    return (x - m) / jnp.sqrt(v + eps)

def _scatter_add(tgt, idx, src, axis=0):
    return tgt.at[idx].add(src)

def _segment_sum(src, seg, n):
    return jax.ops.segment_sum(src, seg, n)
kernel_name = 'mk_adj_ffn_d2_adj_r2_287ffd'

def setup_inputs(seed: int=0):
    np.random.seed(seed)
    _w = jnp.asarray

    def _rec_inputs():
        import jax
        import jax.numpy as jnp
        _gk = jax.random.key(seed)
        x = -0.0003929 + 0.9999 * jax.random.normal(jax.random.fold_in(_gk, 1), (32, 256, 256), jnp.float32)
        _w = (1.0 + jnp.arange(256, dtype=jnp.float32)) ** (-0.5)
        _w = _w / _w.mean()
        _pij = jnp.clip(0.0078125 * _w[:, None] * _w[None, :], 0.0, 1.0)
        _a = jax.random.uniform(jax.random.fold_in(_gk, 2), (256, 256)) < _pij
        _a = jnp.logical_or(_a, jnp.eye(256, dtype=bool))
        _af = _a.astype(jnp.float32)
        _af = _af * jax.random.uniform(jax.random.fold_in(_gk, 3), (256, 256), jnp.float32, 0.05, 1)
        adj = _af
        return (x, adj)
    x, adj = _rec_inputs()

    def _L0_gnn_setup():
        import jax, jax.numpy as jnp
        import numpy as np
        B, N, D, O = (8, 2048, 256, 256)
        key = jax.random.key(seed)
        k1, k2, k3, k4 = jax.random.split(key, 4)
        x = jax.random.normal(k1, (B, N, D), dtype=jnp.float32)
        adj = jax.random.uniform(k2, (N, N), dtype=jnp.float32)
        weight = jax.random.normal(k3, (D, O), dtype=jnp.float32) * 0.02
        bias = jax.random.normal(k4, (O,), dtype=jnp.float32) * 0.02
        return {'x': x, 'adj': adj, 'weight': weight, 'bias': bias}
    _L0_gnn_all = _L0_gnn_setup()
    _L0_gnn_in = {k: v for k, v in _L0_gnn_all.items() if k in ('weight', 'bias')}
    del _L0_gnn_all

    def _L0_ffn_setup():
        import jax, jax.numpy as jnp
        import numpy as np
        FP8_MAX = 448.0
        K, N = (256, 256)
        key = jax.random.key(seed)
        kx, kw = jax.random.split(key)
        x = jax.random.normal(kx, (8, 4096, K), dtype=jnp.float32)
        weight = jax.random.normal(kw, (K, N), dtype=jnp.float32) * 0.02
        return {'x': x, 'weight': weight}
    _L0_ffn_all = _L0_ffn_setup()
    _L0_ffn_in = {k: v for k, v in _L0_ffn_all.items() if k in ('weight',)}
    del _L0_ffn_all

    def _L1_gnn_setup():
        import jax, jax.numpy as jnp
        import numpy as np
        B, N, D = (8, 1024, 256)
        key = jax.random.key(seed)
        k1, k2, k3, k4, k5 = jax.random.split(key, 5)
        neuron_states = jax.random.normal(k1, (B, N, D), dtype=jnp.float32)
        adjacency = jax.random.randint(k2, (N, N), 0, 2).astype(jnp.float32)
        scale = 1.0 / np.sqrt(D)
        Wq = jax.random.normal(k3, (D, D), dtype=jnp.float32) * scale
        Wk = jax.random.normal(k4, (D, D), dtype=jnp.float32) * scale
        Wv = jax.random.normal(k5, (D, D), dtype=jnp.float32) * scale
        return {'neuron_states': neuron_states, 'adjacency': adjacency, 'Wq': Wq, 'Wk': Wk, 'Wv': Wv}
    _L1_gnn_all = _L1_gnn_setup()
    _L1_gnn_in = {k: v for k, v in _L1_gnn_all.items() if k in ('Wq', 'Wk', 'Wv')}
    del _L1_gnn_all

    def _L1_ffn_setup():
        import jax, jax.numpy as jnp
        import numpy as np
        MARK_AX = 0
        OP_MUL = 1
        OPCODE_BASE = 2
        ALU_LO, ALU_HI = (64, 80)
        AX_CARRY_LO, AX_CARRY_HI = (96, 112)
        OUTPUT_LO, OUTPUT_HI = (128, 144)
        NIB_A, NIB_B, RESULT, OP_START = (0, 1, 2, 3)
        GE_DIM = 160
        N_POS = 8
        N_LAYERS = 7
        OPCODE = 27

        def _decode_nibble(x16):
            return jnp.argmax(x16 > 0.5, axis=-1).astype(x16.dtype)
        key = jax.random.key(seed)
        k1, k2, k3 = jax.random.split(key, 3)
        x_bd = jax.random.uniform(k1, (4, 4096, 256), dtype=jnp.float32)
        W = jax.random.normal(k2, (N_LAYERS, GE_DIM, GE_DIM), dtype=jnp.float32) * 0.05
        b = jax.random.normal(k3, (N_LAYERS, GE_DIM), dtype=jnp.float32) * 0.01
        return {'x_bd': x_bd, 'W': W, 'b': b}
    _L1_ffn_all = _L1_ffn_setup()
    _L1_ffn_in = {k: v for k, v in _L1_ffn_all.items() if k in ('W', 'b')}
    del _L1_ffn_all
    return {'x': x, 'adj': adj, 'L0_gnn_weight': _L0_gnn_in['weight'], 'L0_gnn_bias': _L0_gnn_in['bias'], 'L0_ffn_weight': _L0_ffn_in['weight'], 'L1_gnn_Wq': _L1_gnn_in['Wq'], 'L1_gnn_Wk': _L1_gnn_in['Wk'], 'L1_gnn_Wv': _L1_gnn_in['Wv'], 'L1_ffn_W': _L1_ffn_in['W'], 'L1_ffn_b': _L1_ffn_in['b']}

def reference(x, adj, L0_gnn_weight, L0_gnn_bias, L0_ffn_weight, L1_gnn_Wq, L1_gnn_Wk, L1_gnn_Wv, L1_ffn_W, L1_ffn_b):
    import jax
    import jax.numpy as jnp

    def _L0_gnn_ref(x, adj, weight, bias):
        import jax, jax.numpy as jnp
        import numpy as np
        B, N, D, O = (8, 2048, 256, 256)
        y = jnp.einsum('nm,bmd->bnd', adj, x)
        out = jnp.einsum('bnd,do->bno', y, weight) + bias
        return out

    def _L0_ffn_ref(x, weight):
        import jax, jax.numpy as jnp
        import numpy as np
        FP8_MAX = 448.0
        K, N = (256, 256)
        B, S, _ = x.shape
        x2d = x.reshape(-1, K)
        x_amax = jnp.max(jnp.abs(x2d))
        x_scale = FP8_MAX / jnp.maximum(x_amax, 1e-12)
        x_fp8 = jnp.clip(x2d * x_scale, -FP8_MAX, FP8_MAX).astype(jnp.float8_e4m3fn)
        w_amax = jnp.max(jnp.abs(weight))
        w_scale = FP8_MAX / jnp.maximum(w_amax, 1e-12)
        w_fp8 = jnp.clip(weight.T * w_scale, -FP8_MAX, FP8_MAX).astype(jnp.float8_e4m3fn)
        res = jnp.matmul(x_fp8.astype(jnp.float32), w_fp8.astype(jnp.float32).T)
        out = res * (1.0 / x_scale * (1.0 / w_scale))
        return out.reshape(B, S, N).astype(x.dtype)

    def _L1_gnn_ref(neuron_states, adjacency, Wq, Wk, Wv):
        import jax, jax.numpy as jnp
        import numpy as np
        B, N, D = (8, 1024, 256)
        q = jnp.einsum('bnd,ed->bne', neuron_states, Wq)
        k = jnp.einsum('bnd,ed->bne', neuron_states, Wk)
        v = jnp.einsum('bnd,ed->bne', neuron_states, Wv)
        rel = jnp.einsum('bnd,bmd->bnm', q, k)
        rel = adjacency.T[None, :, :] * rel
        rel = rel / jnp.linalg.norm(rel, axis=2, keepdims=True)
        return jnp.einsum('bnm,bmd->bnd', rel, v)

    def _L1_ffn_ref(x_bd, W, b):
        import jax, jax.numpy as jnp
        import numpy as np
        MARK_AX = 0
        OP_MUL = 1
        OPCODE_BASE = 2
        ALU_LO, ALU_HI = (64, 80)
        AX_CARRY_LO, AX_CARRY_HI = (96, 112)
        OUTPUT_LO, OUTPUT_HI = (128, 144)
        NIB_A, NIB_B, RESULT, OP_START = (0, 1, 2, 3)
        GE_DIM = 160
        N_POS = 8
        N_LAYERS = 7
        OPCODE = 27

        def _decode_nibble(x16):
            return jnp.argmax(x16 > 0.5, axis=-1).astype(x16.dtype)
        B, S, D = x_bd.shape
        mask = (x_bd[..., MARK_AX] >= 0.5) & (x_bd[..., OP_MUL] >= 0.5)
        a_lo = _decode_nibble(x_bd[..., ALU_LO:ALU_LO + 16])
        a_hi = _decode_nibble(x_bd[..., ALU_HI:ALU_HI + 16])
        b_lo = _decode_nibble(x_bd[..., AX_CARRY_LO:AX_CARRY_LO + 16])
        b_hi = _decode_nibble(x_bd[..., AX_CARRY_HI:AX_CARRY_HI + 16])
        op_val = x_bd[..., OPCODE_BASE + OPCODE]
        x_ge = jnp.zeros((B, S, N_POS, GE_DIM), dtype=x_bd.dtype)
        x_ge = x_ge.at[..., 0, NIB_A].set(a_lo)
        x_ge = x_ge.at[..., 1, NIB_A].set(a_hi)
        x_ge = x_ge.at[..., 0, NIB_B].set(b_lo)
        x_ge = x_ge.at[..., 1, NIB_B].set(b_hi)
        x_ge = x_ge.at[..., :, OP_START + OPCODE].set(op_val[..., None])
        h = x_ge
        for i in range(N_LAYERS):
            h = jnp.einsum('bspd,ed->bspe', h, W[i]) + b[i]
            if i < N_LAYERS - 1:
                h = jax.nn.relu(h)
        res_lo = jnp.clip(jnp.round(h[..., 0, RESULT]), 0, 15).astype(jnp.int32)
        res_hi = jnp.clip(jnp.round(h[..., 1, RESULT]), 0, 15).astype(jnp.int32)
        m = mask[..., None].astype(x_bd.dtype)
        add_lo = 2.0 * jax.nn.one_hot(res_lo, 16, dtype=x_bd.dtype) * m
        add_hi = 2.0 * jax.nn.one_hot(res_hi, 16, dtype=x_bd.dtype) * m
        out = x_bd.at[..., OUTPUT_LO:OUTPUT_LO + 16].add(add_lo)
        out = out.at[..., OUTPUT_HI:OUTPUT_HI + 16].add(add_hi)
        return out
    x = x + _L0_gnn_ref(_layernorm(x, axis=-1), adj, L0_gnn_weight, L0_gnn_bias)
    x = x + _L0_ffn_ref(_layernorm(x, axis=-1), L0_ffn_weight)
    x = x + _L1_gnn_ref(_layernorm(x, axis=-1), adj, L1_gnn_Wq, L1_gnn_Wk, L1_gnn_Wv)
    x = x + _L1_ffn_ref(_layernorm(x, axis=-1), L1_ffn_W, L1_ffn_b)
    return x

_drawn_inputs = setup_inputs


def setup_inputs(seed=0):
    import zlib

    import numpy as np

    out = dict(_drawn_inputs(seed))
    spreads = {}
    factors = {}
    for name, (base, spread) in spreads.items():
        noise = np.random.default_rng([zlib.crc32(name.encode()), seed]).standard_normal(out[name].shape)
        drawn = base * np.exp(spread * noise) if base else spread * noise
        out[name] = jnp.asarray(drawn.astype(out[name].dtype))
    for name, factor in factors.items():
        out[name] = (out[name] * factor).astype(out[name].dtype)
    return out
```

```python
from contextlib import ExitStack

import concourse.bass as bass
from concourse import mybir
from concourse.alu_op_type import AluOpType as ALU

ACT = mybir.ActivationFunctionType
AX = mybir.AxisListType
F32 = mybir.dt.float32
BF16 = mybir.dt.bfloat16
I32 = mybir.dt.int32

P = 128
EPS = 1e-5
FP8_MAX = 448.0
AMAX_FLOOR = 1e-12
MAGIC_SHIFT = float(1 << 20)
MIN_NORMAL = 2.0 ** -6
EXPONENT_BITS = 0x7F800000
HALF_BIT = 0x00400000
INT_MAGIC = float(1 << 23)

MARK_COL, MUL_COL, OPCODE_COL = 0, 1, 29
NIBBLES_COL, NIBBLES = 64, 4
OUTPUT_COL, OUTPUT_W = 128, 32
NIB = 16
GE_A, GE_B, GE_OP, GE_RESULT = 0, 1, 30, 2
N_POS_USED = 2


def mlp_columns(layers, ge):
    rem, hid = ge - P, layers - 2
    chunks = P // rem
    widths = {"sq": hid * (2 * P + rem), "rm": hid * chunks * P, "in": N_POS_USED * (P + rem),
              "out_m": rem, "out_r": P, "b_main": layers, "b_rem": layers, "b_out": 1}
    at, start = {}, 0
    for name, width in widths.items():
        at[name] = slice(start, start + width)
        start += width
    return at, start


def adj_ffn_kernel(nc, x, adj, adj_turned, gnn_w, gnn_b, ffn_w, wq, wk, wv_turned, mlp, layers, ge, out):
    B, N, D = x.shape
    LAYERS, GE = layers, ge
    NT = N // P
    DT = D // P
    TILES = B * NT
    UB = 2
    UT = UB * NT
    UNITS = B // UB
    UW = UT * D
    BW = NT * D
    REM = GE - P
    CHUNKS = P // REM
    CW = 512
    SLOTS = CW * CHUNKS // N_POS_USED // P
    HALF = SLOTS // 2
    BLOCKS = TILES // SLOTS
    HID = LAYERS - 2
    RELUS = LAYERS - 1
    NF = NIBBLES + 1

    x_rows = x.rearrange("b (h p) d -> p (b h) d", p=P)
    out_rows = out.rearrange("b (h p) d -> p (b h) d", p=P)

    with ExitStack() as ctx:
        def sb(name, shape, dt=F32):
            return ctx.enter_context(nc.sbuf_tensor(name, shape, dt))

        def sem(name):
            return ctx.enter_context(nc.semaphore(name))

        x_all = sb("x_all", [P, TILES, D])
        xn_all = sb("xn_all", [P, TILES, D])
        ident = sb("ident", [P, P])
        ident_bf = sb("ident_bf", [P, P], BF16)
        eps = sb("eps", [P, 1])
        ones = sb("ones", [P, TILES])
        adj_nat = sb("adj_nat", [P, NT, N])
        adj_t = sb("adj_t", [P, NT, N])
        gnn_w_sb = sb("gnn_w_sb", [P, DT, D])
        ffn_w_sb = sb("ffn_w_sb", [P, DT, D])
        ffn_wq = sb("ffn_wq", [P, DT, D], BF16)
        wq_sb = sb("wq_sb", [P, DT, D])
        wk_sb = sb("wk_sb", [P, DT, D])
        qk_w = sb("qk_w", [P, DT, D])
        wv_t = sb("wv_t", [P, DT, D])
        at, mlp_width = mlp_columns(LAYERS, GE)
        mlp_sb = sb("mlp_sb", [P, mlp_width])
        w_sq = mlp_sb[:, at["sq"]].rearrange("p (l e) -> p l e", l=HID)
        w_mm, w_rr, w_mr = w_sq[:, :, 0:P], w_sq[:, :, P:2 * P], w_sq[:, :, 2 * P:2 * P + REM]
        w_rm = mlp_sb[:, at["rm"]].rearrange("p (l c e) -> p l c e", l=HID, c=CHUNKS)
        w_in = mlp_sb[:, at["in"]]
        w_in_m = w_in[:, 0:N_POS_USED * P].rearrange("p (a e) -> p a e", a=N_POS_USED)
        w_in_r = w_in[:, N_POS_USED * P:].rearrange("p (a e) -> p a e", a=N_POS_USED)
        w6_m, w6_r = mlp_sb[:, at["out_m"]], mlp_sb[:, at["out_r"]]
        b_main, b_rem, b_out = mlp_sb[:, at["b_main"]], mlp_sb[:, at["b_rem"]], mlp_sb[:, at["b_out"]]
        iota_slot = sb("iota_slot", [P, TILES])
        iota_down = sb("iota_down", [P, NIBBLES * NIB])
        iota_up = sb("iota_up", [P, NIB])

        buf_w = sb("buf_w", [P, UW])
        buf_m = sb("buf_m", [P, UW])
        buf_t = sb("buf_t", [P, UW])
        buf_n = sb("buf_n", [P, UW])
        buf_1 = sb("buf_1", [P, UW])
        buf_2 = sb("buf_2", [P, UW])
        buf_3 = sb("buf_3", [P, UW])
        buf_4 = sb("buf_4", [P, UW])
        buf_5 = sb("buf_5", [P, UW])
        q_rows = sb("q_rows", [P, UT, D], BF16)
        q_t = sb("q_t", [P, UB, DT, N], BF16)

        stats = sb("stats", [P, 2, UT, 6])
        mv = sb("mv", [P, 2, UT, 2])
        std = sb("std", [P, 4, UT])
        rstd = sb("rstd", [P, 4, UT])
        amax_u = sb("amax_u", [P, UNITS])
        amax_p = sb("amax_p", [P, 2])
        amax = sb("amax", [P, 2])
        fscale = sb("fscale", [P, 2])
        fscale_up = sb("fscale_up", [P, 1])
        finv = sb("finv", [P, 2])
        fout = sb("fout", [P, 1])
        most = sb("most", [P, 1])
        most_i = sb("most_i", [P, 1], I32)
        found = sb("found", [P, N_POS_USED, SLOTS])

        psum = ctx.enter_context(nc.psum_tensor("psum", [P, 8, 512], F32))

        bias_bc = q_rows[:, 0:2, :].rearrange("p t d -> p (t d)").bitcast(F32)

        def tiles(buf):
            return buf[:].rearrange("p (t d) -> p t d", d=D)

        xn_a = [tiles(buf_n), tiles(buf_1)]
        y_t = [b[:].rearrange("p (b e n) -> p b e n", b=UB, e=DT) for b in (buf_2, buf_3)]
        xn_b = tiles(buf_n)
        xn_t = buf_1[:].rearrange("p (e b n) -> p e b n", e=DT, b=UB)
        qk_t = buf_2[:].rearrange("p (e b n) -> p e b n", e=DT, b=UB)
        v_sb = buf_3[:].rearrange("p (b m d) -> p b m d", b=UB, m=NT)
        rel_t = buf_4[:].rearrange("p (b m n) -> p b m n", b=UB, m=NT)
        rel_sq = buf_5[:].rearrange("p (b m n) -> p b m n", b=UB, m=NT)
        hit = wq_sb[:].rearrange("p e d -> p (e d)")[:, 0:UT * NIBBLES * NIB].rearrange("p (t i) -> p t i", t=UT)
        code = wk_sb[:].rearrange("p e d -> p (e d)")[:, 0:TILES * NIBBLES].rearrange("p (t g) -> p t g", g=NIBBLES)
        feats = gnn_w_sb[:].rearrange("p e d -> p (e d)")[:, 0:NF * TILES].rearrange("p (f t) -> p f t", f=NF)
        free = ffn_w_sb[:].rearrange("p e d -> p (e d)")
        mask = free[:, 0:2 * TILES].rearrange("p (a t) -> p a t", a=2)
        pos, slot_of, spread_r = (free[:, i * TILES:(i + 1) * TILES] for i in (2, 3, 4))
        digit = free[:, 5 * TILES:(5 + N_POS_USED) * TILES].rearrange("p (t a) -> p t a", a=N_POS_USED)
        f_rows = buf_w[:].rearrange("p (s f) -> p s f", f=P)
        f_t = buf_m[:].rearrange("p (h c) -> p h c", h=2)
        hid = [buf_1[:, 0:CW], buf_1[:, CW:2 * CW], buf_2[:, 0:CW], buf_2[:, CW:2 * CW]]
        hid_r = [buf_3[:, 0:CW], buf_5[:, 0:CW]]
        last_sb = buf_3[:, CW:2 * CW]
        sel = buf_4[:, 0:SLOTS * TILES].rearrange("p (s t) -> p s t", s=SLOTS)
        prod = buf_4[:, SLOTS * TILES:2 * SLOTS * TILES]
        onehot = xn_all[:, 0:TILES * OUTPUT_W // D, :].rearrange("p a b -> p (a b)")

        def unit(buf, k):
            return buf[:, bass.ds(UT * k, UT), :] if not isinstance(k, int) else buf[:, UT * k:UT * (k + 1), :]

        def half(buf, k, b):
            t = UT * k + NT * b
            return buf[:, bass.ds(t, NT), :] if not isinstance(k, int) else buf[:, t:t + NT, :]

        def column(buf, k):
            return buf[:, bass.ds(k, 1)] if not isinstance(k, int) else buf[:, k:k + 1]

        def after(k, first=0):
            return k >= first if isinstance(k, int) else True

        x_loaded = [sem("x_loaded_even"), sem("x_loaded_odd")]
        adj_loaded, gnn_loaded, ffn_loaded = sem("adj_loaded"), sem("gnn_loaded"), sem("ffn_loaded")
        att_loaded, mlp_loaded = sem("att_loaded"), sem("mlp_loaded")
        consts_ready, zeros_ready = sem("consts_ready"), sem("zeros_ready")
        ident_ready = sem("ident_ready")
        ln_stats = [sem(f"ln{i}_stats") for i in range(4)]
        ln_moments = [sem(f"ln{i}_moments") for i in range(4)]
        ln_std = [sem(f"ln{i}_std") for i in range(4)]
        ln_rstd = [sem(f"ln{i}_rstd") for i in range(4)]
        ln_rows = [sem(f"ln{i}_rows") for i in range(4)]
        y_done, y_moved, gnn_done, bias_added = sem("y_done"), sem("y_moved"), sem("gnn_done"), sem("bias_added")
        x1_added, amax_seen = sem("x1_added"), sem("amax_seen")
        prep_done, prep_moved = sem("prep_done"), sem("prep_moved")
        amax_parts, amax_ready, scale_step, scales_ready = (
            sem("amax_parts"), sem("amax_ready"), sem("scale_step"), sem("scales_ready"))
        wq_step, ffn_wq_ready = sem("wq_step"), sem("ffn_wq_ready")
        scaled_ready, exponent_ready, magic_ready = sem("scaled_ready"), sem("exponent_ready"), sem("magic_ready")
        summed_ready, q_ready = sem("summed_ready"), sem("q_ready")
        q_turned, q_t_ready, ffn_done, x2_added = sem("q_turned"), sem("q_t_ready"), sem("ffn_done"), sem("x2_added")
        xt_turned, xt_moved, qk_done, qk_moved = sem("xt_turned"), sem("xt_moved"), sem("qk_done"), sem("qk_moved")
        v_done, v_moved, rel_done, rel_masked = sem("v_done"), sem("v_moved"), sem("rel_done"), sem("rel_masked")
        sq_ready, ss_done, norm_ready, inv_ready = sem("sq_ready"), sem("ss_done"), sem("norm_ready"), sem("inv_ready")
        att_done, x3_added = sem("att_done"), sem("x3_added")
        hits_ready, codes_ready, base_ready = sem("hits_ready"), sem("codes_ready"), sem("base_ready")
        base_left, base_right, output_stored = sem("base_left"), sem("base_right"), sem("output_stored")
        f_zeroed, mask_step, feats_step, slots_step = sem("f_zeroed"), sem("mask_step"), sem("feats_step"), sem("slots_step")
        counted, most_ready, most_int = sem("counted"), sem("most_ready"), sem("most_int")
        selected, product, f_ready = sem("selected"), sem("product"), sem("f_ready")
        f_turned, f_t_ready = sem("f_turned"), sem("f_t_ready")
        main_done = [sem(f"main{c}_done") for c in range(CHUNKS)]
        hid_ready = [sem(f"hid{c}_ready") for c in range(CHUNKS)]
        rem_done, hid_r_ready = sem("rem_done"), sem("hid_r_ready")
        last_done, last_ready, last_turned = sem("last_done"), sem("last_ready"), sem("last_turned")
        clip_step, spread_step, spread_sum = sem("clip_step"), sem("spread_step"), sem("spread_sum")
        digit_zeroed, digit_ready, final_step, final_ready = (
            sem("digit_zeroed"), sem("digit_ready"), sem("final_step"), sem("final_ready"))

        waited = {}

        def stand_alone(engine, name):
            if name not in waited:
                waited[name] = sem(f"waited_{name}")
            engine.sem_inc(waited[name], 1)

        Y, G = (1, 2), (3, 4)
        QT, QK, FFN, VB, REL, XT, ATT, SS = 0, (1, 2), (3, 4), (5, 6), (1, 2), (3, 4), (5, 6), 7
        PREP = 7
        MAIN, RB, LAST, FT = (1, 2, 3, 4), 5, 0, (6, 7)

        block = ctx.enter_context(nc.Block())

        @block.sync
        def _(sp):
            for par in range(2):
                sp.dma_start(unit(x_all, par), unit(x_rows, par)).then_inc(x_loaded[par], 16)
            with sp.Fori(1, UNITS // 2) as j:
                for par in range(2):
                    sp.wait_ge(x_loaded[par], 16 * j)
                    stand_alone(sp, "sp")
                    sp.dma_start(unit(x_all, 2 * j + par), unit(x_rows, 2 * j + par)).then_inc(x_loaded[par], 16)

            def store(k):
                sp.wait_ge(base_ready, k + 1)
                stand_alone(sp, "sp")
                if after(k, 1):
                    sp.wait_ge(base_left, 16 * k)
                    sp.wait_ge(base_right, 16 * k)
                stand_alone(sp, "sp")
                sp.dma_start(unit(out_rows, k)[:, :, 0:OUTPUT_COL],
                             unit(x_all, k)[:, :, 0:OUTPUT_COL]).then_inc(base_left, 16)
                sp.dma_start(unit(out_rows, k)[:, :, OUTPUT_COL + OUTPUT_W:D],
                             unit(x_all, k)[:, :, OUTPUT_COL + OUTPUT_W:D]).then_inc(base_right, 16)

            store(0)
            with sp.Fori(1, UNITS) as k:
                store(k)
            sp.wait_ge(final_ready, 1)
            sp.dma_start(out_rows[:, :, OUTPUT_COL:OUTPUT_COL + OUTPUT_W],
                         x_all[:, :, OUTPUT_COL:OUTPUT_COL + OUTPUT_W]).then_inc(output_stored, 16)
            sp.wait_ge(base_left, 16 * UNITS)
            sp.wait_ge(base_right, 16 * UNITS)
            sp.wait_ge(output_stored, 16)

        @block.gpsimd
        def _(pool):
            pool.memset(ident[:], 0.0).then_inc(zeros_ready, 1)
            pool.wait_ge(zeros_ready, 1)
            pool.affine_select(out=ident[:], in_=ident[:], compare_op=ALU.not_equal, fill=1.0, base=0,
                               pattern=[[-1, P]], channel_multiplier=1).then_inc(ident_ready, 1)
            pool.memset(eps[:], EPS)
            pool.memset(ones[:], 1.0).then_inc(consts_ready, 1)
            pool.wait_ge(ident_ready, 1)
            pool.tensor_copy(ident_bf[:], ident[:]).then_inc(consts_ready, 1)
            pool.iota(iota_slot[:], [[1, TILES]], base=1, channel_multiplier=0, allow_small_or_imprecise_dtypes=True)
            pool.iota(iota_down[:], [[0, NIBBLES], [-1, NIB]], base=NIB, channel_multiplier=0,
                      allow_small_or_imprecise_dtypes=True)
            pool.iota(iota_up[:], [[1, NIB]], base=1, channel_multiplier=0,
                      allow_small_or_imprecise_dtypes=True).then_inc(consts_ready, 1)
            pool.wait_ge(gnn_loaded, 32)

            def add_bias(k):
                pool.wait_ge(ln_rows[0], k + 1)
                pool.tensor_tensor(unit(x_all, k), unit(x_all, k),
                                   bias_bc.unsqueeze(1).to_broadcast([P, UT, D]), ALU.add).then_inc(bias_added, 1)

            with pool.Fori(0, UNITS) as k:
                add_bias(k)

            pool.wait_ge(amax_parts, 2)
            pool.partition_all_reduce(amax[:], amax_p[:], P, bass.bass_isa.ReduceOp.max).then_inc(amax_ready, 1)

            with pool.Fori(0, UNITS) as k:
                pool.wait_ge(ln_rows[3], k + 1)
                pool.tensor_tensor(unit(x_all, k), unit(x_all, k), unit(xn_all, k), ALU.add).then_inc(base_ready, 1)

            pool.memset(buf_w[:], 0.0).then_inc(f_zeroed, 1)
            pool.wait_ge(counted, 1)
            pool.partition_all_reduce(most[:], pos[:, TILES - 1:TILES], P, bass.bass_isa.ReduceOp.max).then_inc(most_ready, 1)

        @block.scalar
        def _(act):
            def load(dst, src, s):
                act.dma_start(dst, src).then_inc(s, 16)

            def rows(w):
                return w.rearrange("(t p) d -> p t d", p=P)

            load(adj_t[:], rows(adj_turned), adj_loaded)
            load(gnn_w_sb[:], rows(gnn_w), gnn_loaded)
            load(bias_bc, gnn_b.partition_broadcast(P), gnn_loaded)
            load(ffn_w_sb[:], rows(ffn_w), ffn_loaded)
            load(adj_nat[:], rows(adj), att_loaded)
            for dst, src in ((wq_sb, wq), (wk_sb, wk), (wv_t, wv_turned)):
                load(dst[:], rows(src), att_loaded)
            load(mlp_sb[:], mlp, mlp_loaded)

            def root(n, k, src=None):
                act.wait_ge(ln_moments[n], k + 1)
                act.activation(std[:, n], mv[:, n % 2, :, 1], ACT.Sqrt, bias=eps[:, 0:1]).then_inc(ln_std[n], 1)

            act.wait_ge(consts_ready, 1)
            root(0, 0)

            def phase_a(k, par, last=False):
                if not last:
                    root(0, k + 1)
                for b in range(UB):
                    act.wait_ge(y_done, UB * k + b + 1)
                    act.copy(y_t[par][:, b].rearrange("p e n -> p (e n)"), psum[:, Y[b], :]).then_inc(y_moved, 1)
                if after(k, 1):
                    root(1, k - 1)

            phase_a(0, 0)
            phase_a(1, 1)
            with act.Fori(1, UNITS // 2 - 1) as j:
                for par in range(2):
                    phase_a(2 * j + par, par)
            phase_a(UNITS - 2, 0)
            phase_a(UNITS - 1, 1, last=True)

            root(1, UNITS - 1)
            act.wait_ge(prep_done, 1)
            act.copy(qk_w[:].rearrange("p e d -> p (e d)"), psum[:, PREP, :]).then_inc(prep_moved, 1)

            def scale_up(k):
                if after(k, 1):
                    act.wait_ge(q_ready, k)
                act.activation(buf_w[:], unit(xn_all, k).rearrange("p t d -> p (t d)"), ACT.Copy,
                               scale=fscale_up[:, 0:1]).then_inc(scaled_ready, 1)

            def move_q(k):
                act.wait_ge(q_turned, k + 1)
                act.copy(q_t[:].rearrange("p b e n -> p (b e n)"), psum[:, QT, :].bitcast(BF16)).then_inc(q_t_ready, 1)

            def move_xt(k):
                for b in range(UB):
                    act.wait_ge(xt_turned, UB * k + b + 1)
                    act.copy(xn_t[:, :, b, :], psum[:, XT[b], :].rearrange("p (e n) -> p e n", e=DT)).then_inc(xt_moved, 1)

            def move_qk(k):
                for e in range(DT):
                    act.wait_ge(qk_done, DT * k + e + 1)
                    act.copy(qk_t[:, e].rearrange("p b n -> p (b n)"), psum[:, QK[e], :]).then_inc(qk_moved, 1)

            def move_v(k, b):
                act.wait_ge(v_done, UB * k + b + 1)
                act.copy(v_sb[:, b].rearrange("p m d -> p (m d)"), psum[:, VB[b], :]).then_inc(v_moved, 1)

            def square_rel(k):
                for b in range(UB):
                    act.wait_ge(rel_masked, UB * k + b + 1)
                    act.activation(rel_sq[:, b], rel_t[:, b], ACT.Square).then_inc(sq_ready, 1)

            def root_norm(k):
                act.wait_ge(ss_done, k + 1)
                act.activation(std[:, 0], psum[:, SS, 0:UT], ACT.Sqrt).then_inc(norm_ready, 1)

            act.wait_ge(scales_ready, 1)
            scale_up(0)
            scale_up(1)
            move_q(0)
            root(2, 0)
            move_xt(0)

            def phase_b(k, final=None):
                nxt = final is None or final < UNITS - 1
                nxt2 = final is None or final < UNITS - 2
                if nxt:
                    move_q(k + 1)
                if after(k, 1):
                    root(3, k - 1)
                move_qk(k)
                if nxt2:
                    scale_up(k + 2)
                move_v(k, 0)
                if nxt:
                    root(2, k + 1)
                move_v(k, 1)
                square_rel(k)
                if nxt:
                    move_xt(k + 1)
                root_norm(k)

            phase_b(0)
            with act.Fori(1, UNITS - 2) as k:
                phase_b(k)
            phase_b(UNITS - 2, UNITS - 2)
            phase_b(UNITS - 1, UNITS - 1)
            root(3, UNITS - 1)

            act.wait_ge(mlp_loaded, 16)

            def relu(dst, src, bias, s):
                act.activation(dst, src, ACT.Relu, bias=bias).then_inc(s, 1)

            def mlp_block(j):
                for h in range(2):
                    act.wait_ge(f_turned, 2 * j + h + 1)
                    act.copy(f_t[:, h, :], psum[:, FT[h], :]).then_inc(f_t_ready, 1)
                for l in range(RELUS):
                    act.wait_ge(rem_done, RELUS * j + l + 1)
                    relu(hid_r[l % 2], psum[:, RB, :], b_rem[:, l:l + 1], hid_r_ready)
                    for c in range(0, CHUNKS, 2):
                        act.wait_ge(main_done[c], RELUS * j + l + 1)
                        relu(hid[c], psum[:, MAIN[c], :], b_main[:, l:l + 1], hid_ready[c])
                act.wait_ge(last_done, j + 1)
                act.activation(last_sb, psum[:, LAST, :], ACT.Identity, bias=b_out[:, 0:1]).then_inc(last_ready, 1)

            mlp_block(0)
            act.wait_ge(most_int, 1)
            n = act.value_load(most_i[0:1, 0:1])
            with act.Fori(1, BLOCKS) as j:
                with act.If(SLOTS * j < n):
                    mlp_block(j)

        @block.tensor
        def _(pe):
            pe.wait_ge(adj_loaded, 16)
            pe.wait_ge(gnn_loaded, 32)

            def y_part(k, par):
                pe.wait_ge(ln_rows[0], k + 1)
                for b in range(UB):
                    if after(k, 1):
                        pe.wait_ge(y_moved, UB * (k - 1) + b + 1)
                    for e in range(DT):
                        for m in range(NT):
                            mm = pe.matmul(psum[:, Y[b], e * N:(e + 1) * N],
                                           xn_a[par][:, b * NT + m, e * P:(e + 1) * P], adj_t[:, m, :],
                                           start=m == 0, stop=m == NT - 1)
                    mm.then_inc(y_done, 1)

            def gnn_part(k, par):
                for b in range(UB):
                    pe.wait_ge(y_moved, UB * k + b + 1)
                    if after(k, 1):
                        pe.wait_ge(x1_added, UB * (k - 1) + b + 1)
                    for h in range(NT):
                        for e in range(DT):
                            mm = pe.matmul(psum[:, G[b], h * D:(h + 1) * D],
                                           y_t[par][:, b, e, h * P:(h + 1) * P], gnn_w_sb[:, e, :],
                                           start=e == 0, stop=e == DT - 1)
                    mm.then_inc(gnn_done, 1)

            y_part(0, 0)
            y_part(1, 1)
            gnn_part(0, 0)
            with pe.Fori(1, UNITS // 2) as j:
                for par in range(2):
                    y_part(2 * j + par, par)
                    gnn_part(2 * j + par - 1, 1 - par)
            gnn_part(UNITS - 1, 1)

            pe.wait_ge(att_loaded, 64)
            for i in range(DT):
                for e in range(DT):
                    mm = pe.matmul(psum[:, PREP, i * D:(i + 1) * D], wq_sb[:, e, i * P:(i + 1) * P], wk_sb[:, e, :],
                                   start=e == 0, stop=e == DT - 1)
            mm.then_inc(prep_done, 1)

            def turn_q(k):
                pe.wait_ge(q_ready, k + 1)
                if after(k, 1):
                    pe.wait_ge(q_t_ready, k)
                bank = psum[:, QT, :].bitcast(BF16)
                for b in range(UB):
                    for e in range(DT):
                        for m in range(NT):
                            at = ((b * DT + e) * NT + m) * P
                            mm = pe.transpose(bank[:, at:at + P], q_rows[:, b * NT + m, e * P:(e + 1) * P], ident_bf[:])
                mm.then_inc(q_turned, 1)

            def ffn(k):
                pe.wait_ge(q_t_ready, k + 1)
                for b in range(UB):
                    if after(k, 1):
                        pe.wait_ge(xt_moved, UB * (k - 1) + b + 1)
                    for h in range(NT):
                        for e in range(DT):
                            mm = pe.matmul(psum[:, FFN[b], h * D:(h + 1) * D], q_t[:, b, e, h * P:(h + 1) * P],
                                           ffn_wq[:, e, :], start=e == 0, stop=e == DT - 1)
                    mm.then_inc(ffn_done, 1)

            def turn_x(k):
                pe.wait_ge(ln_rows[2], k + 1)
                for b in range(UB):
                    for e in range(DT):
                        for m in range(NT):
                            at = (e * NT + m) * P
                            mm = pe.transpose(psum[:, XT[b], at:at + P], xn_b[:, b * NT + m, e * P:(e + 1) * P], ident[:])
                    mm.then_inc(xt_turned, 1)

            def qk(k):
                pe.wait_ge(xt_moved, UB * (k + 1))
                for o in range(DT):
                    if after(k, 1):
                        pe.wait_ge(rel_masked, UB * (k - 1) + o + 1)
                    for e in range(DT):
                        mm = pe.matmul(psum[:, QK[o], :], qk_w[:, e, o * P:(o + 1) * P],
                                       xn_t[:, e].rearrange("p b n -> p (b n)"), start=e == 0, stop=e == DT - 1)
                    mm.then_inc(qk_done, 1)

            def values(k):
                for b in range(UB):
                    if after(k, 1):
                        pe.wait_ge(x3_added, UB * (k - 1) + b + 1)
                    for m in range(NT):
                        for e in range(DT):
                            mm = pe.matmul(psum[:, VB[b], m * D:(m + 1) * D], xn_t[:, e, b, m * P:(m + 1) * P],
                                           wv_t[:, e, :], start=e == 0, stop=e == DT - 1)
                    mm.then_inc(v_done, 1)

            def relations(k):
                pe.wait_ge(qk_moved, DT * (k + 1))
                for b in range(UB):
                    for m in range(NT):
                        for e in range(DT):
                            mm = pe.matmul(psum[:, REL[b], m * N:(m + 1) * N], xn_t[:, e, b, m * P:(m + 1) * P],
                                           qk_t[:, e, b, :], start=e == 0, stop=e == DT - 1)
                    mm.then_inc(rel_done, 1)

            def attend(k):
                for b in range(UB):
                    pe.wait_ge(rel_masked, UB * k + b + 1)
                    pe.wait_ge(v_moved, UB * k + b + 1)
                    for h in range(NT):
                        for m in range(NT):
                            mm = pe.matmul(psum[:, ATT[b], h * D:(h + 1) * D], rel_t[:, b, m, h * P:(h + 1) * P],
                                           v_sb[:, b, m, :], start=m == 0, stop=m == NT - 1)
                    mm.then_inc(att_done, 1)

            def sum_squares(k):
                pe.wait_ge(sq_ready, UB * (k + 1))
                if after(k, 1):
                    pe.wait_ge(norm_ready, k)
                for b in range(UB):
                    for h in range(NT):
                        for m in range(NT):
                            mm = pe.matmul(psum[:, SS, b * NT + h:b * NT + h + 1], rel_sq[:, b, m, h * P:(h + 1) * P],
                                           ones[:, 0:1], start=m == 0, stop=m == NT - 1)
                mm.then_inc(ss_done, 1)

            pe.wait_ge(prep_moved, 1)
            pe.wait_ge(ident_ready, 1)
            pe.wait_ge(consts_ready, 2)
            pe.wait_ge(x1_added, UB * UNITS)
            pe.wait_ge(ffn_wq_ready, 1)
            turn_q(0)
            ffn(0)
            turn_x(0)

            def phase_b(k, last=False):
                if not last:
                    turn_q(k + 1)
                qk(k)
                if not last:
                    ffn(k + 1)
                values(k)
                relations(k)
                if not last:
                    turn_x(k + 1)
                attend(k)
                sum_squares(k)

            phase_b(0)
            with pe.Fori(1, UNITS - 1) as k:
                phase_b(k)
            phase_b(UNITS - 1, last=True)

            pe.wait_ge(mlp_loaded, 16)

            def mlp_block(j):
                pe.wait_ge(f_ready, j + 1)
                for h in range(2):
                    for s in range(HALF):
                        mm = pe.transpose(psum[:, FT[h], s * P:(s + 1) * P], f_rows[:, h * HALF + s, :], ident[:])
                    mm.then_inc(f_turned, 1)
                for c in range(CHUNKS):
                    if c % 2 == 0:
                        pe.wait_ge(f_t_ready, 2 * j + c // 2 + 1)
                    pe.matmul(psum[:, MAIN[c], :], w_in_m[:, c % 2, :], f_t[:, c // 2, :],
                              start=True, stop=True).then_inc(main_done[c], 1)
                for c in range(CHUNKS):
                    mm = pe.matmul(psum[REM * c:REM * (c + 1), RB, :], w_in_r[:, c % 2, :], f_t[:, c // 2, :],
                                   start=True, stop=True)
                mm.then_inc(rem_done, 1)
                for l in range(1, HID + 1):
                    done = RELUS * j + l

                    def from_main(c):
                        pe.wait_ge(hid_ready[c], done)
                        pe.matmul(psum[:, MAIN[c], :], w_mm[:, l - 1, :], hid[c], start=True, stop=False)

                    for c in range(CHUNKS - 1):
                        from_main(c)
                    pe.wait_ge(hid_r_ready, done)
                    pe.wait_ge(hid_ready[CHUNKS - 1], done)
                    for c in range(CHUNKS):
                        pe.matmul(psum[REM * c:REM * (c + 1), RB, :], w_mr[:, l - 1, :], hid[c],
                                  start=True, stop=False, skip_group_check=True)
                    pe.matmul(psum[:, RB, :], w_rr[:, l - 1, :], hid_r[(l - 1) % 2], start=False, stop=True,
                              skip_group_check=True).then_inc(rem_done, 1)
                    from_main(CHUNKS - 1)
                    for c in range(CHUNKS):
                        pe.matmul(psum[:, MAIN[c], :], w_rm[:, l - 1, c, :], hid_r[(l - 1) % 2],
                                  start=False, stop=True).then_inc(main_done[c], 1)
                for c in range(CHUNKS):
                    pe.wait_ge(hid_ready[c], RELUS * (j + 1))
                    pe.matmul(psum[REM * c:REM * (c + 1), LAST, :], w6_m[:], hid[c],
                              start=True, stop=False, skip_group_check=True)
                pe.wait_ge(hid_r_ready, RELUS * (j + 1))
                pe.matmul(psum[:, LAST, :], w6_r[:], hid_r[HID % 2], start=False, stop=True,
                          skip_group_check=True).then_inc(last_done, 1)
                pe.wait_ge(last_ready, j + 1)
                for s in range(HALF):
                    mm = pe.transpose(psum[:, FT[0], s * P:(s + 1) * P], last_sb[:, s * P:(s + 1) * P], ident[:])
                mm.then_inc(last_turned, 1)

            mlp_block(0)
            pe.wait_ge(most_int, 1)
            n = pe.value_load(most_i[0:1, 0:1])
            with pe.Fori(1, BLOCKS) as j:
                with pe.If(SLOTS * j < n):
                    mlp_block(j)

        @block.vector
        def _(dve):
            def moments(n, k):
                stand_alone(dve, "dve")
                for i in range(UT):
                    ins = dve.bn_stats(stats[:, n % 2, i], tile_of(x_all, k, i))
                ins.then_inc(ln_stats[n], 1)
                dve.wait_ge(ln_stats[n], k + 1)
                stand_alone(dve, "dve")
                for i in range(UT):
                    ins = dve.bn_aggr(mv[:, n % 2, i], stats[:, n % 2, i])
                ins.then_inc(ln_moments[n], 1)

            def tile_of(buf, k, i):
                return buf[:, UT * k + i, :]

            def normalise(n, k, dst):
                dve.wait_ge(ln_std[n], k + 1)
                dve.reciprocal(rstd[:, n], std[:, n]).then_inc(ln_rstd[n], 1)
                dve.wait_ge(ln_rstd[n], k + 1)
                for i in range(UT):
                    ins = dve.tensor_scalar(dst(i), tile_of(x_all, k, i), mv[:, n % 2, i, 0:1], rstd[:, n, i:i + 1],
                                            ALU.subtract, ALU.mult)
                ins.then_inc(ln_rows[n], 1)

            dve.wait_ge(ffn_loaded, 16)
            dve.tensor_reduce(amax_p[:, 1:2], ffn_w_sb[:].rearrange("p e d -> p (e d)"), AX.X, ALU.max,
                              apply_absolute_value=True).then_inc(amax_parts, 1)

            def first_norm(k, par, j):
                dve.wait_ge(x_loaded[par], 16 * (j + 1))
                moments(0, k)

            def first_rows(k, par):
                if after(k, 2):
                    dve.wait_ge(y_done, UB * (k - 1))
                normalise(0, k, lambda i: xn_a[par][:, i, :])

            def add_gnn(k):
                dve.wait_ge(bias_added, k + 1)
                for b in range(UB):
                    dve.wait_ge(gnn_done, UB * k + b + 1)
                    dve.tensor_tensor(half(x_all, k, b), psum[:, G[b], :].rearrange("p (h d) -> p h d", h=NT),
                                      half(x_all, k, b), ALU.add).then_inc(x1_added, 1)
                dve.wait_ge(x1_added, UB * (k + 1))

            def see_amax(k):
                dve.wait_ge(ln_rows[1], k + 1)
                dve.tensor_reduce(column(amax_u, k), unit(xn_all, k).rearrange("p t d -> p (t d)"), AX.X, ALU.max,
                                  apply_absolute_value=True).then_inc(amax_seen, 1)

            def phase_a(k, par, j, nxt=True):
                if nxt:
                    first_norm(k + 1, 1 - par, j + par)
                if after(k, 2):
                    see_amax(k - 2)
                if nxt:
                    first_rows(k + 1, 1 - par)
                if after(k, 1):
                    add_gnn(k - 1)
                    moments(1, k - 1)
                    normalise(1, k - 1, lambda i: tile_of(xn_all, k - 1, i))

            first_norm(0, 0, 0)
            first_rows(0, 0)
            phase_a(0, 0, 0)
            phase_a(1, 1, 0)
            with dve.Fori(1, UNITS // 2 - 1) as j:
                for par in range(2):
                    phase_a(2 * j + par, par, j)
            phase_a(UNITS - 2, 0, UNITS // 2 - 1)
            phase_a(UNITS - 1, 1, UNITS // 2 - 1, nxt=False)
            phase_a(UNITS, 0, UNITS // 2, nxt=False)
            see_amax(UNITS - 1)

            dve.wait_ge(amax_seen, UNITS)
            dve.tensor_reduce(amax_p[:, 0:1], amax_u[:], AX.X, ALU.max).then_inc(amax_parts, 1)
            dve.wait_ge(amax_ready, 1)
            dve.wait_ge(consts_ready, 3)
            dve.tensor_scalar(amax[:], amax[:], AMAX_FLOOR, None, ALU.max).then_inc(scale_step, 1)
            dve.wait_ge(scale_step, 1)
            dve.reciprocal(finv[:], amax[:]).then_inc(scale_step, 1)
            dve.wait_ge(scale_step, 2)
            dve.tensor_scalar(fscale[:], finv[:], FP8_MAX, None, ALU.mult).then_inc(scale_step, 1)
            dve.wait_ge(scale_step, 3)
            dve.tensor_scalar(fscale_up[:], fscale[:, 0:1], MAGIC_SHIFT, None, ALU.mult).then_inc(scales_ready, 1)
            dve.reciprocal(finv[:], fscale[:]).then_inc(scale_step, 1)
            dve.wait_ge(scale_step, 4)
            dve.tensor_tensor(fout[:], finv[:, 0:1], finv[:, 1:2], ALU.mult).then_inc(scale_step, 1)

            def exponents(m, w):
                return dve.tensor_scalar(m.bitcast(I32), w.bitcast(I32), EXPONENT_BITS, HALF_BIT,
                                         ALU.bitwise_and, ALU.bitwise_or)

            def at_least(m):
                return dve.tensor_scalar(m, m, 1.5 * MIN_NORMAL * MAGIC_SHIFT, None, ALU.max)

            def quantise(k):
                src = unit(xn_all, k).rearrange("p t d -> p (t d)")
                dve.wait_ge(scaled_ready, k + 1)
                exponents(buf_m[:], buf_w[:]).then_inc(exponent_ready, 1)
                dve.wait_ge(exponent_ready, k + 1)
                at_least(buf_m[:]).then_inc(magic_ready, 1)
                dve.wait_ge(magic_ready, k + 1)
                dve.scalar_tensor_tensor(out=buf_t[:], in0=src, scalar=fscale[:, 0:1], in1=buf_m[:],
                                         op0=ALU.mult, op1=ALU.add).then_inc(summed_ready, 1)
                dve.wait_ge(summed_ready, k + 1)
                if after(k, 1):
                    dve.wait_ge(q_turned, k)
                dve.tensor_tensor(q_rows[:].rearrange("p t d -> p (t d)"), buf_t[:], buf_m[:],
                                  ALU.subtract).then_inc(q_ready, 1)

            quantise(0)
            w_flat = ffn_w_sb[:].rearrange("p e d -> p (e d)")
            wa, wb, wc = (b[:, 0:DT * D] for b in (buf_1, buf_2, buf_3))
            dve.tensor_scalar(wa, w_flat, fscale[:, 1:2], MAGIC_SHIFT, ALU.mult, ALU.mult).then_inc(wq_step, 1)
            dve.wait_ge(wq_step, 1)
            exponents(wb, wa).then_inc(wq_step, 1)
            dve.wait_ge(wq_step, 2)
            at_least(wb).then_inc(wq_step, 1)
            dve.wait_ge(wq_step, 3)
            dve.scalar_tensor_tensor(out=wc, in0=w_flat, scalar=fscale[:, 1:2], in1=wb,
                                     op0=ALU.mult, op1=ALU.add).then_inc(wq_step, 1)
            dve.wait_ge(wq_step, 4)
            dve.tensor_tensor(ffn_wq[:].rearrange("p e d -> p (e d)"), wc, wb, ALU.subtract).then_inc(ffn_wq_ready, 1)

            def add_ffn(k):
                for b in range(UB):
                    dve.wait_ge(ffn_done, UB * k + b + 1)
                    dve.scalar_tensor_tensor(out=half(x_all, k, b), in0=psum[:, FFN[b], :].rearrange("p (h d) -> p h d", h=NT),
                                             scalar=fout[:, 0:1], in1=half(x_all, k, b),
                                             op0=ALU.mult, op1=ALU.add).then_inc(x2_added, 1)
                dve.wait_ge(x2_added, UB * (k + 1))

            def mask_relations(k):
                for b in range(UB):
                    dve.wait_ge(rel_done, UB * k + b + 1)
                    dve.tensor_tensor(rel_t[:, b], psum[:, REL[b], :].rearrange("p (m n) -> p m n", m=NT), adj_nat[:],
                                      ALU.mult).then_inc(rel_masked, 1)

            def add_att(k):
                dve.wait_ge(norm_ready, k + 1)
                dve.reciprocal(rstd[:, 0], std[:, 0]).then_inc(inv_ready, 1)
                dve.wait_ge(inv_ready, k + 1)
                for b in range(UB):
                    dve.wait_ge(att_done, UB * k + b + 1)
                    for h in range(NT):
                        i = b * NT + h
                        ins = dve.scalar_tensor_tensor(
                            out=tile_of(x_all, k, i), in0=psum[:, ATT[b], h * D:(h + 1) * D],
                            scalar=rstd[:, 0, i:i + 1], in1=tile_of(x_all, k, i), op0=ALU.mult, op1=ALU.add)
                    ins.then_inc(x3_added, 1)
                dve.wait_ge(x3_added, UB * (k + 1))

            def nibbles(k):
                dve.wait_ge(ln_rows[3], k + 1)
                dve.scalar_tensor_tensor(
                    out=hit, in0=unit(xn_all, k)[:, :, NIBBLES_COL:NIBBLES_COL + NIBBLES * NIB], scalar=0.5,
                    in1=iota_down[:].unsqueeze(1).to_broadcast([P, UT, NIBBLES * NIB]),
                    op0=ALU.is_gt, op1=ALU.mult).then_inc(hits_ready, 1)
                dve.wait_ge(hits_ready, k + 1)
                dve.tensor_reduce(unit(code, k), hit.rearrange("p t (g i) -> p t g i", g=NIBBLES),
                                  AX.X, ALU.max).then_inc(codes_ready, 1)

            def finish(k):
                add_att(k)
                moments(3, k)

            def fourth_rows(k):
                normalise(3, k, lambda i: tile_of(xn_all, k, i))

            dve.wait_ge(scale_step, 5)
            add_ffn(0)
            moments(2, 0)
            normalise(2, 0, lambda i: xn_b[:, i, :])
            quantise(1)

            def phase_b(k, final=None):
                nxt = final is None or final < UNITS - 1
                nxt2 = final is None or final < UNITS - 2
                if after(k, 1):
                    finish(k - 1)
                if nxt:
                    add_ffn(k + 1)
                    moments(2, k + 1)
                if after(k, 1):
                    fourth_rows(k - 1)
                if nxt:
                    normalise(2, k + 1, lambda i: xn_b[:, i, :])
                if after(k, 1):
                    nibbles(k - 1)
                mask_relations(k)
                if nxt2:
                    quantise(k + 2)

            phase_b(0)
            with dve.Fori(1, UNITS - 2) as k:
                phase_b(k)
            phase_b(UNITS - 2, UNITS - 2)
            phase_b(UNITS - 1, UNITS - 1)
            finish(UNITS - 1)
            fourth_rows(UNITS - 1)
            nibbles(UNITS - 1)

            def xn_col(c):
                return xn_all[:, :, c]

            dve.tensor_scalar(mask[:, 0], xn_col(MUL_COL), 0.5, None, ALU.is_ge).then_inc(mask_step, 1)
            dve.wait_ge(mask_step, 1)
            dve.scalar_tensor_tensor(out=mask[:, 1], in0=xn_col(MARK_COL), scalar=0.5, in1=mask[:, 0],
                                     op0=ALU.is_ge, op1=ALU.mult).then_inc(mask_step, 1)
            dve.wait_ge(mask_step, 2)
            dve.tensor_tensor_scan(pos, ones[:], mask[:, 1], 0.0, ALU.mult, ALU.add).then_inc(counted, 1)
            dve.wait_ge(counted, 1)
            dve.tensor_tensor(slot_of, pos, mask[:, 1], ALU.mult).then_inc(slots_step, 1)
            dve.wait_ge(codes_ready, UNITS)
            by_tile = feats[:, 0:NIBBLES, :].rearrange("p f t -> p t f")
            dve.tensor_scalar(by_tile, code, -1.0, float(NIB), ALU.mult, ALU.add).then_inc(feats_step, 1)
            dve.wait_ge(feats_step, 1)
            dve.scalar_tensor_tensor(out=by_tile, in0=code, scalar=0.0, in1=by_tile,
                                     op0=ALU.is_gt, op1=ALU.mult).then_inc(feats_step, 1)
            dve.tensor_copy(feats[:, NIBBLES, :], xn_col(OPCODE_COL)).then_inc(feats_step, 1)
            dve.memset(digit, 0.0).then_inc(digit_zeroed, 1)
            dve.wait_ge(most_ready, 1)
            dve.tensor_copy(most_i[:], most[:]).then_inc(most_int, 1)
            dve.wait_ge(slots_step, 1)
            dve.wait_ge(feats_step, 3)
            dve.wait_ge(f_zeroed, 1)
            dve.wait_ge(mlp_loaded, 16)

            def mlp_block(j):
                if after(j, 1):
                    dve.wait_ge(f_turned, 2 * j)
                slots = iota_slot[:, bass.ds(SLOTS * j, SLOTS)] if not isinstance(j, int) else iota_slot[:, 0:SLOTS]
                dve.tensor_tensor(sel, slot_of.unsqueeze(1).to_broadcast([P, SLOTS, TILES]),
                                  slots.unsqueeze(2).to_broadcast([P, SLOTS, TILES]), ALU.is_equal).then_inc(selected, 1)
                dve.wait_ge(selected, j + 1)
                prod_s = prod.rearrange("p (s t) -> p s t", s=SLOTS)
                steps = 2 * NF - 1
                for f in range(NF):
                    if f:
                        dve.wait_ge(product, steps * j + 2 * f)
                    elif after(j, 1):
                        dve.wait_ge(f_ready, j)
                    dve.tensor_tensor(prod_s, sel, feats[:, f, :].unsqueeze(1).to_broadcast([P, SLOTS, TILES]),
                                      ALU.mult).then_inc(product, 1)
                    dve.wait_ge(product, steps * j + 2 * f + 1)
                    dve.tensor_reduce(f_rows[:, :, f:f + 1], prod_s, AX.X,
                                      ALU.add).then_inc(product if f < NF - 1 else f_ready, 1)
                for l in range(RELUS):
                    for c in range(1, CHUNKS, 2):
                        dve.wait_ge(main_done[c], RELUS * j + l + 1)
                        dve.tensor_scalar(hid[c], psum[:, MAIN[c], :], b_main[:, l:l + 1], 0.0,
                                          ALU.add, ALU.max).then_inc(hid_ready[c], 1)
                dve.wait_ge(last_turned, j + 1)
                got = psum[:, FT[0], :].rearrange("p (s c r) -> p s c r", c=CHUNKS, r=REM)[:, :, :, 0]
                into = found[:].rearrange("p a (h s) -> p s h a", h=2)
                for a in range(N_POS_USED):
                    ins = dve.tensor_scalar(into[:, :, :, a], got[:, :, a:CHUNKS:N_POS_USED], 0.0, float(NIB - 1), ALU.max, ALU.min)
                ins.then_inc(clip_step, 1)
                dve.wait_ge(clip_step, 3 * j + 1)
                dve.tensor_scalar(found[:], found[:], INT_MAGIC, INT_MAGIC, ALU.add, ALU.subtract).then_inc(clip_step, 1)
                dve.wait_ge(clip_step, 3 * j + 2)
                dve.tensor_scalar(found[:], found[:], 1.0, None, ALU.add).then_inc(clip_step, 1)
                dve.wait_ge(clip_step, 3 * j + 3)
                prod_t = prod.rearrange("p (t s) -> p t s", s=SLOTS)
                for a in range(N_POS_USED):
                    if after(j, 1) or a:
                        dve.wait_ge(spread_sum, N_POS_USED * j + a)
                    else:
                        dve.wait_ge(digit_zeroed, 1)
                    dve.tensor_tensor(prod_t, sel.rearrange("p s t -> p t s"),
                                      found[:, a, :].unsqueeze(1).to_broadcast([P, TILES, SLOTS]),
                                      ALU.mult).then_inc(spread_step, 1)
                    dve.wait_ge(spread_step, 2 * (N_POS_USED * j + a) + 1)
                    dve.tensor_reduce(spread_r.unsqueeze(2), prod_t, AX.X, ALU.add).then_inc(spread_step, 1)
                    dve.wait_ge(spread_step, 2 * (N_POS_USED * j + a) + 2)
                    dve.tensor_tensor(digit[:, :, a], digit[:, :, a], spread_r, ALU.add).then_inc(spread_sum, 1)

            mlp_block(0)
            dve.wait_ge(most_int, 1)
            n = dve.value_load(most_i[0:1, 0:1])
            with dve.Fori(1, BLOCKS) as j:
                with dve.If(SLOTS * j < n):
                    mlp_block(j)
            dve.drain().then_inc(digit_ready, 1)
            dve.wait_ge(digit_ready, 1)
            dve.wait_ge(base_ready, UNITS)
            dve.tensor_tensor(onehot.rearrange("p (t a i) -> p t a i", t=TILES, a=N_POS_USED),
                              digit.unsqueeze(3).to_broadcast([P, TILES, N_POS_USED, NIB]),
                              iota_up[:].unsqueeze(1).unsqueeze(1).to_broadcast([P, TILES, N_POS_USED, NIB]),
                              ALU.is_equal).then_inc(final_step, 1)
            dve.wait_ge(final_step, 1)
            cols = x_all[:, :, OUTPUT_COL:OUTPUT_COL + OUTPUT_W]
            dve.scalar_tensor_tensor(out=cols, in0=onehot.rearrange("p (t c) -> p t c", t=TILES), scalar=2.0, in1=cols,
                                     op0=ALU.mult, op1=ALU.add).then_inc(final_ready, 1)


def lay_out_mlp(w, b):
    import numpy as np

    layers, ge, _ = w.shape
    rem, hid = ge - P, layers - 2
    chunks = P // rem
    at, width = mlp_columns(layers, ge)
    laid = np.zeros((P, width), w.dtype)
    sq = laid[:, at["sq"]].reshape(P, hid, 2 * P + rem)
    rm = laid[:, at["rm"]].reshape(P, hid, chunks, P)
    turned = w.transpose(2, 0, 1)[:, 1:1 + hid]
    sq[:, :, 0:P] = turned[0:P, :, 0:P]
    sq[:, :, 2 * P:] = turned[0:P, :, P:]
    for c in range(chunks):
        quadrant = slice(rem * c, rem * (c + 1))
        sq[quadrant, :, P + rem * c:P + rem * (c + 1)] = turned[P:, :, P:]
        rm[quadrant, :, c, :] = turned[P:, :, 0:P]
        laid[quadrant, at["out_r"].start + rem * c] = w[-1, GE_RESULT, P:]
        laid[quadrant, at["b_rem"]] = b[:, P:].T
    laid[:, at["sq"]] = sq.reshape(P, -1)
    laid[:, at["rm"]] = rm.reshape(P, -1)
    start = at["in"].start
    for a in range(N_POS_USED):
        for row, col in ((a, GE_A), (N_POS_USED + a, GE_B), (NIBBLES, GE_OP)):
            laid[row, start + a * P:start + (a + 1) * P] = w[0, 0:P, col]
            left = start + N_POS_USED * P + a * rem
            laid[row, left:left + rem] = w[0, P:, col]
    laid[:, at["out_m"].start] = w[-1, GE_RESULT, 0:P]
    laid[:, at["b_main"]] = b[:, 0:P].T
    laid[:, at["b_out"]] = b[-1, GE_RESULT]
    return laid


def kernel(x, adj, L0_gnn_weight, L0_gnn_bias, L0_ffn_weight, L1_gnn_Wq, L1_gnn_Wk, L1_gnn_Wv, L1_ffn_W, L1_ffn_b):
    import numpy as np
    import concourse.bacc as bacc
    from concourse.bass_utils import run_bass_kernel_spmd

    mlp_w, mlp_b = np.asarray(L1_ffn_W), np.asarray(L1_ffn_b)
    laid = {
        "x": np.asarray(x), "adj": np.asarray(adj), "adj_turned": np.asarray(adj).T,
        "gnn_w": np.asarray(L0_gnn_weight), "gnn_b": np.asarray(L0_gnn_bias), "ffn_w": np.asarray(L0_ffn_weight),
        "wq": np.asarray(L1_gnn_Wq), "wk": np.asarray(L1_gnn_Wk), "wv_turned": np.asarray(L1_gnn_Wv).T,
        "mlp": lay_out_mlp(mlp_w, mlp_b),
    }
    laid = {f"in_{name}": np.ascontiguousarray(a) for name, a in laid.items()}
    nc = bacc.Bacc("TRN2", target_bir_lowering=False, num_devices=1)
    args = [nc.dram_tensor(name, a.shape, mybir.dt.from_np(a.dtype), kind="ExternalInput").ap()
            for name, a in laid.items()]
    out = nc.dram_tensor("out", x.shape, F32, kind="ExternalOutput").ap()
    adj_ffn_kernel(nc, *args, mlp_w.shape[0], mlp_w.shape[1], out)
    return run_bass_kernel_spmd(nc, [laid], core_ids=[0]).results[0]["out"]
```

```python
from contextlib import ExitStack

import concourse.bass as bass
from concourse import mybir
from concourse.alu_op_type import AluOpType as ALU

ACT = mybir.ActivationFunctionType
AX = mybir.AxisListType
F32 = mybir.dt.float32
BF16 = mybir.dt.bfloat16
I32 = mybir.dt.int32
F32R = mybir.dt.float32r
PARTS = ("high", "low")
PRODUCTS = ((0, 0), (0, 1), (1, 0))

P = 128
EPS = 1e-5
FP8_MAX = 448.0
AMAX_FLOOR = 1e-12
MAGIC_SHIFT = float(1 << 20)
MIN_NORMAL = 2.0 ** -6
LEAST_MAGIC = 1.5 * MIN_NORMAL * MAGIC_SHIFT
EXPONENT_BITS = 0x7F800000
HALF_BIT = 0x00400000
INT_MAGIC = float(1 << 23)

MARK_COL, MUL_COL, OPCODE_COL = 0, 1, 29
NIBBLES_COL, NIBBLES = 64, 4
OUTPUT_COL, OUTPUT_W = 128, 32
NIB = 16
GE_A, GE_B, GE_OP, GE_RESULT = 0, 1, 30, 2
N_POS_USED = 2


def mlp_columns(layers, ge):
    rem, hid = ge - P, layers - 2
    chunks = P // rem
    widths = {"sq": hid * (2 * P + rem), "rm": hid * chunks * P, "in": N_POS_USED * (P + rem),
              "out_m": rem, "out_r": P, "b_main": layers, "b_rem": layers, "b_out": 1}
    at, start = {}, 0
    for name, width in widths.items():
        at[name] = slice(start, start + width)
        start += width
    return at, start


def adj_ffn_kernel(nc, x, adj, adj_turned, gnn_w, gnn_b, ffn_w, wq, wk, wv_turned, mlp, layers, ge, out):
    B, N, D = x.shape
    LAYERS, GE = layers, ge
    NT = N // P
    DT = D // P
    TILES = B * NT
    UB = 2
    UT = UB * NT
    UNITS = B // UB
    UW = UT * D
    BW = NT * D
    REM = GE - P
    CHUNKS = P // REM
    CW = 512
    SLOTS = CW * CHUNKS // N_POS_USED // P
    HALF = SLOTS // 2
    BLOCKS = TILES // SLOTS
    HID = LAYERS - 2
    RELUS = LAYERS - 1
    NF = NIBBLES + 1

    x_rows = x.rearrange("b (h p) d -> p (b h) d", p=P)
    out_rows = out.rearrange("b (h p) d -> p (b h) d", p=P)

    with ExitStack() as ctx:
        def sb(name, shape, dt=F32):
            return ctx.enter_context(nc.sbuf_tensor(name, shape, dt))

        def sem(name):
            return ctx.enter_context(nc.semaphore(name))

        AHEAD = 3

        x_all = sb("x_all", [P, TILES, D])
        xn_all = sb("xn_all", [P, TILES, D])
        ident = sb("ident", [P, P])
        ident_bf = sb("ident_bf", [P, P], BF16)
        eps = sb("eps", [P, 1])
        ones = sb("ones", [P, TILES])
        adj_nat = sb("adj_nat", [P, NT, N])
        adj_t = sb("adj_t", [P, NT, N])
        gnn_w_sb = sb("gnn_w_sb", [P, DT, D])
        ffn_w_sb = sb("ffn_w_sb", [P, DT, D])
        ffn_wq = sb("ffn_wq", [P, DT, D], BF16)
        qk_w = [sb(f"qk_w_{part}", [P, DT, D], F32R) for part in PARTS]
        wv_t = [sb(f"wv_t_{part}", [P, DT, D], F32R) for part in PARTS]
        at, mlp_width = mlp_columns(LAYERS, GE)
        mlp_sb = sb("mlp_sb", [P, mlp_width])
        w_sq = mlp_sb[:, at["sq"]].rearrange("p (l e) -> p l e", l=HID)
        w_mm, w_rr, w_mr = w_sq[:, :, 0:P], w_sq[:, :, P:2 * P], w_sq[:, :, 2 * P:2 * P + REM]
        w_rm = mlp_sb[:, at["rm"]].rearrange("p (l c e) -> p l c e", l=HID, c=CHUNKS)
        w_in = mlp_sb[:, at["in"]]
        w_in_m = w_in[:, 0:N_POS_USED * P].rearrange("p (a e) -> p a e", a=N_POS_USED)
        w_in_r = w_in[:, N_POS_USED * P:].rearrange("p (a e) -> p a e", a=N_POS_USED)
        w6_m, w6_r = mlp_sb[:, at["out_m"]], mlp_sb[:, at["out_r"]]
        b_main, b_rem, b_out = mlp_sb[:, at["b_main"]], mlp_sb[:, at["b_rem"]], mlp_sb[:, at["b_out"]]
        iota_slot = sb("iota_slot", [P, TILES])
        iota_down = sb("iota_down", [P, NIBBLES * NIB])
        iota_up = sb("iota_up", [P, NIB])

        buf_w = sb("buf_w", [P, UW])
        buf_m = sb("buf_m", [P, UW])
        buf_t = sb("buf_t", [P, UW])
        buf_n = sb("buf_n", [P, UW])
        buf_r = sb("buf_r", [P, UW])
        xn_t = [sb(f"xn_t_{part}", [P, DT, UB, N], F32R) for part in PARTS]
        qk_t = [sb(f"qk_t_{part}", [P, DT, UB, N], F32R) for part in PARTS]
        v_sb = [sb(f"v_{part}", [P, UB, NT, D], F32R) for part in PARTS]
        rel_t = [sb(f"rel_{part}", [P, UB, NT, N], F32R) for part in PARTS]
        q_rows = sb("q_rows", [P, UT, D], BF16)
        q_t = sb("q_t", [P, UB, DT, N], BF16)

        stats = sb("stats", [P, UT, 6])
        mv = sb("mv", [P, UT, 2])
        sums = sb("sums", [P, UT])
        squares = sb("squares", [P, UT])
        nmean = sb("nmean", [P, UT])
        shift = sb("shift", [P, 4, UT])
        std = sb("std", [P, 4, UT])
        rstd = sb("rstd", [P, 4, UT])
        amax_u = sb("amax_u", [P, UNITS])
        amax_p = sb("amax_p", [P, 2])
        amax = sb("amax", [P, 2])
        fscale = sb("fscale", [P, 2])
        fscale_up = sb("fscale_up", [P, 1])
        finv = sb("finv", [P, 2])
        fout = sb("fout", [P, 1])
        most = sb("most", [P, 1])
        most_i = sb("most_i", [P, 1], I32)
        found = sb("found", [P, N_POS_USED, SLOTS])

        psum = ctx.enter_context(nc.psum_tensor("psum", [P, 8, 512], F32))

        bias_bc = q_rows[:, 0:2, :].rearrange("p t d -> p (t d)").bitcast(F32)

        def tiles(buf):
            return buf[:].rearrange("p (t d) -> p t d", d=D)

        xn_a = [tiles(buf_n), tiles(buf_w)]
        y_t = [b[:].rearrange("p (b e n) -> p b e n", b=UB, e=DT) for b in (buf_m, buf_t)]
        wq_sb, wk_sb = (buf_r[:, i * DT * D:(i + 1) * DT * D].rearrange("p (e d) -> p e d", e=DT) for i in (0, 1))
        wv_raw = q_t[:].rearrange("p b e n -> p (b e n)").bitcast(F32)
        xn_b = tiles(buf_n)
        rel_32 = buf_r[:].rearrange("p (b m n) -> p b m n", b=UB, m=NT)
        rel_sq = buf_w[:].rearrange("p (b m n) -> p b m n", b=UB, m=NT)
        hit = adj_t[:, 0, :].rearrange("p (t i) -> p t i", t=UT)
        code = adj_t[:, 1, :].rearrange("p (t g) -> p t g", g=NIBBLES)
        feats = gnn_w_sb[:].rearrange("p e d -> p (e d)")[:, 0:NF * TILES].rearrange("p (f t) -> p f t", f=NF)
        free = ffn_w_sb[:].rearrange("p e d -> p (e d)")
        mask = free[:, 0:2 * TILES].rearrange("p (a t) -> p a t", a=2)
        pos, slot_of, spread_r = (free[:, i * TILES:(i + 1) * TILES] for i in (2, 3, 4))
        digit = free[:, 5 * TILES:(5 + N_POS_USED) * TILES].rearrange("p (t a) -> p t a", a=N_POS_USED)
        room = xn_all[:].rearrange("p t d -> p (t d)")
        taken = [0]

        def take(n):
            taken[0] += n
            return room[:, taken[0] - n:taken[0]]

        f_rows = take(SLOTS * P).rearrange("p (s f) -> p s f", f=P)
        f_t = take(2 * CW).rearrange("p (h c) -> p h c", h=2)
        hid = [take(CW) for _ in range(CHUNKS)]
        hid_r = [take(CW) for _ in range(2)]
        last_sb = take(CW)
        sel = take(SLOTS * TILES).rearrange("p (s t) -> p s t", s=SLOTS)
        prod = take(SLOTS * TILES)
        onehot = take(TILES * OUTPUT_W)

        def unit(buf, k):
            return buf[:, bass.ds(UT * k, UT), :] if not isinstance(k, int) else buf[:, UT * k:UT * (k + 1), :]

        def half(buf, k, b):
            t = UT * k + NT * b
            return buf[:, bass.ds(t, NT), :] if not isinstance(k, int) else buf[:, t:t + NT, :]

        def column(buf, k):
            return buf[:, bass.ds(k, 1)] if not isinstance(k, int) else buf[:, k:k + 1]

        def after(k, first=0):
            return k >= first if isinstance(k, int) else True

        x_loaded = [sem("x_loaded_even"), sem("x_loaded_odd")]
        adj_loaded, gnn_loaded, ffn_loaded = sem("adj_loaded"), sem("gnn_loaded"), sem("ffn_loaded")
        att_loaded, mlp_loaded = sem("att_loaded"), sem("mlp_loaded")
        consts_ready, zeros_ready = sem("consts_ready"), sem("zeros_ready")
        ident_ready = sem("ident_ready")
        ln_squares = [sem(f"ln{i}_squares") for i in range(4)]
        ln_shift = [sem(f"ln{i}_shift") for i in range(4)]
        ln_stats = [sem(f"ln{i}_stats") for i in range(4)]
        ln_moments = [sem(f"ln{i}_moments") for i in range(4)]
        ln_std = [sem(f"ln{i}_std") for i in range(4)]
        ln_rstd = [sem(f"ln{i}_rstd") for i in range(4)]
        ln_rows = [sem(f"ln{i}_rows") for i in range(4)]
        y_done, y_moved, gnn_done, bias_added = sem("y_done"), sem("y_moved"), sem("gnn_done"), sem("bias_added")
        x1_added, amax_seen = sem("x1_added"), sem("amax_seen")
        prep_done, prep_moved = sem("prep_done"), sem("prep_moved")
        amax_parts, amax_ready, scale_step, scales_ready = (
            sem("amax_parts"), sem("amax_ready"), sem("scale_step"), sem("scales_ready"))
        wq_step, ffn_wq_ready = sem("wq_step"), sem("ffn_wq_ready")
        scaled_ready, exponent_ready, magic_ready = sem("scaled_ready"), sem("exponent_ready"), sem("magic_ready")
        summed_ready, q_ready = sem("summed_ready"), sem("q_ready")
        q_turned, q_t_ready, ffn_done, x2_added = sem("q_turned"), sem("q_t_ready"), sem("ffn_done"), sem("x2_added")
        xt_turned, xt_moved, qk_done, qk_moved = sem("xt_turned"), sem("xt_moved"), sem("qk_done"), sem("qk_moved")
        v_done, v_moved, rel_done, rel_masked = sem("v_done"), sem("v_moved"), sem("rel_done"), sem("rel_masked")
        xt_low, qk_low, v_low = sem("xt_low"), sem("qk_low"), sem("v_low")
        rel_high, rel_low, weights_high, weights_low = (
            sem("rel_high"), sem("rel_low"), sem("weights_high"), sem("weights_low"))
        sq_ready, ss_done, norm_ready, inv_ready = sem("sq_ready"), sem("ss_done"), sem("norm_ready"), sem("inv_ready")
        att_done, x3_added = sem("att_done"), sem("x3_added")
        hits_ready, codes_ready, base_ready = sem("hits_ready"), sem("codes_ready"), sem("base_ready")
        base_left, base_right, output_stored = sem("base_left"), sem("base_right"), sem("output_stored")
        f_zeroed, mask_step, feats_step, slots_step = sem("f_zeroed"), sem("mask_step"), sem("feats_step"), sem("slots_step")
        counted, most_ready, most_int = sem("counted"), sem("most_ready"), sem("most_int")
        selected, product, f_ready = sem("selected"), sem("product"), sem("f_ready")
        f_turned, f_t_ready = sem("f_turned"), sem("f_t_ready")
        main_done = [sem(f"main{c}_done") for c in range(CHUNKS)]
        hid_ready = [sem(f"hid{c}_ready") for c in range(CHUNKS)]
        rem_done, hid_r_ready = sem("rem_done"), sem("hid_r_ready")
        last_done, last_ready, last_turned = sem("last_done"), sem("last_ready"), sem("last_turned")
        clip_step, spread_step, spread_sum = sem("clip_step"), sem("spread_step"), sem("spread_sum")
        digit_zeroed, digit_ready, final_step, final_ready = (
            sem("digit_zeroed"), sem("digit_ready"), sem("final_step"), sem("final_ready"))

        waited = {}

        def stand_alone(engine, name):
            if name not in waited:
                waited[name] = sem(f"waited_{name}")
            engine.sem_inc(waited[name], 1)

        Y, G = (1, 2), (3, 4)
        QT, QK, FFN, VB, REL, XT, ATT, SS = 0, (1, 2), (3, 4), (5, 6), (1, 2), (3, 4), (5, 6), 7
        PREP = 7
        MAIN, RB, LAST, FT = (1, 2, 3, 4), 5, 0, (6, 7)

        block = ctx.enter_context(nc.Block())

        @block.sync
        def _(sp):
            for par in range(2):
                sp.dma_start(unit(x_all, par), unit(x_rows, par)).then_inc(x_loaded[par], 16)
            with sp.Fori(1, UNITS // 2) as j:
                for par in range(2):
                    sp.wait_ge(x_loaded[par], 16 * j)
                    stand_alone(sp, "sp")
                    sp.dma_start(unit(x_all, 2 * j + par), unit(x_rows, 2 * j + par)).then_inc(x_loaded[par], 16)

            def store(k):
                sp.wait_ge(base_ready, k + 1)
                stand_alone(sp, "sp")
                if after(k, 1):
                    sp.wait_ge(base_left, 16 * k)
                    sp.wait_ge(base_right, 16 * k)
                stand_alone(sp, "sp")
                sp.dma_start(unit(out_rows, k)[:, :, 0:OUTPUT_COL],
                             unit(x_all, k)[:, :, 0:OUTPUT_COL]).then_inc(base_left, 16)
                sp.dma_start(unit(out_rows, k)[:, :, OUTPUT_COL + OUTPUT_W:D],
                             unit(x_all, k)[:, :, OUTPUT_COL + OUTPUT_W:D]).then_inc(base_right, 16)

            store(0)
            with sp.Fori(1, UNITS) as k:
                store(k)
            sp.wait_ge(final_ready, 1)
            sp.dma_start(out_rows[:, :, OUTPUT_COL:OUTPUT_COL + OUTPUT_W],
                         x_all[:, :, OUTPUT_COL:OUTPUT_COL + OUTPUT_W]).then_inc(output_stored, 16)
            sp.wait_ge(base_left, 16 * UNITS)
            sp.wait_ge(base_right, 16 * UNITS)
            sp.wait_ge(output_stored, 16)

        @block.gpsimd
        def _(pool):
            pool.memset(ident[:], 0.0).then_inc(zeros_ready, 1)
            pool.wait_ge(zeros_ready, 1)
            pool.affine_select(out=ident[:], in_=ident[:], compare_op=ALU.not_equal, fill=1.0, base=0,
                               pattern=[[-1, P]], channel_multiplier=1).then_inc(ident_ready, 1)
            pool.memset(eps[:], EPS)
            pool.memset(ones[:], 1.0).then_inc(consts_ready, 1)
            pool.wait_ge(ident_ready, 1)
            pool.tensor_copy(ident_bf[:], ident[:]).then_inc(consts_ready, 1)
            pool.iota(iota_slot[:], [[1, TILES]], base=1, channel_multiplier=0, allow_small_or_imprecise_dtypes=True)
            pool.iota(iota_down[:], [[0, NIBBLES], [-1, NIB]], base=NIB, channel_multiplier=0,
                      allow_small_or_imprecise_dtypes=True)
            pool.iota(iota_up[:], [[1, NIB]], base=1, channel_multiplier=0,
                      allow_small_or_imprecise_dtypes=True).then_inc(consts_ready, 1)
            pool.wait_ge(amax_parts, 1)
            pool.partition_all_reduce(amax[:, 1:2], amax_p[:, 1:2], P, bass.bass_isa.ReduceOp.max).then_inc(amax_ready, 1)
            pool.wait_ge(gnn_loaded, 32)

            def add_bias(k):
                pool.wait_ge(ln_rows[0], k + 1)
                pool.tensor_tensor(unit(x_all, k), unit(x_all, k),
                                   bias_bc.unsqueeze(1).to_broadcast([P, UT, D]), ALU.add).then_inc(bias_added, 1)

            with pool.Fori(0, UNITS) as k:
                add_bias(k)

            pool.wait_ge(amax_parts, 2)
            pool.partition_all_reduce(amax[:, 0:1], amax_p[:, 0:1], P, bass.bass_isa.ReduceOp.max).then_inc(amax_ready, 1)

            def scale_up(k):
                if after(k, 4):
                    pool.wait_ge(ss_done, k - 3)
                else:
                    pool.wait_ge(exponent_ready, k)
                pool.tensor_tensor(tiles(buf_w), unit(xn_all, k),
                                   fscale_up[:].unsqueeze(1).to_broadcast([P, UT, D]), ALU.mult).then_inc(scaled_ready, 1)

            def at_least_normal(k):
                pool.wait_ge(exponent_ready, k + 1)
                stand_alone(pool, "pool")
                pool.tensor_scalar(buf_m[:], buf_m[:], LEAST_MAGIC, None, ALU.max).then_inc(magic_ready, 1)

            def rounded(k):
                pool.wait_ge(summed_ready, k + 1)
                if after(k, 1):
                    pool.wait_ge(q_turned, k)
                pool.tensor_tensor(q_rows[:].rearrange("p t d -> p (t d)"), buf_t[:], buf_m[:],
                                   ALU.subtract).then_inc(q_ready, 1)

            def add_rows(k):
                pool.wait_ge(ln_rows[3], k + 1)
                pool.tensor_tensor(unit(x_all, k), unit(x_all, k), unit(xn_all, k), ALU.add).then_inc(base_ready, 1)

            def low_relations(k):
                for b in range(UB):
                    pool.wait_ge(rel_high, UB * k + b + 1)
                    if after(k, 1):
                        pool.wait_ge(att_done, UB * k)
                    pool.tensor_tensor(rel_t[1][:, b], rel_32[:, b], rel_t[0][:, b].bitcast(F32),
                                       ALU.subtract).then_inc(rel_low, 1)

            for k in range(1, AHEAD):
                at_least_normal(k)
                rounded(k)

            def phase_b(k, final=None):
                more = final is None or final + AHEAD < UNITS
                if more:
                    scale_up(k + AHEAD)
                    at_least_normal(k + AHEAD)
                if after(k, 2):
                    add_rows(k - 2)
                low_relations(k)
                if more:
                    rounded(k + AHEAD)

            phase_b(0)
            phase_b(1)
            with pool.Fori(2, UNITS - AHEAD) as k:
                phase_b(k)
            for k in range(UNITS - AHEAD, UNITS):
                phase_b(k, final=k)
            add_rows(UNITS - 2)
            add_rows(UNITS - 1)

            pool.wait_ge(counted, 1)
            pool.partition_all_reduce(most[:], pos[:, TILES - 1:TILES], P, bass.bass_isa.ReduceOp.max).then_inc(most_ready, 1)

        @block.scalar
        def _(act):
            def load(dst, src, s):
                act.dma_start(dst, src).then_inc(s, 16)

            def rows(w):
                return w.rearrange("(t p) d -> p t d", p=P)

            load(adj_t[:], rows(adj_turned), adj_loaded)
            load(gnn_w_sb[:], rows(gnn_w), gnn_loaded)
            load(bias_bc, gnn_b.partition_broadcast(P), gnn_loaded)
            load(ffn_w_sb[:], rows(ffn_w), ffn_loaded)
            load(adj_nat[:], rows(adj), att_loaded)
            for dst, src in ((wq_sb, wq), (wk_sb, wk), (wv_raw.rearrange("p (e d) -> p e d", e=DT), wv_turned)):
                load(dst, rows(src), att_loaded)
            load(mlp_sb[:], mlp, mlp_loaded)

            def root(n, k, src=None):
                act.wait_ge(ln_moments[n], k + 1)
                act.activation(std[:, n], mv[:, :, 1], ACT.Sqrt, bias=eps[:, 0:1]).then_inc(ln_std[n], 1)

            def spread(n, k):
                act.wait_ge(ln_moments[n], k + 1)
                stand_alone(act, "act")
                for i in range(UT):
                    ins = act.activation(xn_all[:, UT * k + i, :], x_all[:, UT * k + i, :], ACT.Square,
                                         bias=nmean[:, i:i + 1], accum_out=squares[:, i:i + 1])
                ins.then_inc(ln_squares[n], 1)
                act.wait_ge(ln_squares[n], k + 1)
                act.activation(std[:, n], squares[:], ACT.Sqrt, scale=1.0 / D, bias=eps[:, 0:1]).then_inc(ln_std[n], 1)

            def scale_rows(n, k):
                act.wait_ge(ln_shift[n], k + 1)
                stand_alone(act, "act")
                for i in range(UT):
                    ins = act.activation(xn_all[:, UT * k + i, :], x_all[:, UT * k + i, :], ACT.Identity,
                                         scale=rstd[:, n, i:i + 1], bias=shift[:, n, i:i + 1])
                ins.then_inc(ln_rows[n], 1)

            act.wait_ge(consts_ready, 1)
            root(0, 0)

            def move_y(k, par, b):
                act.wait_ge(y_done, UB * k + b + 1)
                act.copy(y_t[par][:, b].rearrange("p e n -> p (e n)"), psum[:, Y[b], :]).then_inc(y_moved, 1)

            def phase_a(k, par, final=None):
                nxt2 = final is None or final + 2 < UNITS
                nxt3 = final is None or final + 3 < UNITS
                if nxt2:
                    move_y(k + 2, par, 0)
                spread(1, k)
                if nxt2:
                    move_y(k + 2, par, 1)
                if nxt3:
                    root(0, k + 3)
                scale_rows(1, k)

            root(0, 1)
            for b in range(UB):
                move_y(0, 0, b)
            root(0, 2)
            for b in range(UB):
                move_y(1, 1, b)
            phase_a(0, 0)
            with act.Fori(0, UNITS // 2 - 2) as j:
                phase_a(2 * j + 1, 1)
                phase_a(2 * j + 2, 0)
            for k in range(UNITS - 3, UNITS):
                phase_a(k, k % 2, final=k)

            act.wait_ge(prep_done, 1)
            act.copy(qk_w[0][:].rearrange("p e d -> p (e d)"), psum[:, PREP, :]).then_inc(weights_high, 1)
            act.copy(wv_t[0][:].rearrange("p e d -> p (e d)"), wv_raw).then_inc(weights_high, 1)

            def scale_up(k):
                if k:
                    act.wait_ge(exponent_ready, k)
                act.activation(buf_w[:], unit(xn_all, k).rearrange("p t d -> p (t d)"), ACT.Copy,
                               scale=fscale_up[:, 0:1]).then_inc(scaled_ready, 1)

            def rows_b(k):
                act.wait_ge(ln_shift[2], k + 1)
                if after(k, 1):
                    act.wait_ge(xt_turned, UB * k)
                stand_alone(act, "act")
                for i in range(UT):
                    ins = act.activation(xn_b[:, i, :], x_all[:, UT * k + i, :], ACT.Identity,
                                         scale=rstd[:, 2, i:i + 1], bias=shift[:, 2, i:i + 1])
                ins.then_inc(ln_rows[2], 1)

            def move_q(k):
                act.wait_ge(q_turned, k + 1)
                act.copy(q_t[:].rearrange("p b e n -> p (b e n)"), psum[:, QT, :].bitcast(BF16)).then_inc(q_t_ready, 1)

            def move_xt(k):
                for b in range(UB):
                    act.wait_ge(xt_turned, UB * k + b + 1)
                    act.copy(xn_t[0][:, :, b, :], psum[:, XT[b], :].rearrange("p (e n) -> p e n", e=DT)).then_inc(xt_moved, 1)

            def move_qk(k, e):
                act.wait_ge(qk_done, DT * k + e + 1)
                act.copy(qk_t[0][:, e].rearrange("p b n -> p (b n)"), psum[:, QK[e], :]).then_inc(qk_moved, 1)

            def move_v(k, b):
                act.wait_ge(v_done, UB * k + b + 1)
                act.copy(v_sb[0][:, b].rearrange("p m d -> p (m d)"), psum[:, VB[b], :]).then_inc(v_moved, 1)

            def high_relations(k):
                for b in range(UB):
                    act.wait_ge(rel_masked, UB * k + b + 1)
                    act.copy(rel_t[0][:, b], rel_32[:, b]).then_inc(rel_high, 1)

            def square_relations(k, scaled_later):
                if scaled_later:
                    act.wait_ge(exponent_ready, k + AHEAD + 1)
                for b in range(UB):
                    act.activation(rel_sq[:, b], rel_32[:, b], ACT.Square).then_inc(sq_ready, 1)

            def root_norm(k):
                act.wait_ge(ss_done, k + 1)
                act.activation(std[:, 0], psum[:, SS, 0:UT], ACT.Sqrt).then_inc(norm_ready, 1)

            act.wait_ge(scales_ready, 1)
            scale_up(0)
            scale_up(1)
            move_q(0)
            root(2, 0)
            scale_up(2)
            rows_b(0)
            move_xt(0)
            move_q(1)
            root(2, 1)

            def phase_b(k, final=None):
                nxt = final is None or final + 1 < UNITS
                nxt2 = final is None or final + 2 < UNITS
                if nxt:
                    rows_b(k + 1)
                move_qk(k, 0)
                move_qk(k, 1)
                if nxt2:
                    move_q(k + 2)
                if after(k, 1):
                    spread(3, k - 1)
                move_v(k, 0)
                move_v(k, 1)
                high_relations(k)
                if nxt:
                    move_xt(k + 1)
                square_relations(k, final is None or final + AHEAD < UNITS)
                if after(k, 1):
                    scale_rows(3, k - 1)
                if nxt2:
                    root(2, k + 2)
                root_norm(k)

            phase_b(0)
            with act.Fori(1, UNITS - AHEAD) as k:
                phase_b(k)
            for k in range(UNITS - AHEAD, UNITS):
                phase_b(k, final=k)
            spread(3, UNITS - 1)
            scale_rows(3, UNITS - 1)

            act.wait_ge(mlp_loaded, 16)

            def relu(dst, src, bias, s):
                act.activation(dst, src, ACT.Relu, bias=bias).then_inc(s, 1)

            def mlp_block(j):
                for h in range(2):
                    act.wait_ge(f_turned, 2 * j + h + 1)
                    act.copy(f_t[:, h, :], psum[:, FT[h], :]).then_inc(f_t_ready, 1)
                for l in range(RELUS):
                    act.wait_ge(rem_done, RELUS * j + l + 1)
                    relu(hid_r[l % 2], psum[:, RB, :], b_rem[:, l:l + 1], hid_r_ready)
                    for c in range(0, CHUNKS, 2):
                        act.wait_ge(main_done[c], RELUS * j + l + 1)
                        relu(hid[c], psum[:, MAIN[c], :], b_main[:, l:l + 1], hid_ready[c])
                act.wait_ge(last_done, j + 1)
                act.activation(last_sb, psum[:, LAST, :], ACT.Identity, bias=b_out[:, 0:1]).then_inc(last_ready, 1)

            mlp_block(0)
            act.wait_ge(most_int, 1)
            n = act.value_load(most_i[0:1, 0:1])
            with act.Fori(1, BLOCKS) as j:
                with act.If(SLOTS * j < n):
                    mlp_block(j)

        @block.tensor
        def _(pe):
            pe.wait_ge(adj_loaded, 16)
            pe.wait_ge(gnn_loaded, 32)

            def y_part(k, par):
                pe.wait_ge(ln_rows[0], k + 1)
                for b in range(UB):
                    if after(k, 1):
                        pe.wait_ge(y_moved, UB * (k - 1) + b + 1)
                    for e in range(DT):
                        for m in range(NT):
                            mm = pe.matmul(psum[:, Y[b], e * N:(e + 1) * N],
                                           xn_a[par][:, b * NT + m, e * P:(e + 1) * P], adj_t[:, m, :],
                                           start=m == 0, stop=m == NT - 1)
                    mm.then_inc(y_done, 1)

            def gnn_part(k, par):
                for b in range(UB):
                    pe.wait_ge(y_moved, UB * k + b + 1)
                    if after(k, 1):
                        pe.wait_ge(x1_added, UB * (k - 1) + b + 1)
                    for h in range(NT):
                        for e in range(DT):
                            mm = pe.matmul(psum[:, G[b], h * D:(h + 1) * D],
                                           y_t[par][:, b, e, h * P:(h + 1) * P], gnn_w_sb[:, e, :],
                                           start=e == 0, stop=e == DT - 1)
                    mm.then_inc(gnn_done, 1)

            y_part(0, 0)
            y_part(1, 1)
            gnn_part(0, 0)
            with pe.Fori(1, UNITS // 2) as j:
                for par in range(2):
                    y_part(2 * j + par, par)
                    gnn_part(2 * j + par - 1, 1 - par)
            gnn_part(UNITS - 1, 1)

            pe.wait_ge(att_loaded, 64)
            for i in range(DT):
                for e in range(DT):
                    mm = pe.matmul(psum[:, PREP, i * D:(i + 1) * D], wq_sb[:, e, i * P:(i + 1) * P], wk_sb[:, e, :],
                                   start=e == 0, stop=e == DT - 1)
            mm.then_inc(prep_done, 1)

            def turn_q(k):
                pe.wait_ge(q_ready, k + 1)
                if after(k, 1):
                    pe.wait_ge(q_t_ready, k)
                bank = psum[:, QT, :].bitcast(BF16)
                for b in range(UB):
                    for e in range(DT):
                        for m in range(NT):
                            at = ((b * DT + e) * NT + m) * P
                            mm = pe.transpose(bank[:, at:at + P], q_rows[:, b * NT + m, e * P:(e + 1) * P], ident_bf[:])
                mm.then_inc(q_turned, 1)

            def ffn(k):
                pe.wait_ge(q_t_ready, k + 1)
                for b in range(UB):
                    if after(k, 2):
                        pe.wait_ge(xt_low, UB * (k - 2) + b + 1)
                    elif k == 1:
                        pe.wait_ge(xt_low, b + 1)
                    for h in range(NT):
                        for e in range(DT):
                            mm = pe.matmul(psum[:, FFN[b], h * D:(h + 1) * D], q_t[:, b, e, h * P:(h + 1) * P],
                                           ffn_wq[:, e, :], start=e == 0, stop=e == DT - 1)
                    mm.then_inc(ffn_done, 1)

            def turn_x(k, ffn_ahead=1):
                pe.wait_ge(ln_rows[2], k + 1)
                pe.wait_ge(x2_added, UB * (k + ffn_ahead + 1))
                for b in range(UB):
                    for e in range(DT):
                        for m in range(NT):
                            at = (e * NT + m) * P
                            mm = pe.transpose(psum[:, XT[b], at:at + P], xn_b[:, b * NT + m, e * P:(e + 1) * P], ident[:])
                    mm.then_inc(xt_turned, 1)

            def qk(k):
                pe.wait_ge(xt_low, UB * (k + 1))
                for o in range(DT):
                    if after(k, 1):
                        pe.wait_ge(rel_masked, UB * (k - 1) + o + 1)
                    steps = [(e, w, x) for w, x in PRODUCTS for e in range(DT)]
                    for i, (e, w, x) in enumerate(steps):
                        mm = pe.matmul(psum[:, QK[o], :], qk_w[w][:, e, o * P:(o + 1) * P],
                                       xn_t[x][:, e].rearrange("p b n -> p (b n)"), start=i == 0, stop=i == len(steps) - 1)
                    mm.then_inc(qk_done, 1)

            def values(k, b):
                if after(k, 1):
                    pe.wait_ge(x3_added, UB * (k - 1) + b + 1)
                for m in range(NT):
                    steps = [(e, x, w) for x, w in PRODUCTS for e in range(DT)]
                    for i, (e, x, w) in enumerate(steps):
                        mm = pe.matmul(psum[:, VB[b], m * D:(m + 1) * D], xn_t[x][:, e, b, m * P:(m + 1) * P],
                                       wv_t[w][:, e, :], start=i == 0, stop=i == len(steps) - 1)
                mm.then_inc(v_done, 1)

            def relations(k):
                pe.wait_ge(qk_moved, DT * (k + 1))
                pe.wait_ge(qk_low, DT * (k + 1))
                for b in range(UB):
                    for m in range(NT):
                        steps = [(e, x, q) for x, q in PRODUCTS for e in range(DT)]
                        for i, (e, x, q) in enumerate(steps):
                            mm = pe.matmul(psum[:, REL[b], m * N:(m + 1) * N], xn_t[x][:, e, b, m * P:(m + 1) * P],
                                           qk_t[q][:, e, b, :], start=i == 0, stop=i == len(steps) - 1)
                    mm.then_inc(rel_done, 1)

            def attend(k):
                for b in range(UB):
                    pe.wait_ge(rel_high, UB * k + b + 1)
                    pe.wait_ge(v_low, UB * k + b + 1)
                    for h in range(NT):
                        steps = [(m, r, v) for r, v in PRODUCTS for m in range(NT)]
                        for i, (m, r, v) in enumerate(steps):
                            if h == 0 and r == 1 and m == 0:
                                pe.wait_ge(rel_low, UB * k + b + 1)
                            mm = pe.matmul(psum[:, ATT[b], h * D:(h + 1) * D], rel_t[r][:, b, m, h * P:(h + 1) * P],
                                           v_sb[v][:, b, m, :], start=i == 0, stop=i == len(steps) - 1)
                    mm.then_inc(att_done, 1)

            def sum_squares(k):
                pe.wait_ge(sq_ready, UB * (k + 1))
                if after(k, 1):
                    pe.wait_ge(norm_ready, k)
                for b in range(UB):
                    for h in range(NT):
                        for m in range(NT):
                            mm = pe.matmul(psum[:, SS, b * NT + h:b * NT + h + 1], rel_sq[:, b, m, h * P:(h + 1) * P],
                                           ones[:, 0:1], start=m == 0, stop=m == NT - 1)
                mm.then_inc(ss_done, 1)

            pe.wait_ge(weights_low, 2)
            pe.wait_ge(ident_ready, 1)
            pe.wait_ge(consts_ready, 2)
            pe.wait_ge(x1_added, UB * UNITS)
            pe.wait_ge(ffn_wq_ready, 1)
            turn_q(0)
            ffn(0)
            turn_x(0, ffn_ahead=0)
            turn_q(1)
            ffn(1)

            def phase_b(k, final=None):
                nxt = final is None or final + 1 < UNITS
                nxt2 = final is None or final + 2 < UNITS
                qk(k)
                if nxt2:
                    turn_q(k + 2)
                values(k, 0)
                if nxt2:
                    ffn(k + 2)
                values(k, 1)
                relations(k)
                if nxt:
                    turn_x(k + 1, ffn_ahead=1 if nxt2 else 0)
                attend(k)
                sum_squares(k)

            phase_b(0)
            with pe.Fori(1, UNITS - 2) as k:
                phase_b(k)
            for k in (UNITS - 2, UNITS - 1):
                phase_b(k, final=k)

            pe.wait_ge(mlp_loaded, 16)

            def mlp_block(j):
                pe.wait_ge(f_ready, j + 1)
                for h in range(2):
                    for s in range(HALF):
                        mm = pe.transpose(psum[:, FT[h], s * P:(s + 1) * P], f_rows[:, h * HALF + s, :], ident[:])
                    mm.then_inc(f_turned, 1)
                for c in range(CHUNKS):
                    if c % 2 == 0:
                        pe.wait_ge(f_t_ready, 2 * j + c // 2 + 1)
                    pe.matmul(psum[:, MAIN[c], :], w_in_m[:, c % 2, :], f_t[:, c // 2, :],
                              start=True, stop=True).then_inc(main_done[c], 1)
                for c in range(CHUNKS):
                    mm = pe.matmul(psum[REM * c:REM * (c + 1), RB, :], w_in_r[:, c % 2, :], f_t[:, c // 2, :],
                                   start=True, stop=True)
                mm.then_inc(rem_done, 1)
                for l in range(1, HID + 1):
                    done = RELUS * j + l

                    def from_main(c):
                        pe.wait_ge(hid_ready[c], done)
                        pe.matmul(psum[:, MAIN[c], :], w_mm[:, l - 1, :], hid[c], start=True, stop=False)

                    for c in range(CHUNKS - 1):
                        from_main(c)
                    pe.wait_ge(hid_r_ready, done)
                    pe.wait_ge(hid_ready[CHUNKS - 1], done)
                    for c in range(CHUNKS):
                        pe.matmul(psum[REM * c:REM * (c + 1), RB, :], w_mr[:, l - 1, :], hid[c],
                                  start=True, stop=False, skip_group_check=True)
                    pe.matmul(psum[:, RB, :], w_rr[:, l - 1, :], hid_r[(l - 1) % 2], start=False, stop=True,
                              skip_group_check=True).then_inc(rem_done, 1)
                    from_main(CHUNKS - 1)
                    for c in range(CHUNKS):
                        pe.matmul(psum[:, MAIN[c], :], w_rm[:, l - 1, c, :], hid_r[(l - 1) % 2],
                                  start=False, stop=True).then_inc(main_done[c], 1)
                for c in range(CHUNKS):
                    pe.wait_ge(hid_ready[c], RELUS * (j + 1))
                    pe.matmul(psum[REM * c:REM * (c + 1), LAST, :], w6_m[:], hid[c],
                              start=True, stop=False, skip_group_check=True)
                pe.wait_ge(hid_r_ready, RELUS * (j + 1))
                pe.matmul(psum[:, LAST, :], w6_r[:], hid_r[HID % 2], start=False, stop=True,
                          skip_group_check=True).then_inc(last_done, 1)
                pe.wait_ge(last_ready, j + 1)
                for s in range(HALF):
                    mm = pe.transpose(psum[:, FT[0], s * P:(s + 1) * P], last_sb[:, s * P:(s + 1) * P], ident[:])
                mm.then_inc(last_turned, 1)

            mlp_block(0)
            pe.wait_ge(most_int, 1)
            n = pe.value_load(most_i[0:1, 0:1])
            with pe.Fori(1, BLOCKS) as j:
                with pe.If(SLOTS * j < n):
                    mlp_block(j)

        @block.vector
        def _(dve):
            def moments(n, k):
                stand_alone(dve, "dve")
                for i in range(UT):
                    ins = dve.bn_stats(stats[:, i], tile_of(x_all, k, i))
                ins.then_inc(ln_stats[n], 1)
                dve.wait_ge(ln_stats[n], k + 1)
                stand_alone(dve, "dve")
                for i in range(UT):
                    ins = dve.bn_aggr(mv[:, i], stats[:, i])
                ins.then_inc(ln_moments[n], 1)

            def tile_of(buf, k, i):
                return buf[:, UT * k + i, :]

            def normalise(n, k, dst):
                dve.wait_ge(ln_std[n], k + 1)
                dve.reciprocal(rstd[:, n], std[:, n]).then_inc(ln_rstd[n], 1)
                dve.wait_ge(ln_rstd[n], k + 1)
                for i in range(UT):
                    ins = dve.tensor_scalar(dst(i), tile_of(x_all, k, i), mv[:, i, 0:1], rstd[:, n, i:i + 1],
                                            ALU.subtract, ALU.mult)
                ins.then_inc(ln_rows[n], 1)

            def mean(n, k):
                dve.tensor_scalar(nmean[:], sums[:], -1.0 / D, None, ALU.mult).then_inc(ln_moments[n], 1)

            def scale_and_shift(n, k):
                dve.wait_ge(ln_std[n], k + 1)
                if after(k, 1):
                    dve.wait_ge(ln_rows[n], k)
                dve.reciprocal(rstd[:, n], std[:, n]).then_inc(ln_rstd[n], 1)
                dve.wait_ge(ln_rstd[n], k + 1)
                if n == 2:
                    dve.scalar_tensor_tensor(out=shift[:, n], in0=mv[:, :, 0], scalar=-1.0, in1=rstd[:, n],
                                             op0=ALU.mult, op1=ALU.mult).then_inc(ln_shift[n], 1)
                else:
                    dve.tensor_tensor(shift[:, n], nmean[:], rstd[:, n], ALU.mult).then_inc(ln_shift[n], 1)

            dve.wait_ge(ffn_loaded, 16)
            dve.tensor_reduce(amax_p[:, 1:2], ffn_w_sb[:].rearrange("p e d -> p (e d)"), AX.X, ALU.max,
                              apply_absolute_value=True).then_inc(amax_parts, 1)

            def low(dst, src, high, s):
                return dve.tensor_tensor(dst, src, high.bitcast(F32), ALU.subtract).then_inc(s, 1)

            def exponents(m, w):
                return dve.tensor_scalar(m.bitcast(I32), w.bitcast(I32), EXPONENT_BITS, HALF_BIT,
                                         ALU.bitwise_and, ALU.bitwise_or)

            def at_least(m):
                return dve.tensor_scalar(m, m, LEAST_MAGIC, None, ALU.max)

            def round_weight():
                dve.wait_ge(amax_ready, 1)
                dve.wait_ge(consts_ready, 3)
                dve.tensor_scalar(amax[:, 1:2], amax[:, 1:2], AMAX_FLOOR, None, ALU.max).then_inc(wq_step, 1)
                dve.wait_ge(wq_step, 1)
                dve.reciprocal(finv[:, 1:2], amax[:, 1:2]).then_inc(wq_step, 1)
                dve.wait_ge(wq_step, 2)
                dve.tensor_scalar(fscale[:, 1:2], finv[:, 1:2], FP8_MAX, None, ALU.mult).then_inc(wq_step, 1)
                dve.wait_ge(wq_step, 3)
                w_flat = ffn_w_sb[:].rearrange("p e d -> p (e d)")
                wa, wb, wc = buf_n[:, 0:DT * D], buf_n[:, DT * D:2 * DT * D], buf_n[:, 0:DT * D]
                dve.tensor_scalar(wa, w_flat, fscale[:, 1:2], MAGIC_SHIFT, ALU.mult, ALU.mult).then_inc(wq_step, 1)
                dve.wait_ge(wq_step, 4)
                exponents(wb, wa).then_inc(wq_step, 1)
                dve.wait_ge(wq_step, 5)
                at_least(wb).then_inc(wq_step, 1)
                dve.wait_ge(wq_step, 6)
                dve.scalar_tensor_tensor(out=wc, in0=w_flat, scalar=fscale[:, 1:2], in1=wb,
                                         op0=ALU.mult, op1=ALU.add).then_inc(wq_step, 1)
                dve.wait_ge(wq_step, 7)
                dve.tensor_tensor(ffn_wq[:].rearrange("p e d -> p (e d)"), wc, wb, ALU.subtract).then_inc(ffn_wq_ready, 1)

            def first_norm(k, par, j):
                dve.wait_ge(x_loaded[par], 16 * (j + 1))
                moments(0, k)

            def first_rows(k, par):
                if after(k, 2):
                    dve.wait_ge(y_done, UB * (k - 1))
                normalise(0, k, lambda i: xn_a[par][:, i, :])

            def add_gnn(k):
                dve.wait_ge(bias_added, k + 1)
                for b in range(UB):
                    dve.wait_ge(gnn_done, UB * k + b + 1)
                    for h in range(NT):
                        i = b * NT + h
                        ins = dve.scalar_tensor_tensor(
                            out=tile_of(x_all, k, i), in0=psum[:, G[b], h * D:(h + 1) * D], scalar=1.0,
                            in1=tile_of(x_all, k, i), op0=ALU.mult, op1=ALU.add, accum_out=sums[:, i:i + 1])
                    ins.then_inc(x1_added, 1)
                dve.wait_ge(x1_added, UB * (k + 1))

            def see_amax(k):
                dve.wait_ge(ln_rows[1], k + 1)
                dve.tensor_reduce(column(amax_u, k), unit(xn_all, k).rearrange("p t d -> p (t d)"), AX.X, ALU.max,
                                  apply_absolute_value=True).then_inc(amax_seen, 1)

            def phase_a(k, par, j3, final=None):
                nxt3 = final is None or final + 3 < UNITS
                add_gnn(k)
                mean(1, k)
                if nxt3:
                    first_norm(k + 3, 1 - par, j3)
                if after(k, 1):
                    see_amax(k - 1)
                scale_and_shift(1, k)
                if nxt3:
                    first_rows(k + 3, 1 - par)

            for k in range(3):
                first_norm(k, k % 2, k // 2)
                first_rows(k, k % 2)
            phase_a(0, 0, 1)
            with dve.Fori(0, UNITS // 2 - 2) as j:
                phase_a(2 * j + 1, 1, j + 2)
                phase_a(2 * j + 2, 0, j + 2)
            for k in range(UNITS - 3, UNITS):
                phase_a(k, k % 2, 0, final=k)
            round_weight()
            see_amax(UNITS - 1)

            dve.wait_ge(amax_seen, UNITS)
            dve.tensor_reduce(amax_p[:, 0:1], amax_u[:], AX.X, ALU.max).then_inc(amax_parts, 1)
            dve.wait_ge(amax_ready, 2)
            dve.tensor_scalar(amax[:, 0:1], amax[:, 0:1], AMAX_FLOOR, None, ALU.max).then_inc(scale_step, 1)
            dve.wait_ge(scale_step, 1)
            dve.reciprocal(finv[:, 0:1], amax[:, 0:1]).then_inc(scale_step, 1)
            dve.wait_ge(scale_step, 2)
            dve.tensor_scalar(fscale[:, 0:1], finv[:, 0:1], FP8_MAX, None, ALU.mult).then_inc(scale_step, 1)
            dve.wait_ge(scale_step, 3)
            dve.tensor_scalar(fscale_up[:], fscale[:, 0:1], MAGIC_SHIFT, None, ALU.mult).then_inc(scales_ready, 1)
            dve.reciprocal(finv[:], fscale[:]).then_inc(scale_step, 1)
            dve.wait_ge(scale_step, 4)
            dve.tensor_tensor(fout[:], finv[:, 0:1], finv[:, 1:2], ALU.mult).then_inc(scale_step, 1)

            def take_exponents(k):
                dve.wait_ge(scaled_ready, k + 1)
                if after(k, 1):
                    dve.wait_ge(q_ready, k)
                exponents(buf_m[:], buf_w[:]).then_inc(exponent_ready, 1)

            def add_magic(k):
                dve.wait_ge(magic_ready, k + 1)
                dve.scalar_tensor_tensor(out=buf_t[:], in0=unit(xn_all, k).rearrange("p t d -> p (t d)"),
                                         scalar=fscale[:, 0:1], in1=buf_m[:],
                                         op0=ALU.mult, op1=ALU.add).then_inc(summed_ready, 1)

            take_exponents(0)
            dve.wait_ge(exponent_ready, 1)
            at_least(buf_m[:]).then_inc(magic_ready, 1)
            add_magic(0)
            dve.wait_ge(summed_ready, 1)
            dve.tensor_tensor(q_rows[:].rearrange("p t d -> p (t d)"), buf_t[:], buf_m[:], ALU.subtract).then_inc(q_ready, 1)
            take_exponents(1)
            dve.wait_ge(weights_high, 2)
            low(qk_w[1][:].rearrange("p e d -> p (e d)"), psum[:, PREP, :], qk_w[0][:].rearrange("p e d -> p (e d)"), weights_low)
            low(wv_t[1][:].rearrange("p e d -> p (e d)"), wv_raw, wv_t[0][:].rearrange("p e d -> p (e d)"), weights_low)

            def add_ffn(k):
                for b in range(UB):
                    dve.wait_ge(ffn_done, UB * k + b + 1)
                    dve.scalar_tensor_tensor(out=half(x_all, k, b), in0=psum[:, FFN[b], :].rearrange("p (h d) -> p h d", h=NT),
                                             scalar=fout[:, 0:1], in1=half(x_all, k, b),
                                             op0=ALU.mult, op1=ALU.add).then_inc(x2_added, 1)
                dve.wait_ge(x2_added, UB * (k + 1))

            def mask_relations(k, b):
                if after(k, 1):
                    dve.wait_ge(sq_ready, UB * k)
                    dve.wait_ge(rel_low, UB * k)
                dve.wait_ge(rel_done, UB * k + b + 1)
                dve.tensor_tensor(rel_32[:, b], psum[:, REL[b], :].rearrange("p (m n) -> p m n", m=NT), adj_nat[:],
                                  ALU.mult).then_inc(rel_masked, 1)

            def add_att(k):
                dve.wait_ge(norm_ready, k + 1)
                dve.reciprocal(rstd[:, 0], std[:, 0]).then_inc(inv_ready, 1)
                dve.wait_ge(inv_ready, k + 1)
                for b in range(UB):
                    dve.wait_ge(att_done, UB * k + b + 1)
                    for h in range(NT):
                        i = b * NT + h
                        ins = dve.scalar_tensor_tensor(
                            out=tile_of(x_all, k, i), in0=psum[:, ATT[b], h * D:(h + 1) * D],
                            scalar=rstd[:, 0, i:i + 1], in1=tile_of(x_all, k, i), op0=ALU.mult, op1=ALU.add,
                            accum_out=sums[:, i:i + 1])
                    ins.then_inc(x3_added, 1)
                dve.wait_ge(x3_added, UB * (k + 1))

            def nibbles(k):
                dve.wait_ge(ln_rows[3], k + 1)
                if after(k, 1):
                    dve.wait_ge(codes_ready, k)
                dve.scalar_tensor_tensor(
                    out=hit, in0=unit(xn_all, k)[:, :, NIBBLES_COL:NIBBLES_COL + NIBBLES * NIB], scalar=0.5,
                    in1=iota_down[:].unsqueeze(1).to_broadcast([P, UT, NIBBLES * NIB]),
                    op0=ALU.is_gt, op1=ALU.mult).then_inc(hits_ready, 1)
                dve.wait_ge(hits_ready, k + 1)
                dve.tensor_reduce(unit(code, k), hit.rearrange("p t (g i) -> p t g i", g=NIBBLES),
                                  AX.X, ALU.max).then_inc(codes_ready, 1)

            def finish(k):
                add_att(k)
                mean(3, k)

            def low_xt(k):
                for b in range(UB):
                    dve.wait_ge(xt_moved, UB * k + b + 1)
                    low(xn_t[1][:, :, b, :], psum[:, XT[b], :].rearrange("p (e n) -> p e n", e=DT), xn_t[0][:, :, b, :], xt_low)

            def low_qk(k, e):
                dve.wait_ge(qk_moved, DT * k + e + 1)
                low(qk_t[1][:, e].rearrange("p b n -> p (b n)"), psum[:, QK[e], :],
                    qk_t[0][:, e].rearrange("p b n -> p (b n)"), qk_low)

            def low_v(k, b):
                dve.wait_ge(v_moved, UB * k + b + 1)
                low(v_sb[1][:, b].rearrange("p m d -> p (m d)"), psum[:, VB[b], :],
                    v_sb[0][:, b].rearrange("p m d -> p (m d)"), v_low)

            dve.wait_ge(scale_step, 5)
            add_ffn(0)
            moments(2, 0)
            scale_and_shift(2, 0)
            add_magic(1)
            take_exponents(2)
            low_xt(0)
            add_ffn(1)
            moments(2, 1)
            add_magic(2)
            scale_and_shift(2, 1)

            def phase_b(k, final=None):
                nxt = final is None or final + 1 < UNITS
                nxt2 = final is None or final + 2 < UNITS
                more = final is None or final + AHEAD < UNITS
                if after(k, 1):
                    finish(k - 1)
                low_qk(k, 0)
                if more:
                    take_exponents(k + AHEAD)
                low_qk(k, 1)
                if after(k, 3):
                    nibbles(k - 3)
                if nxt2:
                    add_ffn(k + 2)
                if after(k, 1):
                    scale_and_shift(3, k - 1)
                low_v(k, 0)
                mask_relations(k, 0)
                low_v(k, 1)
                mask_relations(k, 1)
                if nxt:
                    low_xt(k + 1)
                if nxt2:
                    moments(2, k + 2)
                if more:
                    add_magic(k + AHEAD)
                if nxt2:
                    scale_and_shift(2, k + 2)

            for k in range(3):
                phase_b(k)
            with dve.Fori(3, UNITS - AHEAD) as k:
                phase_b(k)
            for k in range(UNITS - AHEAD, UNITS):
                phase_b(k, final=k)
            finish(UNITS - 1)
            scale_and_shift(3, UNITS - 1)
            for k in range(UNITS - 3, UNITS):
                nibbles(k)

            def xn_col(c):
                return xn_all[:, :, c]

            dve.tensor_scalar(mask[:, 0], xn_col(MUL_COL), 0.5, None, ALU.is_ge).then_inc(mask_step, 1)
            dve.wait_ge(mask_step, 1)
            dve.scalar_tensor_tensor(out=mask[:, 1], in0=xn_col(MARK_COL), scalar=0.5, in1=mask[:, 0],
                                     op0=ALU.is_ge, op1=ALU.mult).then_inc(mask_step, 1)
            dve.wait_ge(mask_step, 2)
            dve.tensor_tensor_scan(pos, ones[:], mask[:, 1], 0.0, ALU.mult, ALU.add).then_inc(counted, 1)
            dve.wait_ge(counted, 1)
            dve.tensor_tensor(slot_of, pos, mask[:, 1], ALU.mult).then_inc(slots_step, 1)
            dve.wait_ge(codes_ready, UNITS)
            by_tile = feats[:, 0:NIBBLES, :].rearrange("p f t -> p t f")
            dve.tensor_scalar(by_tile, code, -1.0, float(NIB), ALU.mult, ALU.add).then_inc(feats_step, 1)
            dve.wait_ge(feats_step, 1)
            dve.scalar_tensor_tensor(out=by_tile, in0=code, scalar=0.0, in1=by_tile,
                                     op0=ALU.is_gt, op1=ALU.mult).then_inc(feats_step, 1)
            dve.tensor_copy(feats[:, NIBBLES, :], xn_col(OPCODE_COL)).then_inc(feats_step, 1)
            dve.memset(digit, 0.0).then_inc(digit_zeroed, 1)
            dve.wait_ge(most_ready, 1)
            dve.tensor_copy(most_i[:], most[:]).then_inc(most_int, 1)
            dve.wait_ge(slots_step, 1)
            dve.wait_ge(feats_step, 3)
            dve.memset(f_rows, 0.0).then_inc(f_zeroed, 1)
            dve.wait_ge(f_zeroed, 1)
            dve.wait_ge(mlp_loaded, 16)

            def mlp_block(j):
                if after(j, 1):
                    dve.wait_ge(f_turned, 2 * j)
                slots = iota_slot[:, bass.ds(SLOTS * j, SLOTS)] if not isinstance(j, int) else iota_slot[:, 0:SLOTS]
                dve.tensor_tensor(sel, slot_of.unsqueeze(1).to_broadcast([P, SLOTS, TILES]),
                                  slots.unsqueeze(2).to_broadcast([P, SLOTS, TILES]), ALU.is_equal).then_inc(selected, 1)
                dve.wait_ge(selected, j + 1)
                prod_s = prod.rearrange("p (s t) -> p s t", s=SLOTS)
                steps = 2 * NF - 1
                for f in range(NF):
                    if f:
                        dve.wait_ge(product, steps * j + 2 * f)
                    elif after(j, 1):
                        dve.wait_ge(f_ready, j)
                    dve.tensor_tensor(prod_s, sel, feats[:, f, :].unsqueeze(1).to_broadcast([P, SLOTS, TILES]),
                                      ALU.mult).then_inc(product, 1)
                    dve.wait_ge(product, steps * j + 2 * f + 1)
                    dve.tensor_reduce(f_rows[:, :, f:f + 1], prod_s, AX.X,
                                      ALU.add).then_inc(product if f < NF - 1 else f_ready, 1)
                for l in range(RELUS):
                    for c in range(1, CHUNKS, 2):
                        dve.wait_ge(main_done[c], RELUS * j + l + 1)
                        dve.tensor_scalar(hid[c], psum[:, MAIN[c], :], b_main[:, l:l + 1], 0.0,
                                          ALU.add, ALU.max).then_inc(hid_ready[c], 1)
                dve.wait_ge(last_turned, j + 1)
                got = psum[:, FT[0], :].rearrange("p (s c r) -> p s c r", c=CHUNKS, r=REM)[:, :, :, 0]
                into = found[:].rearrange("p a (h s) -> p s h a", h=2)
                for a in range(N_POS_USED):
                    ins = dve.tensor_scalar(into[:, :, :, a], got[:, :, a:CHUNKS:N_POS_USED], 0.0, float(NIB - 1), ALU.max, ALU.min)
                ins.then_inc(clip_step, 1)
                dve.wait_ge(clip_step, 3 * j + 1)
                dve.tensor_scalar(found[:], found[:], INT_MAGIC, INT_MAGIC, ALU.add, ALU.subtract).then_inc(clip_step, 1)
                dve.wait_ge(clip_step, 3 * j + 2)
                dve.tensor_scalar(found[:], found[:], 1.0, None, ALU.add).then_inc(clip_step, 1)
                dve.wait_ge(clip_step, 3 * j + 3)
                prod_t = prod.rearrange("p (t s) -> p t s", s=SLOTS)
                for a in range(N_POS_USED):
                    if after(j, 1) or a:
                        dve.wait_ge(spread_sum, N_POS_USED * j + a)
                    else:
                        dve.wait_ge(digit_zeroed, 1)
                    dve.tensor_tensor(prod_t, sel.rearrange("p s t -> p t s"),
                                      found[:, a, :].unsqueeze(1).to_broadcast([P, TILES, SLOTS]),
                                      ALU.mult).then_inc(spread_step, 1)
                    dve.wait_ge(spread_step, 2 * (N_POS_USED * j + a) + 1)
                    dve.tensor_reduce(spread_r.unsqueeze(2), prod_t, AX.X, ALU.add).then_inc(spread_step, 1)
                    dve.wait_ge(spread_step, 2 * (N_POS_USED * j + a) + 2)
                    dve.tensor_tensor(digit[:, :, a], digit[:, :, a], spread_r, ALU.add).then_inc(spread_sum, 1)

            mlp_block(0)
            dve.wait_ge(most_int, 1)
            n = dve.value_load(most_i[0:1, 0:1])
            with dve.Fori(1, BLOCKS) as j:
                with dve.If(SLOTS * j < n):
                    mlp_block(j)
            dve.drain().then_inc(digit_ready, 1)
            dve.wait_ge(digit_ready, 1)
            dve.wait_ge(base_ready, UNITS)
            dve.tensor_tensor(onehot.rearrange("p (t a i) -> p t a i", t=TILES, a=N_POS_USED),
                              digit.unsqueeze(3).to_broadcast([P, TILES, N_POS_USED, NIB]),
                              iota_up[:].unsqueeze(1).unsqueeze(1).to_broadcast([P, TILES, N_POS_USED, NIB]),
                              ALU.is_equal).then_inc(final_step, 1)
            dve.wait_ge(final_step, 1)
            cols = x_all[:, :, OUTPUT_COL:OUTPUT_COL + OUTPUT_W]
            dve.scalar_tensor_tensor(out=cols, in0=onehot.rearrange("p (t c) -> p t c", t=TILES), scalar=2.0, in1=cols,
                                     op0=ALU.mult, op1=ALU.add).then_inc(final_ready, 1)


def lay_out_mlp(w, b):
    import numpy as np

    layers, ge, _ = w.shape
    rem, hid = ge - P, layers - 2
    chunks = P // rem
    at, width = mlp_columns(layers, ge)
    laid = np.zeros((P, width), w.dtype)
    sq = laid[:, at["sq"]].reshape(P, hid, 2 * P + rem)
    rm = laid[:, at["rm"]].reshape(P, hid, chunks, P)
    turned = w.transpose(2, 0, 1)[:, 1:1 + hid]
    sq[:, :, 0:P] = turned[0:P, :, 0:P]
    sq[:, :, 2 * P:] = turned[0:P, :, P:]
    for c in range(chunks):
        quadrant = slice(rem * c, rem * (c + 1))
        sq[quadrant, :, P + rem * c:P + rem * (c + 1)] = turned[P:, :, P:]
        rm[quadrant, :, c, :] = turned[P:, :, 0:P]
        laid[quadrant, at["out_r"].start + rem * c] = w[-1, GE_RESULT, P:]
        laid[quadrant, at["b_rem"]] = b[:, P:].T
    laid[:, at["sq"]] = sq.reshape(P, -1)
    laid[:, at["rm"]] = rm.reshape(P, -1)
    start = at["in"].start
    for a in range(N_POS_USED):
        for row, col in ((a, GE_A), (N_POS_USED + a, GE_B), (NIBBLES, GE_OP)):
            laid[row, start + a * P:start + (a + 1) * P] = w[0, 0:P, col]
            left = start + N_POS_USED * P + a * rem
            laid[row, left:left + rem] = w[0, P:, col]
    laid[:, at["out_m"].start] = w[-1, GE_RESULT, 0:P]
    laid[:, at["b_main"]] = b[:, 0:P].T
    laid[:, at["b_out"]] = b[-1, GE_RESULT]
    return laid


def kernel(x, adj, L0_gnn_weight, L0_gnn_bias, L0_ffn_weight, L1_gnn_Wq, L1_gnn_Wk, L1_gnn_Wv, L1_ffn_W, L1_ffn_b):
    import numpy as np
    import concourse.bacc as bacc
    from concourse.bass_utils import run_bass_kernel_spmd

    mlp_w, mlp_b = np.asarray(L1_ffn_W), np.asarray(L1_ffn_b)
    laid = {
        "x": np.asarray(x), "adj": np.asarray(adj), "adj_turned": np.asarray(adj).T,
        "gnn_w": np.asarray(L0_gnn_weight), "gnn_b": np.asarray(L0_gnn_bias), "ffn_w": np.asarray(L0_ffn_weight),
        "wq": np.asarray(L1_gnn_Wq), "wk": np.asarray(L1_gnn_Wk), "wv_turned": np.asarray(L1_gnn_Wv).T,
        "mlp": lay_out_mlp(mlp_w, mlp_b),
    }
    laid = {f"in_{name}": np.ascontiguousarray(a) for name, a in laid.items()}
    nc = bacc.Bacc("TRN2", target_bir_lowering=False, num_devices=1, dynamic_dma_scratch_size=1024)
    args = [nc.dram_tensor(name, a.shape, mybir.dt.from_np(a.dtype), kind="ExternalInput").ap()
            for name, a in laid.items()]
    out = nc.dram_tensor("out", x.shape, F32, kind="ExternalOutput").ap()
    adj_ffn_kernel(nc, *args, mlp_w.shape[0], mlp_w.shape[1], out)
    return run_bass_kernel_spmd(nc, [laid], core_ids=[0]).results[0]["out"]
```

```python
from contextlib import ExitStack

import concourse.bass as bass
from concourse import mybir
from concourse.alu_op_type import AluOpType as ALU

ACT = mybir.ActivationFunctionType
AX = mybir.AxisListType
F32 = mybir.dt.float32
BF16 = mybir.dt.bfloat16
I32 = mybir.dt.int32
F32R = mybir.dt.float32r
PARTS = ("high", "low")
PRODUCTS = ((0, 0), (0, 1), (1, 0))

P = 128
EPS = 1e-5
FP8_MAX = 448.0
AMAX_FLOOR = 1e-12
MAGIC_SHIFT = float(1 << 20)
MIN_NORMAL = 2.0 ** -6
LEAST_MAGIC = 1.5 * MIN_NORMAL * MAGIC_SHIFT
EXPONENT_BITS = 0x7F800000
HALF_BIT = 0x00400000
SIGN_BIT = -(1 << 31)
INT_MAGIC = float(1 << 23)

MARK_COL, MUL_COL, OPCODE_COL = 0, 1, 29
NIBBLES_COL, NIBBLES = 64, 4
OUTPUT_COL, OUTPUT_W = 128, 32
NIB = 16
GE_A, GE_B, GE_OP, GE_RESULT = 0, 1, 30, 2
N_POS_USED = 2


def mlp_columns(layers, ge):
    rem, hid = ge - P, layers - 2
    chunks = P // rem
    widths = {"sq": hid * (2 * P + rem), "rm": hid * chunks * P, "in": N_POS_USED * (P + rem),
              "out_m": rem, "out_r": P, "b_main": layers, "b_rem": layers, "b_out": 1}
    at, start = {}, 0
    for name, width in widths.items():
        at[name] = slice(start, start + width)
        start += width
    return at, start


def adj_ffn_kernel(nc, x, adj, adj_turned, gnn_w, gnn_b, ffn_w, wq, wk, wv_turned, mlp, layers, ge, out):
    B, N, D = x.shape
    LAYERS, GE = layers, ge
    NT = N // P
    DT = D // P
    TILES = B * NT
    UB = 2
    UT = UB * NT
    UNITS = B // UB
    UW = UT * D
    REM = GE - P
    CHUNKS = P // REM
    CW = 512
    SLOTS = CW * CHUNKS // N_POS_USED // P
    GROUP = 16
    GROUPS = TILES // GROUP
    SENT = 2
    HALF = SLOTS // 2
    BLOCKS = TILES // SLOTS
    HID = LAYERS - 2
    RELUS = LAYERS - 1
    NF = NIBBLES + 1

    x_rows = x.rearrange("b (h p) d -> p (b h) d", p=P)
    out_rows = out.rearrange("b (h p) d -> p (b h) d", p=P)

    with ExitStack() as ctx:
        def sb(name, shape, dt=F32):
            return ctx.enter_context(nc.sbuf_tensor(name, shape, dt))

        def sem(name):
            return ctx.enter_context(nc.semaphore(name))

        AHEAD = 3
        PIECES = 4

        x_all = sb("x_all", [P, TILES, D])
        xn_all = sb("xn_all", [P, TILES, D])
        ident = sb("ident", [P, P])
        ident_bf = sb("ident_bf", [P, P], BF16)
        eps = sb("eps", [P, 1])
        ones = sb("ones", [P, TILES])
        adj_nat = sb("adj_nat", [P, NT, N])
        adj_t = sb("adj_t", [P, NT, N])
        gnn_w_sb = sb("gnn_w_sb", [P, DT, D])
        ffn_w_sb = sb("ffn_w_sb", [P, DT, D])
        ffn_wq = sb("ffn_wq", [P, DT, D], BF16)
        qk_w = [sb(f"qk_w_{part}", [P, DT, D], F32R) for part in PARTS]
        wv_t = [sb(f"wv_t_{part}", [P, DT, D], F32R) for part in PARTS]
        at, mlp_width = mlp_columns(LAYERS, GE)
        mlp_sb = sb("mlp_sb", [P, mlp_width])
        w_sq = mlp_sb[:, at["sq"]].rearrange("p (l e) -> p l e", l=HID)
        w_mm, w_rr, w_mr = w_sq[:, :, 0:P], w_sq[:, :, P:2 * P], w_sq[:, :, 2 * P:2 * P + REM]
        w_rm = mlp_sb[:, at["rm"]].rearrange("p (l c e) -> p l c e", l=HID, c=CHUNKS)
        w_in = mlp_sb[:, at["in"]]
        w_in_m = w_in[:, 0:N_POS_USED * P].rearrange("p (a e) -> p a e", a=N_POS_USED)
        w_in_r = w_in[:, N_POS_USED * P:].rearrange("p (a e) -> p a e", a=N_POS_USED)
        w6_m, w6_r = mlp_sb[:, at["out_m"]], mlp_sb[:, at["out_r"]]
        b_main, b_rem, b_out = mlp_sb[:, at["b_main"]], mlp_sb[:, at["b_rem"]], mlp_sb[:, at["b_out"]]
        iota_p = sb("iota_p", [P, P])
        iota_slot = iota_p[:, 0:TILES]
        before = sb("before", [P, P])
        places = sb("places", [P, NIBBLES])
        iota_down = sb("iota_down", [P, NIBBLES * NIB])
        iota_up = sb("iota_up", [P, NIB])

        buf_w = sb("buf_w", [P, UW])
        buf_m = sb("buf_m", [P, UW])
        buf_t = sb("buf_t", [P, UW])
        buf_n = sb("buf_n", [P, UW])
        buf_r = sb("buf_r", [P, UW])
        xn_t = [sb(f"xn_t_{part}", [P, DT, UB, N], F32R) for part in PARTS]
        qk_t = [sb(f"qk_t_{part}", [P, DT, UB, N], F32R) for part in PARTS]
        v_sb = [sb(f"v_{part}", [P, UB, NT, D], F32R) for part in PARTS]
        rel_t = [sb(f"rel_{part}", [P, UB, NT, N], F32R) for part in PARTS]
        q_rows = sb("q_rows", [P, UT, D], BF16)
        q_t = sb("q_t", [P, UB, DT, N], BF16)

        stats = sb("stats", [P, UT, 6])
        mv = sb("mv", [P, UT, 2])
        sums = sb("sums", [P, UT])
        squares = sb("squares", [P, UT])
        nmean = sb("nmean", [P, UT])
        shift = sb("shift", [P, 4, UT])
        std = sb("std", [P, 4, UT])
        rstd = sb("rstd", [P, 4, UT])
        amax_u = sb("amax_u", [P, UNITS])
        amax_p = sb("amax_p", [P, 2])
        amax = sb("amax", [P, 2])
        fscale = sb("fscale", [P, 2])
        fscale_up = sb("fscale_up", [P, 1])
        finv = sb("finv", [P, 2])
        fout = sb("fout", [P, 1])
        most = sb("most", [P, 1])
        most_i = sb("most_i", [P, 1], I32)
        total_i = sb("total_i", [1, 1], I32)
        found = sb("found", [P, N_POS_USED, SLOTS])
        packed = sb("packed", [P, SLOTS])

        psum = ctx.enter_context(nc.psum_tensor("psum", [P, 8, 512], F32))

        bias_bc = q_rows[:, 0:2, :].rearrange("p t d -> p (t d)").bitcast(F32)

        def tiles(buf):
            return buf[:].rearrange("p (t d) -> p t d", d=D)

        xn_a = [tiles(buf_n), tiles(buf_w)]
        y_t = [b[:].rearrange("p (b e n) -> p b e n", b=UB, e=DT) for b in (buf_m, buf_t)]
        wq_sb, wk_sb = (buf_r[:, i * DT * D:(i + 1) * DT * D].rearrange("p (e d) -> p e d", e=DT) for i in (0, 1))
        wv_raw = q_t[:].rearrange("p b e n -> p (b e n)").bitcast(F32)
        xn_b = tiles(buf_n)
        rel_32 = buf_r[:].rearrange("p (b m n) -> p b m n", b=UB, m=NT)
        rel_sq = buf_w[:].rearrange("p (b m n) -> p b m n", b=UB, m=NT)
        hit = adj_t[:, 0, :].rearrange("p (t i) -> p t i", t=UT)
        code = adj_t[:, 1, :].rearrange("p (t g) -> p t g", g=NIBBLES)
        feats = gnn_w_sb[:].rearrange("p e d -> p (e d)")[:, 0:NF * TILES].rearrange("p (f t) -> p f t", f=NF)
        free = ffn_w_sb[:].rearrange("p e d -> p (e d)")
        mask = free[:, 0:2 * TILES].rearrange("p (a t) -> p a t", a=2)
        pos, slot_of, back_sum, result = (free[:, i * TILES:(i + 1) * TILES] for i in (2, 3, 4, 5))
        small = adj_nat[:].rearrange("p m n -> p (m n)")
        sent_of = small[:, 0:SENT * TILES].rearrange("p (f t) -> p f t", f=SENT)
        place_i = small[:, 2 * TILES:4 * TILES].bitcast(I32).rearrange("p (a s) -> p a s", a=2)
        place = small[:, 4 * TILES:6 * TILES].rearrange("p (a s) -> p a s", a=2)
        used = small[:, 6 * TILES:7 * TILES]
        sent = small[:, 7 * TILES:7 * TILES + SENT * GROUP].rearrange("p (s f) -> p s f", f=SENT)
        got_back = small[:, 7 * TILES + SENT * GROUP:7 * TILES + (SENT + 1) * GROUP]
        sel = [b[:].rearrange("p (s t) -> p s t", s=GROUP) for b in (buf_w, buf_m)]
        to_tile = [b[:].rearrange("p (s t) -> p s t", s=GROUP) for b in (buf_t, buf_n)]
        prod = buf_r[:]
        room = xn_all[:].rearrange("p t d -> p (t d)")
        taken = [0]

        def take(n):
            taken[0] += n
            return room[:, taken[0] - n:taken[0]]

        f_rows = take(SLOTS * P).rearrange("p (s f) -> p s f", f=P)
        f_t = take(2 * CW).rearrange("p (h c) -> p h c", h=2)
        hid = [take(CW) for _ in range(CHUNKS)]
        hid_r = [take(CW) for _ in range(2)]
        last_sb = take(CW)
        hid_parts = [[(xn_t, qk_t)[c // 2][part][:, c % 2].rearrange("p b n -> p (b n)") for part in (0, 1)]
                     for c in range(CHUNKS)]
        hid_r_parts = [[rel_t[part][:, par].rearrange("p m n -> p (m n)") for part in (0, 1)] for par in (0, 1)]
        mm_parts = [[v_sb[part][:, par, 0, 0:P] for part in (0, 1)] for par in (0, 1)]
        rm_parts = [[w[part][:].rearrange("p e d -> p (e d)").rearrange("p (c e) -> p c e", c=CHUNKS) for part in (0, 1)]
                    for w in (qk_w, wv_t)]
        to_part = take(GROUP * P).rearrange("p (s q) -> p s q", s=GROUP)
        to_part_t = [take(GROUP * P // 2).bitcast(BF16).rearrange("p (s q) -> p s q", s=GROUP) for _ in range(2)]
        parcels = take(GROUP * SENT * TILES).rearrange("p (s f t) -> p s f t", s=GROUP, f=SENT)
        arrived = take(SENT * TILES).rearrange("p (f t) -> p f t", f=SENT)
        nibbles_i = take((NIBBLES + 1) * TILES).bitcast(I32).rearrange("p (f t) -> p f t", t=TILES)
        rows_f = take(NF * TILES).rearrange("p (f t) -> p f t", f=NF)
        results = take(TILES // 2).bitcast(BF16)
        digit_i = take(3 * TILES).bitcast(I32).rearrange("p (a t) -> p a t", a=3)
        digit = take(N_POS_USED * TILES).rearrange("p (t a) -> p t a", a=N_POS_USED)
        onehot = take(TILES * OUTPUT_W)

        def unit(buf, k):
            return buf[:, bass.ds(UT * k, UT), :] if not isinstance(k, int) else buf[:, UT * k:UT * (k + 1), :]

        def block_of(rows, j):
            return rows[:, :, bass.ds(SLOTS * j, SLOTS)] if not isinstance(j, int) else rows[:, :, SLOTS * j:SLOTS * (j + 1)]

        def half(buf, k, b):
            t = UT * k + NT * b
            return buf[:, bass.ds(t, NT), :] if not isinstance(k, int) else buf[:, t:t + NT, :]

        def column(buf, k):
            return buf[:, bass.ds(k, 1)] if not isinstance(k, int) else buf[:, k:k + 1]

        def after(k, first=0):
            return k >= first if isinstance(k, int) else True

        x_loaded = [sem("x_loaded_even"), sem("x_loaded_odd")]
        adj_loaded, gnn_loaded, ffn_loaded = sem("adj_loaded"), sem("gnn_loaded"), sem("ffn_loaded")
        wv_loaded, att_loaded, mlp_loaded = sem("wv_loaded"), sem("att_loaded"), sem("mlp_loaded")
        consts_ready, zeros_ready = sem("consts_ready"), sem("zeros_ready")
        ident_ready = sem("ident_ready")
        ln_squares = [sem(f"ln{i}_squares") for i in range(4)]
        ln_shift = [sem(f"ln{i}_shift") for i in range(4)]
        ln_stats = [sem(f"ln{i}_stats") for i in range(4)]
        ln_moments = [sem(f"ln{i}_moments") for i in range(4)]
        ln_std = [sem(f"ln{i}_std") for i in range(4)]
        ln_rstd = [sem(f"ln{i}_rstd") for i in range(4)]
        ln_rows = [sem(f"ln{i}_rows") for i in range(4)]
        y_done, y_moved, gnn_done, bias_added = sem("y_done"), sem("y_moved"), sem("gnn_done"), sem("bias_added")
        x1_added, amax_seen = sem("x1_added"), sem("amax_seen")
        prep_done = sem("prep_done")
        amax_parts, amax_ready, scale_step, scales_ready = (
            sem("amax_parts"), sem("amax_ready"), sem("scale_step"), sem("scales_ready"))
        wq_step, ffn_wq_ready = sem("wq_step"), sem("ffn_wq_ready")
        scaled_ready, exponent_ready, magic_ready = sem("scaled_ready"), sem("exponent_ready"), sem("magic_ready")
        summed_ready, q_ready = sem("summed_ready"), sem("q_ready")
        q_turned, q_t_ready, ffn_done, x2_added = sem("q_turned"), sem("q_t_ready"), sem("ffn_done"), sem("x2_added")
        xt_turned, xt_moved, qk_done, qk_moved = sem("xt_turned"), sem("xt_moved"), sem("qk_done"), sem("qk_moved")
        v_done, v_moved, rel_done, rel_masked = sem("v_done"), sem("v_moved"), sem("rel_done"), sem("rel_masked")
        xt_low, qk_low, v_low = sem("xt_low"), sem("qk_low"), sem("v_low")
        rel_high, rel_low, weights_high, weights_low = (
            sem("rel_high"), sem("rel_low"), sem("weights_high"), sem("weights_low"))
        sq_ready, ss_done, norm_ready, inv_ready = sem("sq_ready"), sem("ss_done"), sem("norm_ready"), sem("inv_ready")
        att_done, x3_added = sem("att_done"), sem("x3_added")
        hits_ready, codes_ready, base_ready = sem("hits_ready"), sem("codes_ready"), sem("base_ready")
        base_left, base_right, output_stored = sem("base_left"), sem("base_right"), sem("output_stored")
        mask_step, feats_step, slots_step = sem("mask_step"), sem("feats_step"), sem("slots_step")
        counted, most_ready, most_int, total_int = sem("counted"), sem("most_ready"), sem("most_int"), sem("total_int")
        sums_done, place_step, zeroed = sem("sums_done"), sem("place_step"), sem("zeroed")
        part_distance, part_onehots = sem("part_distance"), sem("part_onehots")
        pick_step, onehots, parcels_ready = sem("pick_step"), sem("onehots"), sem("parcels_ready")
        parcels_sent, parcels_in, all_arrived = sem("parcels_sent"), sem("parcels_in"), sem("all_arrived")
        part_turned, part_moved, unpack_step = sem("part_turned"), sem("part_moved"), sem("unpack_step")
        f_ready, all_results, back_onehots = sem("f_ready"), sem("all_results"), sem("back_onehots")
        sent_back, back_step, digit_step = sem("sent_back"), sem("back_step"), sem("digit_step")
        f_turned, f_t_ready = sem("f_turned"), sem("f_t_ready")
        main_done = [sem(f"main{c}_done") for c in range(CHUNKS)]
        hid_ready = [sem(f"hid{c}_ready") for c in range(CHUNKS)]
        rem_done, hid_r_ready = sem("rem_done"), sem("hid_r_ready")
        hid_high = [sem(f"hid{c}_high") for c in range(CHUNKS)]
        hid_low = [sem(f"hid{c}_low") for c in range(CHUNKS)]
        hid_r_high, hid_r_low = sem("hid_r_high"), sem("hid_r_low")
        layer_high, layer_low = sem("layer_high"), sem("layer_low")
        last_done, last_ready, last_turned = sem("last_done"), sem("last_ready"), sem("last_turned")
        clip_step, all_back, final_step, final_ready = sem("clip_step"), sem("all_back"), sem("final_step"), sem("final_ready")

        def rows_of(w):
            return w.rearrange("(t p) d -> p t d", p=P)

        waited = {}

        def stand_alone(engine, name):
            if name not in waited:
                waited[name] = sem(f"waited_{name}")
            engine.sem_inc(waited[name], 1)

        Y, G = (1, 2), (3, 4)
        QT, QK, FFN, VB, REL, XT, ATT, SS = 0, (1, 2), (3, 4), (5, 6), (1, 2), (3, 4), (5, 6), 7
        PREP = 7
        MAIN, RB, LAST, FT = (1, 2, 3, 4), 5, 0, (6, 7)
        COUNTS, ARRIVE, TURN, BACK = 0, 5, (1, 2, 3, 4), (5, 6)

        block = ctx.enter_context(nc.Block())

        @block.sync
        def _(sp):
            for par in range(2):
                sp.dma_start(unit(x_all, par), unit(x_rows, par)).then_inc(x_loaded[par], 16)
            sp.dma_start(wv_raw.rearrange("p (e d) -> p e d", e=DT), rows_of(wv_turned)).then_inc(wv_loaded, 16)
            sp.dma_start(ffn_w_sb[:], rows_of(ffn_w)).then_inc(ffn_loaded, 16)
            for dst, src in ((wq_sb, wq), (wk_sb, wk), (adj_nat[:], adj)):
                sp.dma_start(dst, rows_of(src)).then_inc(att_loaded, 16)
            sp.dma_start(mlp_sb[:], mlp).then_inc(mlp_loaded, 16)
            with sp.Fori(1, UNITS // 2) as j:
                for par in range(2):
                    sp.wait_ge(x_loaded[par], 16 * j)
                    stand_alone(sp, "sp")
                    sp.dma_start(unit(x_all, 2 * j + par), unit(x_rows, 2 * j + par)).then_inc(x_loaded[par], 16)

            def store(k):
                sp.wait_ge(base_ready, k + 1)
                stand_alone(sp, "sp")
                if after(k, 1):
                    sp.wait_ge(base_left, 16 * k)
                    sp.wait_ge(base_right, 16 * k)
                stand_alone(sp, "sp")
                sp.dma_start(unit(out_rows, k)[:, :, 0:OUTPUT_COL],
                             unit(x_all, k)[:, :, 0:OUTPUT_COL]).then_inc(base_left, 16)
                sp.dma_start(unit(out_rows, k)[:, :, OUTPUT_COL + OUTPUT_W:D],
                             unit(x_all, k)[:, :, OUTPUT_COL + OUTPUT_W:D]).then_inc(base_right, 16)

            store(0)
            with sp.Fori(1, UNITS) as k:
                store(k)
            for h in range(PIECES):
                some = slice(h * TILES // PIECES, (h + 1) * TILES // PIECES)
                sp.wait_ge(final_ready, h + 1)
                sp.dma_start(out_rows[:, some, OUTPUT_COL:OUTPUT_COL + OUTPUT_W],
                             x_all[:, some, OUTPUT_COL:OUTPUT_COL + OUTPUT_W]).then_inc(output_stored, 16)
            sp.wait_ge(base_left, 16 * UNITS)
            sp.wait_ge(base_right, 16 * UNITS)
            sp.wait_ge(output_stored, 16 * PIECES)

        @block.gpsimd
        def _(pool):
            pool.memset(ident[:], 0.0).then_inc(zeros_ready, 1)
            pool.wait_ge(zeros_ready, 1)
            pool.affine_select(out=ident[:], in_=ident[:], compare_op=ALU.not_equal, fill=1.0, base=0,
                               pattern=[[-1, P]], channel_multiplier=1).then_inc(ident_ready, 1)
            pool.memset(eps[:], EPS)
            pool.memset(ones[:], 1.0).then_inc(consts_ready, 1)
            pool.memset(before[:], 1.0).then_inc(zeros_ready, 1)
            pool.wait_ge(zeros_ready, 2)
            pool.affine_select(out=before[:], in_=before[:], compare_op=ALU.is_gt, fill=0.0, base=0,
                               pattern=[[1, P]], channel_multiplier=-1)
            pool.wait_ge(ident_ready, 1)
            pool.tensor_copy(ident_bf[:], ident[:]).then_inc(consts_ready, 1)
            pool.iota(iota_p[:], [[1, P]], base=1, channel_multiplier=0, allow_small_or_imprecise_dtypes=True)
            for g in range(NIBBLES):
                pool.memset(places[:, g:g + 1], float(NIB ** g))
            pool.iota(iota_down[:], [[0, NIBBLES], [-1, NIB]], base=NIB, channel_multiplier=0,
                      allow_small_or_imprecise_dtypes=True)
            pool.iota(iota_up[:], [[1, NIB]], base=1, channel_multiplier=0,
                      allow_small_or_imprecise_dtypes=True).then_inc(consts_ready, 1)
            pool.wait_ge(gnn_loaded, 32)

            def add_bias(k):
                pool.wait_ge(ln_rows[0], k + 1)
                pool.tensor_tensor(unit(x_all, k), unit(x_all, k),
                                   bias_bc.unsqueeze(1).to_broadcast([P, UT, D]), ALU.add).then_inc(bias_added, 1)

            add_bias(0)
            pool.wait_ge(amax_parts, 1)
            pool.partition_all_reduce(amax[:, 1:2], amax_p[:, 1:2], P, bass.bass_isa.ReduceOp.max).then_inc(amax_ready, 1)
            with pool.Fori(1, UNITS) as k:
                add_bias(k)

            pool.wait_ge(amax_parts, 2)
            pool.partition_all_reduce(amax[:, 0:1], amax_p[:, 0:1], P, bass.bass_isa.ReduceOp.max).then_inc(amax_ready, 1)

            def scale_up(k):
                if after(k, 4):
                    pool.wait_ge(ss_done, k - 3)
                else:
                    pool.wait_ge(exponent_ready, k)
                pool.tensor_tensor(tiles(buf_w), unit(xn_all, k),
                                   fscale_up[:].unsqueeze(1).to_broadcast([P, UT, D]), ALU.mult).then_inc(scaled_ready, 1)

            def at_least_normal(k):
                pool.wait_ge(exponent_ready, k + 1)
                stand_alone(pool, "pool")
                pool.tensor_scalar(buf_m[:], buf_m[:], LEAST_MAGIC, None, ALU.max).then_inc(magic_ready, 1)

            def rounded(k):
                pool.wait_ge(summed_ready, k + 1)
                if after(k, 1):
                    pool.wait_ge(q_turned, k)
                pool.tensor_tensor(q_rows[:].rearrange("p t d -> p (t d)"), buf_t[:], buf_m[:],
                                   ALU.subtract).then_inc(q_ready, 1)

            def add_rows(k):
                pool.wait_ge(ln_rows[3], k + 1)
                pool.tensor_tensor(unit(x_all, k), unit(x_all, k), unit(xn_all, k), ALU.add).then_inc(base_ready, 1)

            def low_relations(k):
                for b in range(UB):
                    pool.wait_ge(rel_high, UB * k + b + 1)
                    if after(k, 1):
                        pool.wait_ge(att_done, UB * k)
                    pool.tensor_tensor(rel_t[1][:, b], rel_32[:, b], rel_t[0][:, b].bitcast(F32),
                                       ALU.subtract).then_inc(rel_low, 1)

            at_least_normal(AHEAD - 1)
            rounded(AHEAD - 1)

            def phase_b(k, final=None):
                more = final is None or final + AHEAD < UNITS
                if more:
                    scale_up(k + AHEAD)
                if after(k, 2):
                    add_rows(k - 2)
                if more:
                    at_least_normal(k + AHEAD)
                low_relations(k)
                if more:
                    rounded(k + AHEAD)

            phase_b(0)
            phase_b(1)
            with pool.Fori(2, UNITS - AHEAD) as k:
                phase_b(k)
            for k in range(UNITS - AHEAD, UNITS):
                phase_b(k, final=k)
            add_rows(UNITS - 2)
            add_rows(UNITS - 1)

            pool.wait_ge(counted, 1)
            pool.partition_all_reduce(most[:], pos[:, TILES - 1:TILES], P, bass.bass_isa.ReduceOp.max).then_inc(most_ready, 1)
            pool.wait_ge(feats_step, 3)
            pool.memset(results, 0.0)
            pool.memset(result, 0.0)
            pool.memset(f_rows, 0.0).then_inc(zeroed, 1)

        @block.scalar
        def _(act):
            act.dma_start(adj_t[:], rows_of(adj_turned)).then_inc(adj_loaded, 16)
            act.dma_start(gnn_w_sb[:], rows_of(gnn_w)).then_inc(gnn_loaded, 16)
            act.dma_start(bias_bc, gnn_b.partition_broadcast(P)).then_inc(gnn_loaded, 16)

            def root(n, k, src=None):
                act.wait_ge(ln_moments[n], k + 1)
                act.activation(std[:, n], mv[:, :, 1], ACT.Sqrt, bias=eps[:, 0:1]).then_inc(ln_std[n], 1)

            def spread(n, k):
                act.wait_ge(ln_moments[n], k + 1)
                stand_alone(act, "act")
                for i in range(UT):
                    ins = act.activation(xn_all[:, UT * k + i, :], x_all[:, UT * k + i, :], ACT.Square,
                                         bias=nmean[:, i:i + 1], accum_out=squares[:, i:i + 1])
                ins.then_inc(ln_squares[n], 1)
                act.wait_ge(ln_squares[n], k + 1)
                act.activation(std[:, n], squares[:], ACT.Sqrt, scale=1.0 / D, bias=eps[:, 0:1]).then_inc(ln_std[n], 1)

            def scale_rows(n, k):
                act.wait_ge(ln_shift[n], k + 1)
                stand_alone(act, "act")
                for i in range(UT):
                    ins = act.activation(xn_all[:, UT * k + i, :], x_all[:, UT * k + i, :], ACT.Identity,
                                         scale=rstd[:, n, i:i + 1], bias=shift[:, n, i:i + 1])
                ins.then_inc(ln_rows[n], 1)

            act.wait_ge(consts_ready, 1)
            root(0, 0)

            def move_y(k, par, b):
                act.wait_ge(y_done, UB * k + b + 1)
                act.copy(y_t[par][:, b].rearrange("p e n -> p (e n)"), psum[:, Y[b], :]).then_inc(y_moved, 1)

            def phase_a(k, par, final=None):
                nxt2 = final is None or final + 2 < UNITS
                nxt3 = final is None or final + 3 < UNITS
                if final == UNITS - 1:
                    root(1, k)
                    return
                if nxt2:
                    move_y(k + 2, par, 0)
                spread(1, k)
                if nxt3:
                    root(0, k + 3)
                if nxt2:
                    move_y(k + 2, par, 1)
                scale_rows(1, k)

            root(0, 1)
            for b in range(UB):
                move_y(0, 0, b)
            root(0, 2)
            for b in range(UB):
                move_y(1, 1, b)
            act.wait_ge(wv_loaded, 16)
            act.copy(wv_t[0][:].rearrange("p e d -> p (e d)"), wv_raw).then_inc(weights_high, 1)
            phase_a(0, 0)
            with act.Fori(0, UNITS // 2 - 2) as j:
                phase_a(2 * j + 1, 1)
                phase_a(2 * j + 2, 0)
            for k in range(UNITS - 3, UNITS):
                phase_a(k, k % 2, final=k)

            act.wait_ge(prep_done, 1)
            act.copy(qk_w[0][:].rearrange("p e d -> p (e d)"), psum[:, PREP, :]).then_inc(weights_high, 1)

            def scale_up(k):
                if k:
                    act.wait_ge(exponent_ready, k)
                act.activation(buf_w[:], unit(xn_all, k).rearrange("p t d -> p (t d)"), ACT.Copy,
                               scale=fscale_up[:, 0:1]).then_inc(scaled_ready, 1)

            def rows_b(k):
                act.wait_ge(ln_shift[2], k)
                stand_alone(act, "act")
                for i in range(UT):
                    ins = act.activation(xn_b[:, i, :], x_all[:, UT * k + i, :], ACT.Identity,
                                         scale=rstd[:, 2, i:i + 1], bias=shift[:, 2, i:i + 1])
                ins.then_inc(ln_rows[2], 1)

            def move_q(k):
                act.wait_ge(q_turned, k + 1)
                act.copy(q_t[:].rearrange("p b e n -> p (b e n)"), psum[:, QT, :].bitcast(BF16)).then_inc(q_t_ready, 1)

            def move_xt(k):
                for b in range(UB):
                    act.wait_ge(xt_turned, UB * k + b + 1)
                    act.copy(xn_t[0][:, :, b, :], psum[:, XT[b], :].rearrange("p (e n) -> p e n", e=DT)).then_inc(xt_moved, 1)

            def move_qk(k, e):
                act.wait_ge(qk_done, DT * k + e + 1)
                act.copy(qk_t[0][:, e].rearrange("p b n -> p (b n)"), psum[:, QK[e], :]).then_inc(qk_moved, 1)

            def move_v(k, b):
                act.wait_ge(v_done, UB * k + b + 1)
                act.copy(v_sb[0][:, b].rearrange("p m d -> p (m d)"), psum[:, VB[b], :]).then_inc(v_moved, 1)

            def high_relations(k):
                for b in range(UB):
                    act.wait_ge(rel_masked, UB * k + b + 1)
                    act.copy(rel_t[0][:, b], rel_32[:, b]).then_inc(rel_high, 1)

            def square_relations(k, scaled_later):
                if scaled_later:
                    act.wait_ge(exponent_ready, k + AHEAD + 1)
                for b in range(UB):
                    act.activation(rel_sq[:, b], rel_32[:, b], ACT.Square).then_inc(sq_ready, 1)

            def root_norm(k):
                act.wait_ge(ss_done, k + 1)
                act.activation(std[:, 0], psum[:, SS, 0:UT], ACT.Sqrt).then_inc(norm_ready, 1)

            act.wait_ge(scales_ready, 1)
            scale_up(0)
            scale_up(1)
            move_q(0)
            scale_up(2)
            root(2, 0)
            move_xt(0)
            move_q(1)

            def phase_b(k, final=None):
                nxt = final is None or final + 1 < UNITS
                nxt2 = final is None or final + 2 < UNITS
                if nxt and after(k, 1):
                    rows_b(k + 1)
                move_qk(k, 0)
                move_qk(k, 1)
                if not after(k, 1):
                    root(2, k + 1)
                    rows_b(k + 1)
                if nxt2:
                    move_q(k + 2)
                if after(k, 1):
                    spread(3, k - 1)
                move_v(k, 0)
                high_relations(k)
                move_v(k, 1)
                if nxt:
                    move_xt(k + 1)
                square_relations(k, final is None or final + AHEAD < UNITS)
                if after(k, 1):
                    scale_rows(3, k - 1)
                if nxt2:
                    root(2, k + 2)
                root_norm(k)

            phase_b(0)
            with act.Fori(1, UNITS - AHEAD) as k:
                phase_b(k)
            for k in range(UNITS - AHEAD, UNITS):
                phase_b(k, final=k)
            root(3, UNITS - 1)

            act.wait_ge(mlp_loaded, 16)

            def relu(dst, src, bias, s):
                act.activation(dst, src, ACT.Relu, bias=bias).then_inc(s, 1)

            def high_layer(l):
                act.copy(mm_parts[l % 2][0], w_mm[:, l, :])
                act.copy(rm_parts[l % 2][0], w_rm[:, l]).then_inc(layer_high, 1)

            def mlp_block(j):
                if after(j, 1):
                    for l in (0, 1):
                        high_layer(l)
                for h in range(2):
                    act.wait_ge(f_turned, 2 * j + h + 1)
                    act.copy(f_t[:, h, :], psum[:, FT[h], :]).then_inc(f_t_ready, 1)
                for l in range(RELUS):
                    act.wait_ge(rem_done, RELUS * j + l + 1)
                    relu(hid_r[l % 2], psum[:, RB, :], b_rem[:, l:l + 1], hid_r_ready)
                    if l < HID:
                        act.wait_ge(hid_r_ready, RELUS * j + l + 1)
                        act.copy(hid_r_parts[l % 2][0], hid_r[l % 2]).then_inc(hid_r_high, 1)
                    for c in range(CHUNKS):
                        if c % 2 == 0:
                            act.wait_ge(main_done[c], RELUS * j + l + 1)
                            relu(hid[c], psum[:, MAIN[c], :], b_main[:, l:l + 1], hid_ready[c])
                        if l < HID:
                            act.wait_ge(hid_ready[c], RELUS * j + l + 1)
                            act.copy(hid_parts[c][0], hid[c]).then_inc(hid_high[c], 1)
                    if 1 <= l < HID - 1:
                        high_layer(l + 1)
                act.wait_ge(last_done, j + 1)
                act.activation(last_sb, psum[:, LAST, :], ACT.Identity, bias=b_out[:, 0:1]).then_inc(last_ready, 1)

            def move_part(g, which):
                act.wait_ge(part_turned, g + 1)
                if after(g, 2):
                    act.wait_ge(sent_back, g)
                act.copy(to_part_t[which].rearrange("p s q -> p (s q)"),
                         psum[:, TURN[0]:TURN[-1] + 1, :].rearrange("p b c -> p (b c)")).then_inc(part_moved, 1)

            for l in (0, 1):
                high_layer(l)
            act.wait_ge(place_step, 7)
            for h in range(2):
                some = range(h * GROUP // 2, (h + 1) * GROUP // 2)
                for i in some:
                    ins = act.activation(to_part[:, i, :], iota_p[:], ACT.Abs, scale=-1.0, bias=place[:, 0, i:i + 1])
                ins.then_inc(part_distance, 1)
                act.wait_ge(part_distance, h + 1)
                part = to_part[:, some[0]:some[-1] + 1]
                act.activation(part, part, ACT.Relu, scale=-1.0, bias=ones[:, 0:1]).then_inc(part_onehots, 1)
            move_part(0, 0)
            mlp_block(0)
            act.wait_ge(total_int, 1)
            total = act.value_load(total_i[0:1, 0:1])
            with act.If(SLOTS * P < total):
                with act.Fori(1, BLOCKS) as j:
                    with act.If(SLOTS * P * j < total):
                        mlp_block(j)
            act.wait_ge(most_int, 1)
            longest = act.value_load(most_i[0:1, 0:1])
            with act.If(GROUP < longest):
                with act.Fori(1, GROUPS) as g:
                    with act.If(GROUP * g < longest):
                        move_part(g, 1)

        @block.tensor
        def _(pe):
            pe.wait_ge(adj_loaded, 16)
            pe.wait_ge(gnn_loaded, 32)

            def y_part(k, par):
                pe.wait_ge(ln_rows[0], k + 1)
                for b in range(UB):
                    if after(k, 1):
                        pe.wait_ge(y_moved, UB * (k - 1) + b + 1)
                    for e in range(DT):
                        for m in range(NT):
                            mm = pe.matmul(psum[:, Y[b], e * N:(e + 1) * N],
                                           xn_a[par][:, b * NT + m, e * P:(e + 1) * P], adj_t[:, m, :],
                                           start=m == 0, stop=m == NT - 1)
                    mm.then_inc(y_done, 1)

            def gnn_part(k, par):
                for b in range(UB):
                    pe.wait_ge(y_moved, UB * k + b + 1)
                    if after(k, 1):
                        pe.wait_ge(x1_added, UB * (k - 1) + b + 1)
                    for h in range(NT):
                        for e in range(DT):
                            mm = pe.matmul(psum[:, G[b], h * D:(h + 1) * D],
                                           y_t[par][:, b, e, h * P:(h + 1) * P], gnn_w_sb[:, e, :],
                                           start=e == 0, stop=e == DT - 1)
                    mm.then_inc(gnn_done, 1)

            y_part(0, 0)
            y_part(1, 1)
            gnn_part(0, 0)
            with pe.Fori(1, UNITS // 2) as j:
                for par in range(2):
                    y_part(2 * j + par, par)
                    gnn_part(2 * j + par - 1, 1 - par)
            gnn_part(UNITS - 1, 1)

            pe.wait_ge(att_loaded, 48)
            for i in range(DT):
                for e in range(DT):
                    mm = pe.matmul(psum[:, PREP, i * D:(i + 1) * D], wq_sb[:, e, i * P:(i + 1) * P], wk_sb[:, e, :],
                                   start=e == 0, stop=e == DT - 1)
            mm.then_inc(prep_done, 1)

            def turn_q(k):
                pe.wait_ge(q_ready, k + 1)
                if after(k, 1):
                    pe.wait_ge(q_t_ready, k)
                bank = psum[:, QT, :].bitcast(BF16)
                for b in range(UB):
                    for e in range(DT):
                        for m in range(NT):
                            at = ((b * DT + e) * NT + m) * P
                            mm = pe.transpose(bank[:, at:at + P], q_rows[:, b * NT + m, e * P:(e + 1) * P], ident_bf[:])
                mm.then_inc(q_turned, 1)

            def ffn(k):
                pe.wait_ge(q_t_ready, k + 1)
                for b in range(UB):
                    if after(k, 2):
                        pe.wait_ge(xt_low, UB * (k - 2) + b + 1)
                    elif k == 1:
                        pe.wait_ge(xt_low, b + 1)
                    for h in range(NT):
                        for e in range(DT):
                            mm = pe.matmul(psum[:, FFN[b], h * D:(h + 1) * D], q_t[:, b, e, h * P:(h + 1) * P],
                                           ffn_wq[:, e, :], start=e == 0, stop=e == DT - 1)
                    mm.then_inc(ffn_done, 1)

            def turn_x(k, ffn_ahead=1):
                pe.wait_ge(ln_rows[2], k + 1)
                pe.wait_ge(x2_added, UB * (k + ffn_ahead + 1))
                for b in range(UB):
                    for e in range(DT):
                        for m in range(NT):
                            at = (e * NT + m) * P
                            mm = pe.transpose(psum[:, XT[b], at:at + P], xn_b[:, b * NT + m, e * P:(e + 1) * P], ident[:])
                    mm.then_inc(xt_turned, 1)

            def qk(k):
                if not after(k, 1):
                    pe.wait_ge(weights_low, 2)
                pe.wait_ge(xt_low, UB * (k + 1))
                for o in range(DT):
                    if after(k, 1):
                        pe.wait_ge(rel_masked, UB * (k - 1) + o + 1)
                    steps = [(e, w, x) for w, x in PRODUCTS for e in range(DT)]
                    for i, (e, w, x) in enumerate(steps):
                        mm = pe.matmul(psum[:, QK[o], :], qk_w[w][:, e, o * P:(o + 1) * P],
                                       xn_t[x][:, e].rearrange("p b n -> p (b n)"), start=i == 0, stop=i == len(steps) - 1)
                    mm.then_inc(qk_done, 1)

            def values(k, b):
                if after(k, 1):
                    pe.wait_ge(x3_added, UB * (k - 1) + b + 1)
                for m in range(NT):
                    steps = [(e, x, w) for x, w in PRODUCTS for e in range(DT)]
                    for i, (e, x, w) in enumerate(steps):
                        mm = pe.matmul(psum[:, VB[b], m * D:(m + 1) * D], xn_t[x][:, e, b, m * P:(m + 1) * P],
                                       wv_t[w][:, e, :], start=i == 0, stop=i == len(steps) - 1)
                mm.then_inc(v_done, 1)

            def relations(k):
                pe.wait_ge(qk_moved, DT * (k + 1))
                pe.wait_ge(qk_low, DT * (k + 1))
                for b in range(UB):
                    for m in range(NT):
                        steps = [(e, x, q) for x, q in PRODUCTS for e in range(DT)]
                        for i, (e, x, q) in enumerate(steps):
                            mm = pe.matmul(psum[:, REL[b], m * N:(m + 1) * N], xn_t[x][:, e, b, m * P:(m + 1) * P],
                                           qk_t[q][:, e, b, :], start=i == 0, stop=i == len(steps) - 1)
                    mm.then_inc(rel_done, 1)

            def attend(k):
                for b in range(UB):
                    pe.wait_ge(rel_high, UB * k + b + 1)
                    pe.wait_ge(v_low, UB * k + b + 1)
                    for h in range(NT):
                        steps = [(m, r, v) for r, v in PRODUCTS for m in range(NT)]
                        for i, (m, r, v) in enumerate(steps):
                            if h == 0 and r == 1 and m == 0:
                                pe.wait_ge(rel_low, UB * k + b + 1)
                            mm = pe.matmul(psum[:, ATT[b], h * D:(h + 1) * D], rel_t[r][:, b, m, h * P:(h + 1) * P],
                                           v_sb[v][:, b, m, :], start=i == 0, stop=i == len(steps) - 1)
                    mm.then_inc(att_done, 1)

            def sum_squares(k):
                pe.wait_ge(sq_ready, UB * (k + 1))
                if after(k, 1):
                    pe.wait_ge(norm_ready, k)
                for b in range(UB):
                    for h in range(NT):
                        for m in range(NT):
                            mm = pe.matmul(psum[:, SS, b * NT + h:b * NT + h + 1], rel_sq[:, b, m, h * P:(h + 1) * P],
                                           ones[:, 0:1], start=m == 0, stop=m == NT - 1)
                mm.then_inc(ss_done, 1)

            pe.wait_ge(ident_ready, 1)
            pe.wait_ge(consts_ready, 2)
            pe.wait_ge(x1_added, UB * UNITS)
            turn_q(0)
            pe.wait_ge(ffn_wq_ready, 1)
            ffn(0)
            turn_x(0, ffn_ahead=0)
            turn_q(1)
            ffn(1)

            def phase_b(k, final=None):
                nxt = final is None or final + 1 < UNITS
                nxt2 = final is None or final + 2 < UNITS
                qk(k)
                if nxt2:
                    turn_q(k + 2)
                values(k, 0)
                if nxt2:
                    ffn(k + 2)
                relations(k)
                values(k, 1)
                if nxt:
                    turn_x(k + 1, ffn_ahead=1 if nxt2 else 0)
                attend(k)
                sum_squares(k)

            phase_b(0)
            with pe.Fori(1, UNITS - 2) as k:
                phase_b(k)
            for k in (UNITS - 2, UNITS - 1):
                phase_b(k, final=k)

            pe.wait_ge(mlp_loaded, 16)

            def mlp_block(j):
                pe.wait_ge(f_ready, j + 1)
                for h in range(2):
                    for s in range(HALF):
                        mm = pe.transpose(psum[:, FT[h], s * P:(s + 1) * P], f_rows[:, h * HALF + s, :], ident[:])
                    mm.then_inc(f_turned, 1)
                for c in range(CHUNKS):
                    if c % 2 == 0:
                        pe.wait_ge(f_t_ready, 2 * j + c // 2 + 1)
                    pe.matmul(psum[:, MAIN[c], :], w_in_m[:, c % 2, :], f_t[:, c // 2, :],
                              start=True, stop=True).then_inc(main_done[c], 1)
                    if c == CHUNKS // 2:
                        for r in range(CHUNKS):
                            mm = pe.matmul(psum[REM * r:REM * (r + 1), RB, :], w_in_r[:, r % 2, :], f_t[:, r // 2, :],
                                           start=True, stop=True)
                        mm.then_inc(rem_done, 1)
                for l in range(1, HID + 1):
                    done = RELUS * j + l
                    split = HID * j + l

                    def from_high(c):
                        pe.wait_ge(hid_ready[c], done)
                        pe.wait_ge(hid_high[c], split)
                        for w in (0, 1):
                            pe.matmul(psum[:, MAIN[c], :], mm_parts[(l - 1) % 2][w], hid_parts[c][0],
                                      start=w == 0, stop=False)

                    def from_low(c):
                        pe.wait_ge(hid_low[c], split)
                        pe.matmul(psum[:, MAIN[c], :], mm_parts[(l - 1) % 2][0], hid_parts[c][1], start=False, stop=False)

                    pe.wait_ge(layer_high, split)
                    pe.wait_ge(layer_low, split)
                    from_high(0)
                    from_high(1)
                    pe.wait_ge(hid_r_ready, done)
                    for c in range(CHUNKS):
                        pe.wait_ge(hid_ready[c], done)
                    for c in range(CHUNKS):
                        pe.matmul(psum[REM * c:REM * (c + 1), RB, :], w_mr[:, l - 1, :], hid[c],
                                  start=True, stop=False, skip_group_check=True)
                    pe.matmul(psum[:, RB, :], w_rr[:, l - 1, :], hid_r[(l - 1) % 2], start=False, stop=True,
                              skip_group_check=True).then_inc(rem_done, 1)
                    for c in range(2, CHUNKS):
                        from_high(c)
                    for c in range(CHUNKS):
                        from_low(c)
                    pe.wait_ge(hid_r_low, split)
                    for c in range(CHUNKS):
                        for i, (w, x) in enumerate(PRODUCTS):
                            mm = pe.matmul(psum[:, MAIN[c], :], rm_parts[(l - 1) % 2][w][:, c, :],
                                           hid_r_parts[(l - 1) % 2][x], start=False, stop=i == len(PRODUCTS) - 1)
                        mm.then_inc(main_done[c], 1)
                for c in range(CHUNKS):
                    pe.wait_ge(hid_ready[c], RELUS * (j + 1))
                    pe.matmul(psum[REM * c:REM * (c + 1), LAST, :], w6_m[:], hid[c],
                              start=True, stop=False, skip_group_check=True)
                pe.wait_ge(hid_r_ready, RELUS * (j + 1))
                pe.matmul(psum[:, LAST, :], w6_r[:], hid_r[HID % 2], start=False, stop=True,
                          skip_group_check=True).then_inc(last_done, 1)
                pe.wait_ge(last_ready, j + 1)
                for s in range(HALF):
                    mm = pe.transpose(psum[:, FT[0], s * P:(s + 1) * P], last_sb[:, s * P:(s + 1) * P], ident[:])
                mm.then_inc(last_turned, 1)

            pe.wait_ge(counted, 1)
            counts = pos[:, TILES - 1:TILES]
            pe.matmul(psum[:, COUNTS, 0:1], before[:], counts, start=True, stop=True)
            pe.matmul(psum[0:TILES, COUNTS, 1:2], ones[:], counts, start=True, stop=True).then_inc(sums_done, 1)

            def send(g):
                pe.wait_ge(part_onehots, g + 2)
                if after(g, 1):
                    pe.wait_ge(parcels_in, g)
                for i in range(GROUP):
                    if i % (GROUP // 2) == 0:
                        pe.wait_ge(parcels_ready, 2 * g + i // (GROUP // 2) + 1)
                    mm = pe.matmul(psum[:, ARRIVE, 0:SENT * TILES], to_part[:, i, :],
                                   parcels[:, i].rearrange("p f t -> p (f t)"), start=i == 0, stop=i == GROUP - 1)
                mm.then_inc(parcels_sent, 1)

            def turn_part(g):
                if after(g, 1):
                    pe.wait_ge(back_onehots, 3 * g)
                    pe.wait_ge(part_moved, g)
                per = CW // P
                for i in range(GROUP):
                    if not after(g, 1) and i % (GROUP // 2) == 0:
                        pe.wait_ge(part_onehots, 1 + i // (GROUP // 2))
                    mm = pe.transpose(psum[:, TURN[i // per], i % per * P:(i % per + 1) * P], to_part[:, i, :], ident[:])
                mm.then_inc(part_turned, 1)

            def send_back(g, which):
                pe.wait_ge(part_moved, g + 1)
                if after(g, 1):
                    pe.wait_ge(back_step, 5 * g)
                per = CW // TILES
                for i in range(GROUP):
                    mm = pe.matmul(psum[:, BACK[i // per], i % per * TILES:(i % per + 1) * TILES],
                                   to_part_t[which][:, i, :], results, start=True, stop=True)
                mm.then_inc(sent_back, 1)

            turn_part(0)
            send(0)
            pe.wait_ge(most_int, 1)
            longest = pe.value_load(most_i[0:1, 0:1])
            with pe.If(GROUP < longest):
                with pe.Fori(1, GROUPS) as g:
                    with pe.If(GROUP * g < longest):
                        send(g)
            pe.wait_ge(part_moved, 1)
            mlp_block(0)
            pe.wait_ge(total_int, 1)
            total = pe.value_load(total_i[0:1, 0:1])
            with pe.If(SLOTS * P < total):
                with pe.Fori(1, BLOCKS) as j:
                    with pe.If(SLOTS * P * j < total):
                        mlp_block(j)
            pe.wait_ge(all_results, 1)
            send_back(0, 0)
            with pe.If(GROUP < longest):
                with pe.Fori(1, GROUPS) as g:
                    with pe.If(GROUP * g < longest):
                        turn_part(g)
                        send_back(g, 1)

        @block.vector
        def _(dve):
            def statistics(n, k):
                stand_alone(dve, "dve")
                for i in range(UT):
                    ins = dve.bn_stats(stats[:, i], tile_of(x_all, k, i))
                ins.then_inc(ln_stats[n], 1)

            def aggregate(n, k):
                dve.wait_ge(ln_stats[n], k + 1)
                stand_alone(dve, "dve")
                for i in range(UT):
                    ins = dve.bn_aggr(mv[:, i], stats[:, i])
                ins.then_inc(ln_moments[n], 1)

            def moments(n, k, nth=None):
                statistics(n, k)
                aggregate(n, k if nth is None else nth)

            def tile_of(buf, k, i):
                return buf[:, UT * k + i, :]

            def normalise(n, k, dst):
                dve.wait_ge(ln_std[n], k + 1)
                dve.reciprocal(rstd[:, n], std[:, n]).then_inc(ln_rstd[n], 1)
                dve.wait_ge(ln_rstd[n], k + 1)
                for i in range(UT):
                    ins = dve.tensor_scalar(dst(i), tile_of(x_all, k, i), mv[:, i, 0:1], rstd[:, n, i:i + 1],
                                            ALU.subtract, ALU.mult)
                ins.then_inc(ln_rows[n], 1)

            def mean(n, k):
                dve.tensor_scalar(nmean[:], sums[:], -1.0 / D, None, ALU.mult).then_inc(ln_moments[n], 1)

            def scale_and_shift(n, k):
                dve.wait_ge(ln_std[n], k + 1)
                if after(k, 1):
                    dve.wait_ge(ln_rows[n], k)
                dve.reciprocal(rstd[:, n], std[:, n]).then_inc(ln_rstd[n], 1)
                dve.wait_ge(ln_rstd[n], k + 1)
                if n == 2:
                    dve.scalar_tensor_tensor(out=shift[:, n], in0=mv[:, :, 0], scalar=-1.0, in1=rstd[:, n],
                                             op0=ALU.mult, op1=ALU.mult).then_inc(ln_shift[n], 1)
                else:
                    dve.tensor_tensor(shift[:, n], nmean[:], rstd[:, n], ALU.mult).then_inc(ln_shift[n], 1)

            def low(dst, src, high, s=None):
                ins = dve.tensor_tensor(dst, src, high.bitcast(F32), ALU.subtract)
                if s is not None:
                    ins.then_inc(s, 1)

            def exponents(m, w):
                return dve.tensor_scalar(m.bitcast(I32), w.bitcast(I32), EXPONENT_BITS, HALF_BIT,
                                         ALU.bitwise_and, ALU.bitwise_or)

            def at_least(m):
                return dve.tensor_scalar(m, m, LEAST_MAGIC, None, ALU.max)

            w_flat = ffn_w_sb[:].rearrange("p e d -> p (e d)")
            wa, wb = buf_n[:, 0:DT * D], buf_n[:, DT * D:2 * DT * D]

            def weight_scale():
                dve.wait_ge(amax_ready, 1)
                dve.wait_ge(consts_ready, 3)
                dve.tensor_scalar(amax[:, 1:2], amax[:, 1:2], AMAX_FLOOR, None, ALU.max).then_inc(wq_step, 1)
                dve.wait_ge(wq_step, 1)
                dve.reciprocal(finv[:, 1:2], amax[:, 1:2]).then_inc(wq_step, 1)
                dve.wait_ge(wq_step, 2)
                dve.tensor_scalar(fscale[:, 1:2], finv[:, 1:2], FP8_MAX, None, ALU.mult).then_inc(wq_step, 1)

            def weight_exponents():
                dve.wait_ge(wq_step, 3)
                dve.tensor_scalar(wa, w_flat, fscale[:, 1:2], MAGIC_SHIFT, ALU.mult, ALU.mult).then_inc(wq_step, 1)
                dve.wait_ge(wq_step, 4)
                exponents(wb, wa).then_inc(wq_step, 1)

            def weight_rounded():
                dve.wait_ge(wq_step, 5)
                at_least(wb).then_inc(wq_step, 1)
                dve.wait_ge(wq_step, 6)
                dve.scalar_tensor_tensor(out=wa, in0=w_flat, scalar=fscale[:, 1:2], in1=wb,
                                         op0=ALU.mult, op1=ALU.add).then_inc(wq_step, 1)
                dve.wait_ge(wq_step, 7)
                dve.tensor_tensor(ffn_wq[:].rearrange("p e d -> p (e d)"), wa, wb, ALU.subtract).then_inc(ffn_wq_ready, 1)

            def first_norm(k, par, j):
                dve.wait_ge(x_loaded[par], 16 * (j + 1))
                moments(0, k)

            def first_rows(k, par):
                if after(k, 2):
                    dve.wait_ge(y_done, UB * (k - 1))
                normalise(0, k, lambda i: xn_a[par][:, i, :])

            def add_gnn(k):
                dve.wait_ge(bias_added, k + 1)
                for b in range(UB):
                    dve.wait_ge(gnn_done, UB * k + b + 1)
                    for h in range(NT):
                        i = b * NT + h
                        ins = dve.scalar_tensor_tensor(
                            out=tile_of(x_all, k, i), in0=psum[:, G[b], h * D:(h + 1) * D], scalar=1.0,
                            in1=tile_of(x_all, k, i), op0=ALU.mult, op1=ALU.add, accum_out=sums[:, i:i + 1])
                    ins.then_inc(x1_added, 1)
                dve.wait_ge(x1_added, UB * (k + 1))

            def see_amax(k):
                dve.wait_ge(ln_rows[1], k + 1)
                dve.tensor_reduce(column(amax_u, k), unit(xn_all, k).rearrange("p t d -> p (t d)"), AX.X, ALU.max,
                                  apply_absolute_value=True).then_inc(amax_seen, 1)

            def phase_a(k, par, j3, final=None):
                nxt3 = final is None or final + 3 < UNITS
                add_gnn(k)
                if final == UNITS - 1:
                    moments(1, k, nth=0)
                    see_amax(k - 1)
                    normalise(1, k, lambda i: xn_all[:, UT * k + i, :])
                    return
                mean(1, k)
                if nxt3:
                    first_norm(k + 3, 1 - par, j3)
                if after(k, 1):
                    see_amax(k - 1)
                scale_and_shift(1, k)
                if nxt3:
                    first_rows(k + 3, 1 - par)

            for k in range(3):
                first_norm(k, k % 2, k // 2)
                first_rows(k, k % 2)
                if k == 1:
                    dve.wait_ge(ffn_loaded, 16)
                    dve.tensor_reduce(amax_p[:, 1:2], ffn_w_sb[:].rearrange("p e d -> p (e d)"), AX.X, ALU.max,
                                      apply_absolute_value=True).then_inc(amax_parts, 1)
            dve.wait_ge(weights_high, 1)
            low(wv_t[1][:].rearrange("p e d -> p (e d)"), wv_raw, wv_t[0][:].rearrange("p e d -> p (e d)"), weights_low)
            phase_a(0, 0, 1)
            with dve.Fori(0, UNITS // 2 - 2) as j:
                phase_a(2 * j + 1, 1, j + 2)
                phase_a(2 * j + 2, 0, j + 2)
            for k in range(UNITS - 3, UNITS):
                phase_a(k, k % 2, 0, final=k)
            see_amax(UNITS - 1)

            dve.wait_ge(amax_seen, UNITS)
            dve.tensor_reduce(amax_p[:, 0:1], amax_u[:], AX.X, ALU.max).then_inc(amax_parts, 1)
            weight_scale()
            dve.wait_ge(amax_ready, 2)
            dve.tensor_scalar(amax[:, 0:1], amax[:, 0:1], AMAX_FLOOR, None, ALU.max).then_inc(scale_step, 1)
            dve.wait_ge(scale_step, 1)
            dve.reciprocal(finv[:, 0:1], amax[:, 0:1]).then_inc(scale_step, 1)
            dve.wait_ge(scale_step, 2)
            dve.tensor_scalar(fscale[:, 0:1], finv[:, 0:1], FP8_MAX, None, ALU.mult).then_inc(scale_step, 1)
            dve.wait_ge(scale_step, 3)
            dve.tensor_scalar(fscale_up[:], fscale[:, 0:1], MAGIC_SHIFT, None, ALU.mult).then_inc(scales_ready, 1)
            dve.wait_ge(wq_step, 3)
            dve.reciprocal(finv[:], fscale[:]).then_inc(scale_step, 1)
            dve.wait_ge(scale_step, 4)
            dve.tensor_tensor(fout[:], finv[:, 0:1], finv[:, 1:2], ALU.mult).then_inc(scale_step, 1)

            def take_exponents(k):
                dve.wait_ge(scaled_ready, k + 1)
                if after(k, 1):
                    dve.wait_ge(q_ready, k)
                exponents(buf_m[:], buf_w[:]).then_inc(exponent_ready, 1)

            def add_magic(k):
                dve.wait_ge(magic_ready, k + 1)
                dve.scalar_tensor_tensor(out=buf_t[:], in0=unit(xn_all, k).rearrange("p t d -> p (t d)"),
                                         scalar=fscale[:, 0:1], in1=buf_m[:],
                                         op0=ALU.mult, op1=ALU.add).then_inc(summed_ready, 1)

            weight_exponents()

            def first_magic(k):
                take_exponents(k)
                dve.wait_ge(exponent_ready, k + 1)
                at_least(buf_m[:]).then_inc(magic_ready, 1)

            def first_rounded(k):
                add_magic(k)
                dve.wait_ge(summed_ready, k + 1)
                if k:
                    dve.wait_ge(q_turned, k)
                dve.tensor_tensor(q_rows[:].rearrange("p t d -> p (t d)"), buf_t[:], buf_m[:], ALU.subtract).then_inc(q_ready, 1)

            first_magic(0)
            first_rounded(0)
            weight_rounded()
            first_magic(1)

            def add_ffn(k):
                for b in range(UB):
                    dve.wait_ge(ffn_done, UB * k + b + 1)
                    dve.scalar_tensor_tensor(out=half(x_all, k, b), in0=psum[:, FFN[b], :].rearrange("p (h d) -> p h d", h=NT),
                                             scalar=fout[:, 0:1], in1=half(x_all, k, b),
                                             op0=ALU.mult, op1=ALU.add).then_inc(x2_added, 1)
                dve.wait_ge(x2_added, UB * (k + 1))

            def mask_relations(k, b):
                if after(k, 1):
                    dve.wait_ge(sq_ready, UB * k)
                    dve.wait_ge(rel_low, UB * k)
                dve.wait_ge(rel_done, UB * k + b + 1)
                dve.tensor_tensor(rel_32[:, b], psum[:, REL[b], :].rearrange("p (m n) -> p m n", m=NT), adj_nat[:],
                                  ALU.mult).then_inc(rel_masked, 1)

            def add_att(k):
                dve.wait_ge(norm_ready, k + 1)
                dve.reciprocal(rstd[:, 0], std[:, 0]).then_inc(inv_ready, 1)
                dve.wait_ge(inv_ready, k + 1)
                for b in range(UB):
                    for h in range(NT):
                        i = b * NT + h
                        ins = dve.scalar_tensor_tensor(
                            out=tile_of(x_all, k, i), in0=psum[:, ATT[b], h * D:(h + 1) * D],
                            scalar=rstd[:, 0, i:i + 1], in1=tile_of(x_all, k, i), op0=ALU.mult, op1=ALU.add,
                            accum_out=sums[:, i:i + 1])
                    ins.then_inc(x3_added, 1)
                dve.wait_ge(x3_added, UB * (k + 1))

            def hits(k):
                dve.wait_ge(ln_rows[3], k + 1)
                if after(k, 1):
                    dve.wait_ge(codes_ready, k)
                dve.scalar_tensor_tensor(
                    out=hit, in0=unit(xn_all, k)[:, :, NIBBLES_COL:NIBBLES_COL + NIBBLES * NIB], scalar=0.5,
                    in1=iota_down[:].unsqueeze(1).to_broadcast([P, UT, NIBBLES * NIB]),
                    op0=ALU.is_gt, op1=ALU.mult).then_inc(hits_ready, 1)

            def first_hits(k):
                dve.wait_ge(hits_ready, k + 1)
                dve.tensor_reduce(unit(code, k), hit.rearrange("p t (g i) -> p t g i", g=NIBBLES),
                                  AX.X, ALU.max).then_inc(codes_ready, 1)

            def nibbles(k):
                hits(k)
                first_hits(k)

            def finish(k):
                add_att(k)
                mean(3, k)

            def low_xt(k):
                for b in range(UB):
                    dve.wait_ge(xt_moved, UB * k + b + 1)
                    low(xn_t[1][:, :, b, :], psum[:, XT[b], :].rearrange("p (e n) -> p e n", e=DT), xn_t[0][:, :, b, :], xt_low)

            def low_qk(k, e):
                dve.wait_ge(qk_moved, DT * k + e + 1)
                low(qk_t[1][:, e].rearrange("p b n -> p (b n)"), psum[:, QK[e], :],
                    qk_t[0][:, e].rearrange("p b n -> p (b n)"), qk_low)

            def low_v(k, b):
                dve.wait_ge(v_moved, UB * k + b + 1)
                low(v_sb[1][:, b].rearrange("p m d -> p (m d)"), psum[:, VB[b], :],
                    v_sb[0][:, b].rearrange("p m d -> p (m d)"), v_low)

            dve.wait_ge(scale_step, 5)
            add_ffn(0)
            moments(2, 0)
            normalise(2, 0, lambda i: xn_b[:, i, :])
            dve.wait_ge(weights_high, 2)
            low(qk_w[1][:].rearrange("p e d -> p (e d)"), psum[:, PREP, :], qk_w[0][:].rearrange("p e d -> p (e d)"), weights_low)
            first_rounded(1)
            low_xt(0)
            take_exponents(2)
            add_ffn(1)
            moments(2, 1)
            add_magic(2)
            scale_and_shift(2, 1)

            def phase_b(k, final=None):
                nxt = final is None or final + 1 < UNITS
                nxt2 = final is None or final + 2 < UNITS
                more = final is None or final + AHEAD < UNITS
                if after(k, 1):
                    finish(k - 1)
                low_qk(k, 0)
                low_qk(k, 1)
                if more:
                    take_exponents(k + AHEAD)
                if nxt2:
                    add_ffn(k + 2)
                mask_relations(k, 0)
                if after(k, 1):
                    scale_and_shift(3, k - 1)
                low_v(k, 0)
                mask_relations(k, 1)
                if more:
                    add_magic(k + AHEAD)
                low_v(k, 1)
                if nxt:
                    low_xt(k + 1)
                if nxt2:
                    statistics(2, k + 2)
                if after(k, 2):
                    hits(k - 2)
                if nxt2:
                    aggregate(2, k + 2)
                if after(k, 2):
                    first_hits(k - 2)
                if nxt2:
                    scale_and_shift(2, k + 2)

            for k in range(2):
                phase_b(k)
            with dve.Fori(2, UNITS - AHEAD) as k:
                phase_b(k)
            for k in range(UNITS - AHEAD, UNITS):
                phase_b(k, final=k)
            add_att(UNITS - 1)
            moments(3, UNITS - 1, nth=0)
            nibbles(UNITS - 2)
            normalise(3, UNITS - 1, lambda i: xn_all[:, UT * (UNITS - 1) + i, :])
            nibbles(UNITS - 1)

            def xn_col(c):
                return xn_all[:, :, c]

            dve.tensor_scalar(mask[:, 0], xn_col(MUL_COL), 0.5, None, ALU.is_ge).then_inc(mask_step, 1)
            dve.wait_ge(mask_step, 1)
            dve.scalar_tensor_tensor(out=mask[:, 1], in0=xn_col(MARK_COL), scalar=0.5, in1=mask[:, 0],
                                     op0=ALU.is_ge, op1=ALU.mult).then_inc(mask_step, 1)
            dve.wait_ge(mask_step, 2)
            dve.tensor_tensor_scan(pos, ones[:], mask[:, 1], 0.0, ALU.mult, ALU.add).then_inc(counted, 1)
            dve.wait_ge(counted, 1)
            dve.tensor_tensor(slot_of, pos, mask[:, 1], ALU.mult).then_inc(slots_step, 1)
            dve.wait_ge(codes_ready, UNITS)
            by_tile = feats[:, 0:NIBBLES, :].rearrange("p f t -> p t f")
            dve.tensor_scalar(by_tile, code, -1.0, float(NIB), ALU.mult, ALU.add).then_inc(feats_step, 1)
            dve.wait_ge(feats_step, 1)
            dve.scalar_tensor_tensor(out=by_tile, in0=code, scalar=0.0, in1=by_tile,
                                     op0=ALU.is_gt, op1=ALU.mult).then_inc(feats_step, 1)
            dve.tensor_copy(sent_of[:, 1, :], xn_col(OPCODE_COL)).then_inc(feats_step, 1)
            dve.wait_ge(feats_step, 2)
            dve.tensor_tensor(by_tile, by_tile, places[:].unsqueeze(1).to_broadcast([P, TILES, NIBBLES]),
                              ALU.mult).then_inc(feats_step, 1)
            dve.wait_ge(feats_step, 4)
            dve.tensor_reduce(sent_of[:, 0, :], by_tile, AX.X, ALU.add).then_inc(feats_step, 1)
            dve.wait_ge(sums_done, 1)
            dve.tensor_copy(total_i[:], psum[0:1, COUNTS, 1:2]).then_inc(total_int, 1)
            dve.tensor_copy(packed[:, 0:1], psum[:, COUNTS, 0:1]).then_inc(place_step, 1)
            dve.tensor_scalar(used, iota_slot, pos[:, TILES - 1:TILES], None, ALU.is_le).then_inc(place_step, 1)
            dve.wait_ge(place_step, 1)
            dve.tensor_scalar(place_i[:, 0], iota_slot, packed[:, 0:1], -1.0, ALU.add, ALU.add).then_inc(place_step, 1)
            dve.wait_ge(place_step, 3)
            dve.tensor_scalar(place_i[:, 1], place_i[:, 0], P.bit_length() - 1, None,
                              ALU.logical_shift_right).then_inc(place_step, 1)
            dve.wait_ge(place_step, 4)
            dve.tensor_scalar(place_i[:, 0], place_i[:, 0], P - 1, None, ALU.bitwise_and).then_inc(place_step, 1)
            dve.wait_ge(place_step, 5)
            dve.tensor_scalar(place, place_i, 1.0, None, ALU.add).then_inc(place_step, 1)
            dve.wait_ge(place_step, 6)
            dve.tensor_tensor(place[:, 0], place[:, 0], used, ALU.mult).then_inc(place_step, 1)
            dve.wait_ge(slots_step, 1)
            dve.wait_ge(feats_step, 5)
            dve.wait_ge(place_step, 7)

            def group(row, g):
                return row[:, bass.ds(GROUP * g, GROUP)] if not isinstance(g, int) else row[:, GROUP * g:GROUP * (g + 1)]

            def equal(out, slot_values, values):
                return dve.tensor_tensor(out, slot_values.unsqueeze(2).to_broadcast(out.shape),
                                         values.unsqueeze(1).to_broadcast(out.shape), ALU.is_equal)

            def send(g, which):
                if after(g, 1):
                    dve.wait_ge(pick_step, 3 * g)
                    dve.wait_ge(parcels_ready, 2 * g)
                equal(sel[which], group(iota_slot, g), slot_of).then_inc(pick_step, 1)
                dve.wait_ge(pick_step, 3 * g + 1)
                if after(g, 1):
                    dve.wait_ge(parcels_sent, g)
                dve.tensor_tensor(parcels, sel[which].unsqueeze(2).to_broadcast([P, GROUP, SENT, TILES]),
                                  sent_of.unsqueeze(1).to_broadcast([P, GROUP, SENT, TILES]), ALU.mult).then_inc(pick_step, 1)
                dve.wait_ge(pick_step, 3 * g + 2)
                dve.tensor_reduce(sent, parcels, AX.X, ALU.add).then_inc(pick_step, 1)
                equal(to_tile[which], group(place[:, 1], g), iota_slot).then_inc(onehots, 1)
                if after(g, 1):
                    dve.wait_ge(part_turned, 1)
                    equal(to_part, group(place[:, 0], g), iota_p[:]).then_inc(part_onehots, 1)
                dve.wait_ge(pick_step, 3 * g + 3)
                dve.wait_ge(onehots, g + 1)
                for h in range(2):
                    some = slice(h * GROUP // 2, (h + 1) * GROUP // 2)
                    shape = [P, GROUP // 2, SENT, TILES]
                    dve.tensor_tensor(parcels[:, some], to_tile[which][:, some].unsqueeze(2).to_broadcast(shape),
                                      sent[:, some].unsqueeze(3).to_broadcast(shape), ALU.mult).then_inc(parcels_ready, 1)

            def take_in(g):
                dve.wait_ge(parcels_sent, g + 1)
                came = psum[:, ARRIVE, 0:SENT * TILES].rearrange("p (f t) -> p f t", f=SENT)
                if after(g, 1):
                    dve.wait_ge(parcels_in, g)
                    dve.tensor_tensor(arrived, came, arrived, ALU.add).then_inc(parcels_in, 1)
                else:
                    dve.tensor_copy(arrived, came).then_inc(parcels_in, 1)

            def low_layer(l, nth):
                dve.wait_ge(layer_high, nth)
                low(mm_parts[l % 2][1], w_mm[:, l, :], mm_parts[l % 2][0])
                low(rm_parts[l % 2][1], w_rm[:, l], rm_parts[l % 2][0], layer_low)

            send(0, 0)
            dve.wait_ge(most_ready, 1)
            dve.tensor_copy(most_i[:], most[:]).then_inc(most_int, 1)
            for l in (0, 1):
                low_layer(l, l + 1)
            take_in(0)
            dve.wait_ge(most_int, 1)
            longest = dve.value_load(most_i[0:1, 0:1])
            with dve.If(GROUP < longest):
                with dve.Fori(1, GROUPS) as g:
                    with dve.If(GROUP * g < longest):
                        send(g, 1)
                        take_in(g)
            dve.drain().then_inc(all_arrived, 1)
            dve.wait_ge(all_arrived, 1)
            dve.tensor_copy(nibbles_i[:, NIBBLES], arrived[:, 0]).then_inc(unpack_step, 1)
            dve.wait_ge(unpack_step, 1)
            for f in range(NIBBLES):
                dve.tensor_scalar(nibbles_i[:, f], nibbles_i[:, NIBBLES], (NIB.bit_length() - 1) * f, NIB - 1,
                                  ALU.logical_shift_right, ALU.bitwise_and).then_inc(unpack_step, 1)
            dve.tensor_copy(rows_f[:, NIBBLES], arrived[:, 1]).then_inc(unpack_step, 1)
            dve.wait_ge(unpack_step, 1 + NIBBLES)
            dve.tensor_copy(rows_f[:, 0:NIBBLES], nibbles_i[:, 0:NIBBLES]).then_inc(unpack_step, 1)
            dve.wait_ge(unpack_step, 3 + NIBBLES)
            dve.wait_ge(zeroed, 1)
            dve.wait_ge(mlp_loaded, 16)

            def mlp_block(j):
                if after(j, 1):
                    dve.wait_ge(f_turned, 2 * j)
                dve.tensor_copy(f_rows[:, :, 0:NF], block_of(rows_f, j).rearrange("p f s -> p s f")).then_inc(f_ready, 1)
                if after(j, 1):
                    for l in (0, 1):
                        low_layer(l, HID * j + l + 1)
                for l in range(RELUS):
                    if l < HID:
                        dve.wait_ge(hid_r_high, HID * j + l + 1)
                        low(hid_r_parts[l % 2][1], hid_r[l % 2], hid_r_parts[l % 2][0], hid_r_low)

                    def low_hid(c):
                        dve.wait_ge(hid_ready[c], RELUS * j + l + 1)
                        dve.wait_ge(hid_high[c], HID * j + l + 1)
                        low(hid_parts[c][1], hid[c], hid_parts[c][0], hid_low[c])

                    for c in range(1, CHUNKS, 2):
                        dve.wait_ge(main_done[c], RELUS * j + l + 1)
                        dve.tensor_scalar(hid[c], psum[:, MAIN[c], :], b_main[:, l:l + 1], 0.0,
                                          ALU.add, ALU.max).then_inc(hid_ready[c], 1)
                        if c == 1 and l < HID:
                            low_hid(0)
                    if l < HID:
                        for c in range(1, CHUNKS):
                            low_hid(c)
                    if 1 <= l < HID - 1:
                        low_layer(l + 1, HID * j + l + 2)
                dve.wait_ge(last_turned, j + 1)
                got = psum[:, FT[0], :].rearrange("p (s c r) -> p s c r", c=CHUNKS, r=REM)[:, :, :, 0]
                into = found[:].rearrange("p a (h s) -> p s h a", h=2)
                for a in range(N_POS_USED):
                    ins = dve.tensor_scalar(into[:, :, :, a], got[:, :, a:CHUNKS:N_POS_USED], 0.0, float(NIB - 1), ALU.max, ALU.min)
                ins.then_inc(clip_step, 1)
                dve.wait_ge(clip_step, 4 * j + 1)
                dve.tensor_scalar(found[:], found[:], INT_MAGIC, INT_MAGIC, ALU.add, ALU.subtract).then_inc(clip_step, 1)
                dve.wait_ge(clip_step, 4 * j + 2)
                dve.scalar_tensor_tensor(out=packed[:], in0=found[:, 1], scalar=float(NIB), in1=found[:, 0],
                                         op0=ALU.mult, op1=ALU.add).then_inc(clip_step, 1)
                dve.wait_ge(clip_step, 4 * j + 3)
                into = results[:, bass.ds(SLOTS * j, SLOTS)] if not isinstance(j, int) else results[:, 0:SLOTS]
                dve.tensor_scalar(into, packed[:], 1.0, None, ALU.add).then_inc(clip_step, 1)

            mlp_block(0)
            dve.wait_ge(total_int, 1)
            total = dve.value_load(total_i[0:1, 0:1])
            with dve.If(SLOTS * P < total):
                with dve.Fori(1, BLOCKS) as j:
                    with dve.If(SLOTS * P * j < total):
                        mlp_block(j)
            dve.drain().then_inc(all_results, 1)

            def take_back(g, which):
                if after(g, 1):
                    dve.wait_ge(back_step, 5 * g)
                    dve.wait_ge(part_turned, g)
                    equal(sel[which], group(iota_slot, g), slot_of).then_inc(back_onehots, 1)
                    equal(to_tile[which], group(place[:, 1], g), iota_slot).then_inc(back_onehots, 1)
                    equal(to_part, group(place[:, 0], g), iota_p[:]).then_inc(back_onehots, 1)
                dve.wait_ge(sent_back, g + 1)
                came = psum[:, BACK[0]:BACK[-1] + 1, :].rearrange("p b (s t) -> p (b s) t", t=TILES)
                prod_s = prod.rearrange("p (s t) -> p s t", s=GROUP)
                if after(g, 1):
                    dve.wait_ge(back_onehots, 3 * g)
                dve.tensor_tensor(prod_s, came, to_tile[which], ALU.mult).then_inc(back_step, 1)
                dve.wait_ge(back_step, 5 * g + 1)
                dve.tensor_reduce(got_back.unsqueeze(2), prod_s, AX.X, ALU.add).then_inc(back_step, 1)
                dve.wait_ge(back_step, 5 * g + 2)
                prod_t = prod.rearrange("p (t s) -> p t s", s=GROUP)
                dve.tensor_tensor(prod_t, sel[which].rearrange("p s t -> p t s"),
                                  got_back.unsqueeze(1).to_broadcast([P, TILES, GROUP]), ALU.mult).then_inc(back_step, 1)
                dve.wait_ge(back_step, 5 * g + 3)
                dve.tensor_reduce(back_sum.unsqueeze(2), prod_t, AX.X, ALU.add).then_inc(back_step, 1)
                dve.wait_ge(back_step, 5 * g + 4)
                dve.tensor_tensor(result, result, back_sum, ALU.add).then_inc(back_step, 1)

            take_back(0, 0)
            with dve.If(GROUP < longest):
                with dve.Fori(1, GROUPS) as g:
                    with dve.If(GROUP * g < longest):
                        take_back(g, 1)
            dve.drain().then_inc(all_back, 1)
            dve.wait_ge(all_back, 1)
            dve.tensor_scalar(digit_i[:, 2], result, -1.0, None, ALU.add).then_inc(digit_step, 1)
            dve.wait_ge(digit_step, 1)
            dve.tensor_scalar(digit_i[:, 0], digit_i[:, 2], SIGN_BIT | (NIB - 1), None, ALU.bitwise_and).then_inc(digit_step, 1)
            dve.tensor_scalar(digit_i[:, 1], digit_i[:, 2], NIB.bit_length() - 1, None,
                              ALU.logical_shift_right).then_inc(digit_step, 1)
            dve.wait_ge(digit_step, 3)
            dve.tensor_scalar(digit, digit_i[:, 0:N_POS_USED].rearrange("p a t -> p t a"), 1.0, None,
                              ALU.add).then_inc(digit_step, 1)
            dve.wait_ge(digit_step, 4)
            dve.wait_ge(base_ready, UNITS)
            for h in range(PIECES):
                some = slice(h * TILES // PIECES, (h + 1) * TILES // PIECES)
                shape = [P, TILES // PIECES, N_POS_USED, NIB]
                marks = onehot.rearrange("p (t c) -> p t c", t=TILES)[:, some]
                dve.tensor_tensor(marks.rearrange("p t (a i) -> p t a i", a=N_POS_USED),
                                  digit[:, some].unsqueeze(3).to_broadcast(shape),
                                  iota_up[:].unsqueeze(1).unsqueeze(1).to_broadcast(shape), ALU.is_equal).then_inc(final_step, 1)
                dve.wait_ge(final_step, h + 1)
                cols = x_all[:, some, OUTPUT_COL:OUTPUT_COL + OUTPUT_W]
                dve.scalar_tensor_tensor(out=cols, in0=marks, scalar=2.0, in1=cols,
                                         op0=ALU.mult, op1=ALU.add).then_inc(final_ready, 1)


def lay_out_mlp(w, b):
    import numpy as np

    layers, ge, _ = w.shape
    rem, hid = ge - P, layers - 2
    chunks = P // rem
    at, width = mlp_columns(layers, ge)
    laid = np.zeros((P, width), w.dtype)
    sq = laid[:, at["sq"]].reshape(P, hid, 2 * P + rem)
    rm = laid[:, at["rm"]].reshape(P, hid, chunks, P)
    turned = w.transpose(2, 0, 1)[:, 1:1 + hid]
    sq[:, :, 0:P] = turned[0:P, :, 0:P]
    sq[:, :, 2 * P:] = turned[0:P, :, P:]
    for c in range(chunks):
        quadrant = slice(rem * c, rem * (c + 1))
        sq[quadrant, :, P + rem * c:P + rem * (c + 1)] = turned[P:, :, P:]
        rm[quadrant, :, c, :] = turned[P:, :, 0:P]
        laid[quadrant, at["out_r"].start + rem * c] = w[-1, GE_RESULT, P:]
        laid[quadrant, at["b_rem"]] = b[:, P:].T
    laid[:, at["sq"]] = sq.reshape(P, -1)
    laid[:, at["rm"]] = rm.reshape(P, -1)
    start = at["in"].start
    for a in range(N_POS_USED):
        for row, col in ((a, GE_A), (N_POS_USED + a, GE_B), (NIBBLES, GE_OP)):
            laid[row, start + a * P:start + (a + 1) * P] = w[0, 0:P, col]
            left = start + N_POS_USED * P + a * rem
            laid[row, left:left + rem] = w[0, P:, col]
    laid[:, at["out_m"].start] = w[-1, GE_RESULT, 0:P]
    laid[:, at["b_main"]] = b[:, 0:P].T
    laid[:, at["b_out"]] = b[-1, GE_RESULT]
    return laid


def kernel(x, adj, L0_gnn_weight, L0_gnn_bias, L0_ffn_weight, L1_gnn_Wq, L1_gnn_Wk, L1_gnn_Wv, L1_ffn_W, L1_ffn_b):
    import numpy as np
    import concourse.bacc as bacc
    from concourse.bass_utils import run_bass_kernel_spmd

    mlp_w, mlp_b = np.asarray(L1_ffn_W), np.asarray(L1_ffn_b)
    laid = {
        "x": np.asarray(x), "adj": np.asarray(adj), "adj_turned": np.asarray(adj).T,
        "gnn_w": np.asarray(L0_gnn_weight), "gnn_b": np.asarray(L0_gnn_bias), "ffn_w": np.asarray(L0_ffn_weight),
        "wq": np.asarray(L1_gnn_Wq), "wk": np.asarray(L1_gnn_Wk), "wv_turned": np.asarray(L1_gnn_Wv).T,
        "mlp": lay_out_mlp(mlp_w, mlp_b),
    }
    laid = {f"in_{name}": np.ascontiguousarray(a) for name, a in laid.items()}
    nc = bacc.Bacc("TRN2", target_bir_lowering=False, num_devices=1, dynamic_dma_scratch_size=1024)
    args = [nc.dram_tensor(name, a.shape, mybir.dt.from_np(a.dtype), kind="ExternalInput").ap()
            for name, a in laid.items()]
    out = nc.dram_tensor("out", x.shape, F32, kind="ExternalOutput").ap()
    adj_ffn_kernel(nc, *args, mlp_w.shape[0], mlp_w.shape[1], out)
    return run_bass_kernel_spmd(nc, [laid], core_ids=[0]).results[0]["out"]
```
